# Optimizing a Trainium2 kernel written in Bass

```python
import numpy as np
import jax
import jax.numpy as jnp

def _softmax(x, axis=-1):
    return jax.nn.softmax(x, axis=axis)

def _gelu(x):
    return jax.nn.gelu(x, approximate=True)

def _silu(x):
    return jax.nn.silu(x)

def _sigmoid(x):
    return jax.nn.sigmoid(x)

def _layernorm(x, axis=-1, eps=1e-05):
    m = jnp.mean(x, axis=axis, keepdims=True)
    v = jnp.var(x, axis=axis, keepdims=True)
    return (x - m) / jnp.sqrt(v + eps)

def _scatter_add(tgt, idx, src, axis=0):
    return tgt.at[idx].add(src)

def _segment_sum(src, seg, n):
    return jax.ops.segment_sum(src, seg, n)
kernel_name = 'mk_decoder_preln_d2_seqx_r4_70417a'

def setup_inputs(seed: int=0):
    np.random.seed(seed)
    _w = jnp.asarray

    def _rec_inputs():
        import jax
        import jax.numpy as jnp
        _rk = jax.random.key(seed)
        x = -0.0002928 + 1 * jax.random.normal(jax.random.fold_in(_rk, 1), (2, 1024, 256), jnp.float32)
        _lenS = 1024 - jax.random.randint(jax.random.fold_in(_rk, 7), (2,), 0, max(1, 1024 // 4) + 1, jnp.int32)
        _lenS2 = 77 - jax.random.randint(jax.random.fold_in(_rk, 8), (2,), 0, max(1, 77 // 4) + 1, jnp.int32)
        _ctx_1024P = jax.random.normal(jax.random.fold_in(_rk, 11), (2, 16, 256), jnp.float32)
        _ctx_1024c = jax.random.dirichlet(jax.random.fold_in(_rk, 511), 0.3 * jnp.ones((16,), jnp.float32), (2, 77))
        _ctx_1024t = jnp.einsum('bsk,bkd->bsd', _ctx_1024c, _ctx_1024P)
        _ctx_1024t = _ctx_1024t * jax.lax.rsqrt(jnp.mean(jnp.square(_ctx_1024t)) + 1e-12) * 0.953939
        ctx_1024 = -1.39393e-06 + 0.999914 * (_ctx_1024t + 0.3 * jax.random.normal(jax.random.fold_in(_rk, 611), (2, 77, 256), jnp.float32))
        _validS = jnp.arange(1024)[None, :] < _lenS[:, None]
        _validS2 = jnp.arange(77)[None, :] < _lenS2[:, None]
        _causal = jnp.tril(jnp.ones((1024, 1024), dtype=bool))
        mask_BxS2_bf1 = jnp.ones((2, 77), dtype=bool)
        mask_Bx1x1xS2_ik0 = jnp.where(jnp.broadcast_to(_validS2[:, None, None, :], (2, 1, 1, 77)), 0, 1).astype(jnp.int32)
        return (x, ctx_1024, mask_BxS2_bf1, mask_Bx1x1xS2_ik0)
    x, ctx_1024, mask_BxS2_bf1, mask_Bx1x1xS2_ik0 = _rec_inputs()

    def _L0_attn_setup():
        import jax, jax.numpy as jnp
        import numpy as np
        D_MODEL = 256
        N_HEADS = 16
        HEAD_DIM = D_MODEL // N_HEADS
        D_LATENT = 64
        LAMBDA_DECAY = 0.01
        TIME_STEP = 0.01
        CLAMP = 10000.0

        def _reference_tuple_inner(x, Wq, Wk, Wv, Wo, W_down_kv, W_up_k, W_up_v):
            B, S, _ = x.shape
            q = x @ Wq
            k = x @ Wk
            v = x @ Wv
            latent_kv = (k + v) @ W_down_kv
            k_rec = latent_kv @ W_up_k
            v_rec = latent_kv @ W_up_v

            def heads(t):
                return t.reshape(B, S, N_HEADS, HEAD_DIM).transpose(0, 2, 1, 3)
            qh, kh, vh = (heads(q), heads(k_rec), heads(v_rec))
            scale = 1.0 / (jnp.sqrt(jnp.float32(D_MODEL)) + 1e-08)
            scores = jnp.einsum('bhqd,bhkd->bhqk', qh, kh) * scale
            scores = jnp.clip(jnp.nan_to_num(scores, nan=-1000000000.0), -CLAMP, CLAMP)
            idx = jnp.arange(S, dtype=jnp.float32)
            decay = jnp.exp(-LAMBDA_DECAY * TIME_STEP * jnp.abs(idx[:, None] - idx[None, :]))
            scores = scores * decay[None, None, :, :]
            scores = jnp.clip(jnp.nan_to_num(scores, nan=-1000000000.0), -CLAMP, CLAMP)
            attn = jax.nn.softmax(scores, axis=-1)
            out = jnp.einsum('bhqk,bhkd->bhqd', attn, vh)
            out = out.transpose(0, 2, 1, 3).reshape(B, S, D_MODEL)
            return (out @ Wo, latent_kv)
        key = jax.random.key(seed)
        ks = jax.random.split(key, 8)
        B, S = (2, 512)

        def w(k, i, o):
            return jax.random.normal(k, (i, o), dtype=jnp.float32) * 0.02
        return {'x': jax.random.normal(ks[0], (B, S, D_MODEL), dtype=jnp.float32), 'Wq': w(ks[1], D_MODEL, D_MODEL), 'Wk': w(ks[2], D_MODEL, D_MODEL), 'Wv': w(ks[3], D_MODEL, D_MODEL), 'Wo': w(ks[4], D_MODEL, D_MODEL), 'W_down_kv': w(ks[5], D_MODEL, D_LATENT), 'W_up_k': w(ks[6], D_LATENT, D_MODEL), 'W_up_v': w(ks[7], D_LATENT, D_MODEL)}
    _L0_attn_all = _L0_attn_setup()
    _L0_attn_in = {k: v for k, v in _L0_attn_all.items() if k in ('Wq', 'Wk', 'Wv', 'Wo', 'W_down_kv', 'W_up_k', 'W_up_v')}
    del _L0_attn_all

    def _L0_xattn_setup():
        import jax, jax.numpy as jnp
        import numpy as np
        N_HEADS = 16
        D_MODEL = 256
        HEAD_DIM = D_MODEL // N_HEADS
        MASK_FILL = -100000000.0

        def _split_heads(x):
            B, S, _ = x.shape
            return x.reshape(B, S, N_HEADS, HEAD_DIM).transpose(0, 2, 1, 3)
        key = jax.random.key(seed)
        ks = jax.random.split(key, 12)
        B, L, P = (2, 512, 512)
        s = 1.0 / np.sqrt(D_MODEL).astype(np.float32)
        inp = {'q': jax.random.normal(ks[0], (B, L, D_MODEL), dtype=jnp.float32), 'k': jax.random.normal(ks[1], (B, P, D_MODEL), dtype=jnp.float32), 'v': jax.random.normal(ks[2], (B, P, D_MODEL), dtype=jnp.float32), 'attention_mask': jnp.ones((B, P), dtype=bool), 'Wq': jax.random.normal(ks[3], (D_MODEL, D_MODEL), dtype=jnp.float32) * s, 'bq': jnp.zeros((D_MODEL,), dtype=jnp.float32), 'Wk': jax.random.normal(ks[4], (D_MODEL, D_MODEL), dtype=jnp.float32) * s, 'bk': jnp.zeros((D_MODEL,), dtype=jnp.float32), 'Wv': jax.random.normal(ks[5], (D_MODEL, D_MODEL), dtype=jnp.float32) * s, 'bv': jnp.zeros((D_MODEL,), dtype=jnp.float32), 'Wo': jax.random.normal(ks[6], (D_MODEL, D_MODEL), dtype=jnp.float32) * s, 'bo': jnp.zeros((D_MODEL,), dtype=jnp.float32)}
        return inp
    _L0_xattn_all = _L0_xattn_setup()
    _L0_xattn_in = {k: v for k, v in _L0_xattn_all.items() if k in ('Wq', 'bq', 'Wk', 'bk', 'Wv', 'bv', 'Wo', 'bo')}
    del _L0_xattn_all

    def _L0_ffn_setup():
        import jax, jax.numpy as jnp
        import numpy as np
        EPS = 1e-05

        def rmsnorm(x):
            return x * jax.lax.rsqrt(jnp.mean(x * x, axis=-1, keepdims=True) + EPS)

        def act_quant(x):
            scale = 127.0 / jnp.clip(jnp.max(jnp.abs(x), axis=-1, keepdims=True), 1e-05)
            q = jnp.clip(jnp.round(x * scale), -128.0, 127.0) / scale
            return x + jax.lax.stop_gradient(q - x)

        def weight_quant(w):
            scale = 1.0 / jnp.clip(jnp.mean(jnp.abs(w)), 1e-05)
            q = jnp.clip(jnp.round(w * scale), -1.0, 1.0) / scale
            return w + jax.lax.stop_gradient(q - w)

        def bitlinear(x, w, b):
            xq = act_quant(rmsnorm(x))
            wq = weight_quant(w)
            return jnp.einsum('bsd,fd->bsf', xq, wq) + b
        key = jax.random.key(seed)
        k0, k1, k2 = jax.random.split(key, 3)
        B, S, D, F = (2, 2048, 256, 1024)
        x = jax.random.normal(k0, (B, S, D), dtype=jnp.float32)
        w1 = jax.random.normal(k1, (F, D), dtype=jnp.float32) * (1.0 / np.sqrt(D))
        b1 = jnp.zeros((F,), dtype=jnp.float32)
        w2 = jax.random.normal(k2, (D, F), dtype=jnp.float32) * (1.0 / np.sqrt(F))
        b2 = jnp.zeros((D,), dtype=jnp.float32)
        return {'x': x, 'w1': w1, 'b1': b1, 'w2': w2, 'b2': b2}
    _L0_ffn_all = _L0_ffn_setup()
    _L0_ffn_in = {k: v for k, v in _L0_ffn_all.items() if k in ('w1', 'b1', 'w2', 'b2')}
    del _L0_ffn_all

    def _L1_attn_setup():
        import jax, jax.numpy as jnp
        import numpy as np
        INV_SQRT_M = 1.0 / np.sqrt(256.0).astype(np.float32)

        def _kernel_features(x, random_matrix):
            x_proj = jnp.einsum('bhsd,dm->bhsm', x, random_matrix)
            return (jax.nn.elu(x_proj) + 1.0) * INV_SQRT_M
        key = jax.random.key(seed)
        ks = jax.random.split(key, 7)
        B, S, D, H, M = (4, 1024, 256, 16, 64)
        hd = D // H
        std = 1.0 / np.sqrt(D)
        return {'x': jax.random.normal(ks[0], (B, S, D), jnp.float32), 'Wq': jax.random.normal(ks[1], (D, D), jnp.float32) * std, 'bq': jnp.zeros((D,), jnp.float32), 'Wk': jax.random.normal(ks[2], (D, D), jnp.float32) * std, 'bk': jnp.zeros((D,), jnp.float32), 'Wv': jax.random.normal(ks[3], (D, D), jnp.float32) * std, 'bv': jnp.zeros((D,), jnp.float32), 'Wo': jax.random.normal(ks[4], (D, D), jnp.float32) * std, 'bo': jnp.zeros((D,), jnp.float32), 'random_matrix': jax.random.normal(ks[5], (hd, M), jnp.float32)}
    _L1_attn_all = _L1_attn_setup()
    _L1_attn_in = {k: v for k, v in _L1_attn_all.items() if k in ('Wq', 'bq', 'Wk', 'bk', 'Wv', 'bv', 'Wo', 'bo', 'random_matrix')}
    del _L1_attn_all

    def _L1_xattn_setup():
        import jax, jax.numpy as jnp
        import numpy as np
        D_MODEL = 256
        NUM_HEADS = 16
        D_K = D_MODEL // NUM_HEADS
        B, S = (2, 512)
        NEG = -1000000000.0

        def _split_heads(x):
            b, s, _ = x.shape
            return x.reshape(b, s, NUM_HEADS, D_K).transpose(0, 2, 1, 3)
        key = jax.random.key(seed)
        ks = jax.random.split(key, 13)
        std = 0.02
        inp = {'q': jax.random.normal(ks[0], (B, S, D_MODEL), dtype=jnp.float32), 'k': jax.random.normal(ks[1], (B, S, D_MODEL), dtype=jnp.float32), 'v': jax.random.normal(ks[2], (B, S, D_MODEL), dtype=jnp.float32), 'mask': jax.random.randint(ks[3], (B, 1, 1, S), 0, 2, dtype=jnp.int32), 'Wq': jax.random.normal(ks[4], (D_MODEL, D_MODEL), dtype=jnp.float32) * std, 'bq': jnp.zeros((D_MODEL,), dtype=jnp.float32), 'Wk': jax.random.normal(ks[5], (D_MODEL, D_MODEL), dtype=jnp.float32) * std, 'bk': jnp.zeros((D_MODEL,), dtype=jnp.float32), 'Wv': jax.random.normal(ks[6], (D_MODEL, D_MODEL), dtype=jnp.float32) * std, 'bv': jnp.zeros((D_MODEL,), dtype=jnp.float32), 'Wo': jax.random.normal(ks[7], (D_MODEL, D_MODEL), dtype=jnp.float32) * std, 'bo': jnp.zeros((D_MODEL,), dtype=jnp.float32)}
        return inp
    _L1_xattn_all = _L1_xattn_setup()
    _L1_xattn_in = {k: v for k, v in _L1_xattn_all.items() if k in ('Wq', 'bq', 'Wk', 'bk', 'Wv', 'bv', 'Wo', 'bo')}
    del _L1_xattn_all

    def _L1_ffn_setup():
        import jax, jax.numpy as jnp
        import numpy as np
        N_EMBED = 256
        FFN_HIDDEN = 1024
        NUM_EXPERTS = 8
        TOP_K = 2
        key = jax.random.key(seed)
        ks = jax.random.split(key, 8)
        d, f, E = (N_EMBED, FFN_HIDDEN, NUM_EXPERTS)
        s_d = 1.0 / np.sqrt(d)
        s_f = 1.0 / np.sqrt(f)
        return {'x': jax.random.normal(ks[0], (2, 512, d), dtype=jnp.float32), 'Wg': jax.random.uniform(ks[1], (d, E), jnp.float32, -s_d, s_d), 'bg': jax.random.uniform(ks[2], (E,), jnp.float32, -s_d, s_d), 'W1': jax.random.uniform(ks[3], (E, d, f), jnp.float32, -s_d, s_d), 'b1': jax.random.uniform(ks[4], (E, f), jnp.float32, -s_d, s_d), 'W2': jax.random.uniform(ks[5], (E, f, d), jnp.float32, -s_f, s_f), 'b2': jax.random.uniform(ks[6], (E, d), jnp.float32, -s_f, s_f)}
    _L1_ffn_all = _L1_ffn_setup()
    _L1_ffn_in = {k: v for k, v in _L1_ffn_all.items() if k in ('Wg', 'bg', 'W1', 'b1', 'W2', 'b2')}
    del _L1_ffn_all
    return {'x': x, 'ctx_1024': ctx_1024, 'mask_BxS2_bf1': mask_BxS2_bf1, 'mask_Bx1x1xS2_ik0': mask_Bx1x1xS2_ik0, 'L0_attn_Wq': _L0_attn_in['Wq'], 'L0_attn_Wk': _L0_attn_in['Wk'], 'L0_attn_Wv': _L0_attn_in['Wv'], 'L0_attn_Wo': _L0_attn_in['Wo'], 'L0_attn_W_down_kv': _L0_attn_in['W_down_kv'], 'L0_attn_W_up_k': _L0_attn_in['W_up_k'], 'L0_attn_W_up_v': _L0_attn_in['W_up_v'], 'L0_xattn_Wq': _L0_xattn_in['Wq'], 'L0_xattn_bq': _L0_xattn_in['bq'], 'L0_xattn_Wk': _L0_xattn_in['Wk'], 'L0_xattn_bk': _L0_xattn_in['bk'], 'L0_xattn_Wv': _L0_xattn_in['Wv'], 'L0_xattn_bv': _L0_xattn_in['bv'], 'L0_xattn_Wo': _L0_xattn_in['Wo'], 'L0_xattn_bo': _L0_xattn_in['bo'], 'L0_ffn_w1': _L0_ffn_in['w1'], 'L0_ffn_b1': _L0_ffn_in['b1'], 'L0_ffn_w2': _L0_ffn_in['w2'], 'L0_ffn_b2': _L0_ffn_in['b2'], 'L1_attn_Wq': _L1_attn_in['Wq'], 'L1_attn_bq': _L1_attn_in['bq'], 'L1_attn_Wk': _L1_attn_in['Wk'], 'L1_attn_bk': _L1_attn_in['bk'], 'L1_attn_Wv': _L1_attn_in['Wv'], 'L1_attn_bv': _L1_attn_in['bv'], 'L1_attn_Wo': _L1_attn_in['Wo'], 'L1_attn_bo': _L1_attn_in['bo'], 'L1_attn_random_matrix': _L1_attn_in['random_matrix'], 'L1_xattn_Wq': _L1_xattn_in['Wq'], 'L1_xattn_bq': _L1_xattn_in['bq'], 'L1_xattn_Wk': _L1_xattn_in['Wk'], 'L1_xattn_bk': _L1_xattn_in['bk'], 'L1_xattn_Wv': _L1_xattn_in['Wv'], 'L1_xattn_bv': _L1_xattn_in['bv'], 'L1_xattn_Wo': _L1_xattn_in['Wo'], 'L1_xattn_bo': _L1_xattn_in['bo'], 'L1_ffn_Wg': _L1_ffn_in['Wg'], 'L1_ffn_bg': _L1_ffn_in['bg'], 'L1_ffn_W1': _L1_ffn_in['W1'], 'L1_ffn_b1': _L1_ffn_in['b1'], 'L1_ffn_W2': _L1_ffn_in['W2'], 'L1_ffn_b2': _L1_ffn_in['b2']}

def reference(x, ctx_1024, mask_BxS2_bf1, mask_Bx1x1xS2_ik0, L0_attn_Wq, L0_attn_Wk, L0_attn_Wv, L0_attn_Wo, L0_attn_W_down_kv, L0_attn_W_up_k, L0_attn_W_up_v, L0_xattn_Wq, L0_xattn_bq, L0_xattn_Wk, L0_xattn_bk, L0_xattn_Wv, L0_xattn_bv, L0_xattn_Wo, L0_xattn_bo, L0_ffn_w1, L0_ffn_b1, L0_ffn_w2, L0_ffn_b2, L1_attn_Wq, L1_attn_bq, L1_attn_Wk, L1_attn_bk, L1_attn_Wv, L1_attn_bv, L1_attn_Wo, L1_attn_bo, L1_attn_random_matrix, L1_xattn_Wq, L1_xattn_bq, L1_xattn_Wk, L1_xattn_bk, L1_xattn_Wv, L1_xattn_bv, L1_xattn_Wo, L1_xattn_bo, L1_ffn_Wg, L1_ffn_bg, L1_ffn_W1, L1_ffn_b1, L1_ffn_W2, L1_ffn_b2):
    import jax
    import jax.numpy as jnp

    def _L0_attn_ref(x, Wq, Wk, Wv, Wo, W_down_kv, W_up_k, W_up_v):
        import jax, jax.numpy as jnp
        import numpy as np
        D_MODEL = 256
        N_HEADS = 16
        HEAD_DIM = D_MODEL // N_HEADS
        D_LATENT = 64
        LAMBDA_DECAY = 0.01
        TIME_STEP = 0.01
        CLAMP = 10000.0

        def _reference_tuple_inner(x, Wq, Wk, Wv, Wo, W_down_kv, W_up_k, W_up_v):
            B, S, _ = x.shape
            q = x @ Wq
            k = x @ Wk
            v = x @ Wv
            latent_kv = (k + v) @ W_down_kv
            k_rec = latent_kv @ W_up_k
            v_rec = latent_kv @ W_up_v

            def heads(t):
                return t.reshape(B, S, N_HEADS, HEAD_DIM).transpose(0, 2, 1, 3)
            qh, kh, vh = (heads(q), heads(k_rec), heads(v_rec))
            scale = 1.0 / (jnp.sqrt(jnp.float32(D_MODEL)) + 1e-08)
            scores = jnp.einsum('bhqd,bhkd->bhqk', qh, kh) * scale
            scores = jnp.clip(jnp.nan_to_num(scores, nan=-1000000000.0), -CLAMP, CLAMP)
            idx = jnp.arange(S, dtype=jnp.float32)
            decay = jnp.exp(-LAMBDA_DECAY * TIME_STEP * jnp.abs(idx[:, None] - idx[None, :]))
            scores = scores * decay[None, None, :, :]
            scores = jnp.clip(jnp.nan_to_num(scores, nan=-1000000000.0), -CLAMP, CLAMP)
            attn = jax.nn.softmax(scores, axis=-1)
            out = jnp.einsum('bhqk,bhkd->bhqd', attn, vh)
            out = out.transpose(0, 2, 1, 3).reshape(B, S, D_MODEL)
            return (out @ Wo, latent_kv)
        return _reference_tuple_inner(x, Wq, Wk, Wv, Wo, W_down_kv, W_up_k, W_up_v)[0]

    def _L0_xattn_ref(q, k, v, attention_mask, Wq, bq, Wk, bk, Wv, bv, Wo, bo):
        import jax, jax.numpy as jnp
        import numpy as np
        N_HEADS = 16
        D_MODEL = 256
        HEAD_DIM = D_MODEL // N_HEADS
        MASK_FILL = -100000000.0

        def _split_heads(x):
            B, S, _ = x.shape
            return x.reshape(B, S, N_HEADS, HEAD_DIM).transpose(0, 2, 1, 3)
        qm = _split_heads(q @ Wq.T + bq)
        km = _split_heads(k @ Wk.T + bk)
        vm = _split_heads(v @ Wv.T + bv)
        scores = jnp.einsum('bnlh,bnph->bnlp', qm, km) / np.sqrt(HEAD_DIM).astype(np.float32)
        mask = attention_mask[:, None, None, :]
        scores = jnp.where(mask, scores, MASK_FILL)
        attn = jax.nn.softmax(scores, axis=-1)
        out = jnp.einsum('bnlp,bnph->bnlh', attn, vm)
        B, _, L, _ = out.shape
        out = out.transpose(0, 2, 1, 3).reshape(B, L, D_MODEL)
        return out @ Wo.T + bo

    def _L0_ffn_ref(x, w1, b1, w2, b2):
        import jax, jax.numpy as jnp
        import numpy as np
        EPS = 1e-05

        def rmsnorm(x):
            return x * jax.lax.rsqrt(jnp.mean(x * x, axis=-1, keepdims=True) + EPS)

        def act_quant(x):
            scale = 127.0 / jnp.clip(jnp.max(jnp.abs(x), axis=-1, keepdims=True), 1e-05)
            q = jnp.clip(jnp.round(x * scale), -128.0, 127.0) / scale
            return x + jax.lax.stop_gradient(q - x)

        def weight_quant(w):
            scale = 1.0 / jnp.clip(jnp.mean(jnp.abs(w)), 1e-05)
            q = jnp.clip(jnp.round(w * scale), -1.0, 1.0) / scale
            return w + jax.lax.stop_gradient(q - w)

        def bitlinear(x, w, b):
            xq = act_quant(rmsnorm(x))
            wq = weight_quant(w)
            return jnp.einsum('bsd,fd->bsf', xq, wq) + b
        h = bitlinear(x, w1, b1)
        h = jax.nn.gelu(h, approximate=False)
        return bitlinear(h, w2, b2)

    def _L1_attn_ref(x, Wq, bq, Wk, bk, Wv, bv, Wo, bo, random_matrix):
        import jax, jax.numpy as jnp
        import numpy as np
        INV_SQRT_M = 1.0 / np.sqrt(256.0).astype(np.float32)

        def _kernel_features(x, random_matrix):
            x_proj = jnp.einsum('bhsd,dm->bhsm', x, random_matrix)
            return (jax.nn.elu(x_proj) + 1.0) * INV_SQRT_M
        B, S, D = x.shape
        hd, M = random_matrix.shape
        H = D // hd
        q = (x @ Wq + bq).reshape(B, S, H, hd).transpose(0, 2, 1, 3)
        k = (x @ Wk + bk).reshape(B, S, H, hd).transpose(0, 2, 1, 3)
        v = (x @ Wv + bv).reshape(B, S, H, hd).transpose(0, 2, 1, 3)
        q_prime = _kernel_features(q, random_matrix)
        k_prime = _kernel_features(k, random_matrix)
        kv = jnp.einsum('bhsm,bhsd->bhmd', k_prime, v)
        k_sum = k_prime.sum(axis=2)
        out = jnp.einsum('bhsm,bhmd->bhsd', q_prime, kv)
        normalizer = jnp.einsum('bhsm,bhm->bhs', q_prime, k_sum)[..., None]
        normalizer = jnp.maximum(normalizer, 1e-06)
        out = out / normalizer
        out = out.transpose(0, 2, 1, 3).reshape(B, S, D)
        return out @ Wo + bo

    def _L1_xattn_ref(q, k, v, mask, Wq, bq, Wk, bk, Wv, bv, Wo, bo):
        import jax, jax.numpy as jnp
        import numpy as np
        D_MODEL = 256
        NUM_HEADS = 16
        D_K = D_MODEL // NUM_HEADS
        B, S = (2, 512)
        NEG = -1000000000.0

        def _split_heads(x):
            b, s, _ = x.shape
            return x.reshape(b, s, NUM_HEADS, D_K).transpose(0, 2, 1, 3)
        qh = _split_heads(q @ Wq.T + bq)
        kh = _split_heads(k @ Wk.T + bk)
        vh = _split_heads(v @ Wv.T + bv)
        scale = 1.0 / jnp.sqrt(jnp.float32(D_K))
        scores = jnp.einsum('bhqd,bhkd->bhqk', qh, kh) * scale
        scores = jnp.where(mask == 0, jnp.float32(NEG), scores)
        probs = jax.nn.softmax(scores, axis=-1)
        attn = jnp.einsum('bhqk,bhkd->bhqd', probs, vh)
        out = attn.transpose(0, 2, 1, 3).reshape(q.shape[0], q.shape[1], D_MODEL)
        return out @ Wo.T + bo

    def _L1_ffn_ref(x, Wg, bg, W1, b1, W2, b2):
        import jax, jax.numpy as jnp
        import numpy as np
        N_EMBED = 256
        FFN_HIDDEN = 1024
        NUM_EXPERTS = 8
        TOP_K = 2
        gate_scores = jax.nn.softmax(x @ Wg + bg, axis=-1)
        topk_scores, topk_idx = jax.lax.top_k(gate_scores, TOP_K)
        topk_scores = topk_scores / (jnp.sum(topk_scores, axis=-1, keepdims=True) + 1e-08)
        onehot = jax.nn.one_hot(topk_idx, NUM_EXPERTS, dtype=x.dtype)
        combine_w = jnp.einsum('bsk,bske->bse', topk_scores, onehot)
        output = jnp.zeros_like(x)
        for e in range(NUM_EXPERTS):
            h = jax.nn.gelu(x @ W1[e] + b1[e])
            y = h @ W2[e] + b2[e]
            output = output + y * combine_w[..., e:e + 1]
        return output
    x = x + _L0_attn_ref(_layernorm(x, axis=-1), L0_attn_Wq, L0_attn_Wk, L0_attn_Wv, L0_attn_Wo, L0_attn_W_down_kv, L0_attn_W_up_k, L0_attn_W_up_v)
    x = x + _L0_xattn_ref(_layernorm(x, axis=-1), ctx_1024, ctx_1024, mask_BxS2_bf1, L0_xattn_Wq, L0_xattn_bq, L0_xattn_Wk, L0_xattn_bk, L0_xattn_Wv, L0_xattn_bv, L0_xattn_Wo, L0_xattn_bo)
    x = x + _L0_ffn_ref(_layernorm(x, axis=-1), L0_ffn_w1, L0_ffn_b1, L0_ffn_w2, L0_ffn_b2)
    x = x + _L1_attn_ref(_layernorm(x, axis=-1), L1_attn_Wq, L1_attn_bq, L1_attn_Wk, L1_attn_bk, L1_attn_Wv, L1_attn_bv, L1_attn_Wo, L1_attn_bo, L1_attn_random_matrix)
    x = x + _L1_xattn_ref(_layernorm(x, axis=-1), ctx_1024, ctx_1024, mask_Bx1x1xS2_ik0, L1_xattn_Wq, L1_xattn_bq, L1_xattn_Wk, L1_xattn_bk, L1_xattn_Wv, L1_xattn_bv, L1_xattn_Wo, L1_xattn_bo)
    x = x + _L1_ffn_ref(_layernorm(x, axis=-1), L1_ffn_Wg, L1_ffn_bg, L1_ffn_W1, L1_ffn_b1, L1_ffn_W2, L1_ffn_b2)
    return x

_drawn_inputs = setup_inputs


def setup_inputs(seed=0):
    import zlib

    import numpy as np

    out = dict(_drawn_inputs(seed))
    spreads = {'L0_xattn_bq': (0.0, 0.8),
     'L0_xattn_bk': (0.0, 2.0),
     'L0_xattn_bv': (0.0, 0.8),
     'L0_xattn_bo': (0.0, 0.8),
     'L0_ffn_b1': (0.0, 0.8),
     'L0_ffn_b2': (0.0, 0.8),
     'L1_attn_bq': (0.0, 2.0),
     'L1_attn_bk': (0.0, 2.0),
     'L1_attn_bv': (0.0, 0.8),
     'L1_attn_bo': (0.0, 0.8),
     'L1_xattn_bq': (0.0, 2.0),
     'L1_xattn_bk': (0.0, 2.0),
     'L1_xattn_bv': (0.0, 2.0),
     'L1_xattn_bo': (0.0, 0.8)}
    factors = {'L0_attn_Wq': 8.0,
     'L0_attn_Wk': 8.0,
     'L0_attn_Wv': 8.0,
     'L0_attn_Wo': 8.0,
     'L0_attn_W_down_kv': 8.0,
     'L0_attn_W_up_k': 8.0,
     'L0_attn_W_up_v': 8.0,
     'L1_attn_Wq': 25.816,
     'L1_attn_Wk': 22.552,
     'L1_attn_random_matrix': 35.24,
     'L1_xattn_Wq': 64.0,
     'L1_xattn_Wk': 64.0,
     'L1_ffn_bg': 24.344,
     'L1_ffn_b1': 64.0,
     'L1_ffn_b2': 138.562,
     'ctx_1024': 3.053,
     'L0_xattn_Wq': 6.534,
     'L0_xattn_Wk': 6.409,
     'L1_attn_Wv': 8.0,
     'L1_attn_Wo': 8.0,
     'L1_xattn_Wv': 8.0,
     'L1_xattn_Wo': 8.0,
     'L1_ffn_Wg': 8.0,
     'L1_ffn_W1': 8.0,
     'L1_ffn_W2': 8.0}
    for name, (base, spread) in spreads.items():
        noise = np.random.default_rng([zlib.crc32(name.encode()), seed]).standard_normal(out[name].shape)
        drawn = base * np.exp(spread * noise) if base else spread * noise
        out[name] = jnp.asarray(drawn.astype(out[name].dtype))
    for name, factor in factors.items():
        out[name] = (out[name] * factor).astype(out[name].dtype)
    return out
```

```python
from contextlib import ExitStack

import numpy as np

import concourse.bass as bass
from concourse import mybir

F32 = mybir.dt.float32
F32R = mybir.dt.float32r
BF16 = mybir.dt.bfloat16
U32 = mybir.dt.uint32
U8 = mybir.dt.uint8
I32 = mybir.dt.int32
ALU = mybir.AluOpType
ACT = mybir.ActivationFunctionType
AX = mybir.AxisListType.X

P = 128
B, S, D, H = 2, 1024, 256, 16
HD = D // H
T = B * S
KD = D // P
HP = P // HD
NT = T // P
TPG = 4
NG = NT // TPG
G = TPG * P
QT = S // P
C = 77
L = 64
F = 1024
FT = F // P
M = 64
E = 8
LN_EPS = 1e-5
CLAMP = 10000.0
DECAY = 0.01 * 0.01
ROUND = 1.5 * 2.0 ** 23


def wait(eng, sem, value):
    if isinstance(value, int) and value <= 0:
        return
    eng.wait_ge(sem, value)


class Steps:

    def __init__(self, eng, sem, start=0):
        self.eng, self.sem, self.n = eng, sem, start

    def did(self, ins):
        ins.then_inc(self.sem, 1)
        self.n += 1

    def wait(self):
        self.eng.wait_ge(self.sem, self.n)


class Core:

    def __init__(self, nc):
        self.nc, self.block = nc, 0
        self.sems, self.zeroed = [], []

    def sb(self, ctx, name, shape, dt=F32):
        return ctx.enter_context(self.nc.sbuf_tensor(f"{name}_sb", list(shape), dt))

    def sem(self, name):
        self.sems.append(self.nc.alloc_semaphore(name=f"b{self.block}_{name}"))
        return self.sems[-1]

    def next_block(self):
        for s in self.zeroed:
            self.nc.release_semaphore(s)
        for s in self.sems:
            self.nc.gpsimd.sem_clear(s)
        self.sems, self.zeroed = [], self.sems
        self.block += 1


def load_constants(k, d):
    nc = k.nc
    k.next_block()
    x_in, small_in, weights_in = k.sem("x_in"), k.sem("small_in"), k.sem("weights_in")
    with nc.Block() as block:
        @block.sync
        def _(sp):
            sp.dma_start(k.x[:, :, :], d["x"].rearrange("b (t p) n -> p (b t) n", p=P)).then_inc(x_in, 16)
            sp.dma_start(k.ident[:, :], d["c_ident"]).then_inc(small_in, 16)
            sp.dma_start(k.hmask[:, :], d["c_hmask"]).then_inc(small_in, 16)
            sp.dma_start(k.wd[:, :, :], d["L0_attn_W_down_kv"].rearrange("(k p) n -> p k n", p=P)).then_inc(small_in, 16)
            sp.dma_start(k.wuk[:, :], d["L0_attn_W_up_k"]).then_inc(small_in, 16)
            sp.dma_start(k.wuv[:, :], d["L0_attn_W_up_v"]).then_inc(small_in, 16)
            sp.wait_ge(x_in, 16)
            sp.dma_start(k.decay[:, :], d["c_decay"]).then_inc(small_in, 16)
            sp.wait_ge(small_in, 6 * 16)

        @block.scalar
        def _(act):
            for name, w in k.w.items():
                act.dma_start(w[:, :, :], d[name].rearrange("(k p) n -> p k n", p=P)).then_inc(weights_in, 16)
            act.wait_ge(weights_in, 16 * len(k.w))


def normalise(k, to_features=True):
    nc = k.nc
    k.next_block()
    dve_own, var_ready, std_ready = k.sem("dve_own"), k.sem("var_ready"), k.sem("std_ready")
    xn_ready, turned, xt_done = k.sem("xn_ready"), k.sem("turned"), k.sem("xt_done")
    with ExitStack() as c, nc.Block() as block:
        sid = k.block
        st = k.sb(c, f"st{sid}", [P, NT, 6])
        mv = k.sb(c, f"mv{sid}", [P, NT, 2])
        var = k.sb(c, f"var{sid}", [P, NT])
        std = k.sb(c, f"std{sid}", [P, NT])
        std2 = k.sb(c, f"std2{sid}", [P, NT])
        rstd = k.sb(c, f"rstd{sid}", [P, NT])
        xn = k.sb(c, f"xn{sid}", [P, 2, TPG, D])

        @block.vector
        def _(dve):
            own = Steps(dve, dve_own)
            for t in range(NT):
                own.did(dve.bn_stats(st[:, t, :], k.x[:, t, :]))
            own.wait()
            for t in range(NT):
                own.did(dve.bn_aggr(mv[:, t, :], st[:, t, :]))
            own.wait()
            dve.tensor_scalar(var[:, :], mv[:, :, 1], LN_EPS, None, ALU.add).then_inc(var_ready, 1)
            dve.wait_ge(std_ready, 1)
            own.did(dve.reciprocal(rstd[:, :], std[:, :]))
            own.wait()
            own.did(dve.tensor_tensor(std2[:, :], var[:, :], rstd[:, :], ALU.mult))
            own.wait()
            own.did(dve.tensor_tensor(std[:, :], std2[:, :], std[:, :], ALU.add))
            own.wait()
            own.did(dve.tensor_scalar(std2[:, :], std[:, :], 0.5, None, ALU.mult))
            own.wait()
            own.did(dve.reciprocal(rstd[:, :], std2[:, :]))
            own.wait()
            for t in range(NT):
                g, j = divmod(t, TPG)
                if j == 0:
                    wait(dve, turned, g - 1)
                dve.tensor_scalar(xn[:, g % 2, j, :], k.x[:, t, :], mv[:, t, 0:1], rstd[:, t:t + 1],
                                  ALU.subtract, ALU.mult).then_inc(xn_ready, 1)

        @block.scalar
        def _(act):
            act.wait_ge(var_ready, 1)
            act.activation(std[:, :], var[:, :], ACT.Sqrt).then_inc(std_ready, 1)
            for g in range(NG):
                act.wait_ge(turned, g + 1)
                for kd in range(KD):
                    act.activation(k.xt[:, kd, g * G:(g + 1) * G], k.ps[:, 2 * (g % 2) + kd, :],
                                   ACT.Copy).then_inc(xt_done, 1)

        @block.tensor
        def _(pe):
            for g in range(NG):
                wait(pe, xt_done, KD * (g - 1))
                for j in range(TPG):
                    pe.wait_ge(xn_ready, g * TPG + j + 1)
                    for kd in range(KD):
                        last = pe.transpose(k.ps[:, 2 * (g % 2) + kd, j * P:(j + 1) * P],
                                            xn[:, g % 2, j, kd * P:(kd + 1) * P], k.ident[:, :])
                last.then_inc(turned, 1)


def project_out(k, w, bias, attn):
    nc = k.nc
    k.next_block()
    bias_in, biased = k.sem("bias_in"), k.sem("biased")
    turned, at_done = k.sem("turned"), k.sem("at_done")
    out_ready, added = k.sem("out_ready"), k.sem("added")
    with ExitStack() as c, nc.Block() as block:
        sid = k.block
        at = k.sb(c, f"at{sid}", [P, KD, 2, G])
        bb = k.sb(c, f"bb{sid}", [P, D])

        @block.sync
        def _(sp):
            if bias is not None:
                sp.dma_start(bb[:, :], bias.partition_broadcast(P)).then_inc(bias_in, 16)

        @block.gpsimd
        def _(pool):
            if bias is not None:
                pool.wait_ge(bias_in, 16)
                for t in range(NT):
                    pool.tensor_tensor(k.x[:, t, :], k.x[:, t, :], bb[:, :], ALU.add).then_inc(biased, 1)

        @block.tensor
        def _(pe):
            for g in range(NG):
                wait(pe, at_done, KD * (g - 1))
                for j in range(TPG):
                    for kd in range(KD):
                        last = pe.transpose(k.ps[:, 2 * (g % 2) + kd, j * P:(j + 1) * P],
                                            attn[:, g * TPG + j, kd * P:(kd + 1) * P], k.ident[:, :])
                last.then_inc(turned, 1)
                for j in range(TPG):
                    t = g * TPG + j
                    if j == 0:
                        pe.wait_ge(at_done, KD * (g + 1))
                    wait(pe, added, t - TPG + 1)
                    for kd in range(KD):
                        last = pe.matmul(k.ps[:, 4 + j, 0:D], at[:, kd, g % 2, j * P:(j + 1) * P], w[:, kd, :],
                                         start=kd == 0, stop=kd == KD - 1)
                    last.then_inc(out_ready, 1)

        @block.scalar
        def _(act):
            for g in range(NG):
                act.wait_ge(turned, g + 1)
                wait(act, out_ready, (g - 1) * TPG)
                for kd in range(KD):
                    act.activation(at[:, kd, g % 2, :], k.ps[:, 2 * (g % 2) + kd, :], ACT.Copy).then_inc(at_done, 1)

        @block.vector
        def _(dve):
            for t in range(NT):
                if bias is not None:
                    dve.wait_ge(biased, t + 1)
                dve.wait_ge(out_ready, t + 1)
                dve.tensor_tensor(k.x[:, t, :], k.x[:, t, :], k.ps[:, 4 + t % TPG, 0:D], ALU.add).then_inc(added, 1)


def latent_projections(k, v_heads, q_scratch, k_scratch):
    nc = k.nc
    k.next_block()
    wsum_ready, wkv_ready, wkv_done = k.sem("wsum_ready"), k.sem("wkv_ready"), k.sem("wkv_done")
    lat_ready, lat_done = k.sem("lat_ready"), k.sem("lat_done")
    qk_ready, part1_done, rest1_done, part2_done, part3_done = (
        k.sem("qk_ready"), k.sem("part1_done"), k.sem("rest1_done"), k.sem("part2_done"), k.sem("part3_done"))
    v_ready, v_done = k.sem("v_ready"), k.sem("v_done")
    stored = [k.sem(f"stored{s}") for s in range(4)]
    scale = 1.0 / 16.0
    NP = NG * 2 * KD
    with ExitStack() as c, nc.Block() as block:
        wsum = k.sb(c, "wsum", [P, KD, D])
        wkv = k.sb(c, "wkv", [P, KD, L])
        lat = k.sb(c, "lat", [L, T])
        parts = k.sb(c, "parts", [P, 4, 3, G], BF16)
        rest = k.sb(c, "rest", [P, 4, G])

        @block.tensor
        def _(pe):
            pe.wait_ge(wsum_ready, 1)
            for m in range(KD):
                for kd in range(KD):
                    last = pe.matmul(k.ps[:, 7, m * L:(m + 1) * L], wsum[:, kd, m * P:(m + 1) * P], k.wd[:, kd, :],
                                     start=kd == 0, stop=kd == KD - 1)
            last.then_inc(wkv_ready, 1)
            pe.wait_ge(wkv_done, 1)
            for g in range(NG):
                rows = slice(g * G, (g + 1) * G)
                wait(pe, lat_done, g)
                for kd in range(KD):
                    last = pe.matmul(k.ps[0:L, 4, :], wkv[:, kd, :], k.xt[:, kd, rows], start=kd == 0, stop=kd == KD - 1)
                last.then_inc(lat_ready, 1)
                for m in range(KD):
                    n = 4 * g + m
                    wait(pe, rest1_done, n - 3)
                    wait(pe, part1_done, n - 3)
                    for kd in range(KD):
                        last = pe.matmul(k.ps[:, m, :], k.w["L0_attn_Wq"][:, kd, m * P:(m + 1) * P],
                                         k.xt[:, kd, rows], start=kd == 0, stop=kd == KD - 1)
                    last.then_inc(qk_ready, 1)
                pe.wait_ge(lat_done, g + 1)
                for m in range(KD):
                    n = 4 * g + 2 + m
                    wait(pe, rest1_done, n - 3)
                    wait(pe, part1_done, n - 3)
                    pe.matmul(k.ps[:, 2 + m, :], k.wuk[:, m * P:(m + 1) * P], lat[:, rows],
                              start=True, stop=True).then_inc(qk_ready, 1)
                for j in range(TPG):
                    t = g * TPG + j
                    wait(pe, v_done, t - 1)
                    pe.matmul(k.ps[:, 5 + t % 2, 0:D], lat[:, t * P:(t + 1) * P], k.wuv[:, :],
                              start=True, stop=True).then_inc(v_ready, 1)

        @block.vector
        def _(dve):
            dve.tensor_tensor(wsum[:, :, :], k.w["wk_t"][:, :, :], k.w["wv_t"][:, :, :], ALU.add).then_inc(wsum_ready, 1)
            dve.wait_ge(wkv_ready, 1)
            dve.tensor_copy(wkv[:, :, :], k.ps[:, 7, 0:KD * L].rearrange("p (m n) -> p m n", m=KD)).then_inc(wkv_done, 1)
            for n in range(NP):
                s = n % 4
                f = scale if s < 2 else 1.0
                dve.wait_ge(part1_done, n + 1)
                dve.scalar_tensor_tensor(out=rest[:, s, :], in0=k.ps[:, s, :], scalar=f, in1=parts[:, s, 0, :],
                                         op0=ALU.mult, op1=ALU.subtract).then_inc(rest1_done, 1)
                dve.wait_ge(part2_done, n + 1)
                dve.tensor_tensor(parts[:, s, 2, :], rest[:, s, :], parts[:, s, 1, :],
                                  ALU.subtract).then_inc(part3_done, 1)

        @block.scalar
        def _(act):
            for n in range(NP):
                g, s = divmod(n, 4)
                if s == 0:
                    act.wait_ge(lat_ready, g + 1)
                    act.activation(lat[:, g * G:(g + 1) * G], k.ps[0:L, 4, :], ACT.Copy).then_inc(lat_done, 1)
                act.wait_ge(qk_ready, n + 1)
                wait(act, stored[s], 16 * g)
                act.activation(parts[:, s, 0, :], k.ps[:, s, :], ACT.Copy,
                               scale=scale if s < 2 else 1.0).then_inc(part1_done, 1)
                act.wait_ge(rest1_done, n + 1)
                act.activation(parts[:, s, 1, :], rest[:, s, :], ACT.Copy).then_inc(part2_done, 1)
                if s == 3:
                    for t in range(g * TPG, (g + 1) * TPG):
                        b, q = divmod(t, QT)
                        act.wait_ge(v_ready, t + 1)
                        act.activation(v_heads[:, b * H:(b + 1) * H, q, :],
                                       k.ps[:, 5 + t % 2, 0:D].rearrange("p (h d) -> p h d", d=HD),
                                       ACT.Copy).then_inc(v_done, 1)

        @block.sync
        def _(sp):
            for n in range(NP):
                g, s = divmod(n, 4)
                b, half = divmod(g, 2)
                m = s % 2
                scratch = q_scratch if s < 2 else k_scratch
                sp.wait_ge(part3_done, n + 1)
                sp.dma_start(scratch[:, b * D + m * P:b * D + (m + 1) * P, half * G:(half + 1) * G]
                             .rearrange("c p n -> p c n"), parts[:, s, :, :]).then_inc(stored[s], 16)
            for s in range(4):
                sp.wait_ge(stored[s], 16 * NG)


def latent_attention(k, v_heads, attn, decay, q_scratch, k_scratch):
    nc = k.nc
    k.next_block()
    stack_in = [k.sem(f"stack_in{u}") for u in range(2)]
    scored, clipped, peaked, shifted = (
        k.sem("scored"), k.sem("clipped"), k.sem("peaked"), k.sem("shifted"))
    exp_done, p_turned, pt_done, v_staged = k.sem("exp_done"), k.sem("p_turned"), k.sem("pt_done"), k.sem("v_staged")
    mixed, mix_copied, mix_turned, inverted, weighted = (
        k.sem("mixed"), k.sem("mix_copied"), k.sem("mix_turned"), k.sem("inverted"), k.sem("weighted"))
    zeroed = k.sem("zeroed")
    BODY = B
    NB = H
    TB = BODY * QT
    GB = TB // TPG
    TRAIL = 2 * TPG
    MIX_PARTS = [range(0, 3), range(3, 6), range(6, QT)]
    with ExitStack() as c, nc.Block() as block:
        qs = k.sb(c, "q_stack", [96, BODY, S], BF16)
        ks = k.sb(c, "k_stack", [96, BODY, S], BF16)
        vh = k.sb(c, "v_head", [P, BODY, QT, 32])
        sc = k.sb(c, "clipped_scores", [P, 2, S])
        pr = k.sb(c, "probs", [P, 4, S])
        peak = k.sb(c, "peak", [P, 8])
        shift = k.sb(c, "shift", [P, 8])
        minus = k.sb(c, "minus", [P, 1])
        sums = k.sb(c, "sums", [P, 4, TPG])
        inv = k.sb(c, "inv", [P, 2, TPG])
        pt = k.sb(c, "probs_t", [P, TPG, 2, QT, P])
        mix = k.sb(c, "mix", [P, 2, P])

        def bodies(eng, body):
            body(0, True, False)
            with eng.Fori(1, NB - 1) as i:
                body(i, False, False)
            body(NB - 1, False, True)

        def steps(eng, step):
            for s in range(TB):
                step(0, s, lambda tile: tile >= 0)
            with eng.Fori(1, NB - 1) as i:
                for s in range(TB):
                    step(i, s, lambda tile: True)
            for s in range(TB):
                step(NB - 1, s, lambda tile: True)
            for s in range(TRAIL):
                step(NB, s, lambda tile: tile < 0)

        @block.sync
        def _(sp):
            def body(i, first, last):
                for u in range(BODY):
                    wait(sp, scored, (i - 1) * TB + (u + 1) * QT if not first else 0)
                    for stack, scratch, order in ((qs, q_scratch, "q"), (ks, k_scratch, "k")):
                        row = 0
                        for r in range(3):
                            n = 3 - r
                            src = scratch[:, bass.ds(i * HD + u * D, HD), :]
                            if order == "q":
                                for x in range(n):
                                    sp.dma_start(stack[row + x * HD:row + (x + 1) * HD, u, :],
                                                 src[r:r + 1].rearrange("c p n -> (c p) n")).then_inc(stack_in[u], 16)
                            else:
                                for x in range(n):
                                    sp.dma_start(stack[row + x * HD:row + (x + 1) * HD, u, :],
                                                 src[x:x + 1].rearrange("c p n -> (c p) n")).then_inc(stack_in[u], 16)
                            row += n * HD
            bodies(sp, body)

        @block.gpsimd
        def _(pool):
            pool.memset(vh[:, :, :, :], 0.0).then_inc(zeroed, 1)
            pool.memset(minus[:, :], -1.0).then_inc(zeroed, 1)
            pool.wait_ge(zeroed, 2)

            def body(i, first, last):
                for s in range(TB):
                    u, q = divmod(s, QT)
                    n = i * TB + s
                    if q == 0:
                        wait(pool, mixed, i * GB - GB + (u + 1) * (QT // TPG) if not first else 0)
                        pool.tensor_copy(vh[:, u, :, 0:HD], v_heads[:, bass.ds(i + u * H, 1), :, :]
                                         .rearrange("p a t d -> p (a t) d")).then_inc(v_staged, 1)
                    pool.wait_ge(peaked, n + 1)
                    wait(pool, exp_done, n - 7)
                    pool.tensor_tensor(shift[:, s % 8:s % 8 + 1], peak[:, s % 8:s % 8 + 1], minus[:, :],
                                       ALU.mult).then_inc(shifted, 1)
            bodies(pool, body)

        @block.tensor
        def _(pe):
            def scores(i, s):
                n = i * TB + s
                u, q = divmod(s % TB, QT)
                if q == 0:
                    pe.wait_ge(stack_in[u], (i + s // TB + 1) * 12 * 16)
                wait(pe, clipped, n - 1)
                for half in range(2):
                    last = pe.matmul(k.ps[:, 2 * (s % 2) + half, :], qs[:, u, q * P:(q + 1) * P],
                                     ks[:, u, half * 512:(half + 1) * 512], start=True, stop=True)
                last.then_inc(scored, 1)

            def turn(i, s):
                n = i * TB + s
                pe.wait_ge(exp_done, n + 1)
                wait(pe, pt_done, n)
                for kt in range(QT):
                    last = pe.transpose(k.ps[:, 4 + kt // 4, (kt % 4) * P:(kt % 4 + 1) * P],
                                        pr[:, s % 4, kt * P:(kt + 1) * P], k.ident[:, :])
                last.then_inc(p_turned, 1)

            def mix_part(i, gs, part):
                gn = i * GB + gs
                u = gs % GB // (QT // TPG)
                if part == 0:
                    pe.wait_ge(pt_done, (gn + 1) * TPG)
                    pe.wait_ge(v_staged, i * BODY + gs // (QT // TPG) + 1)
                    wait(pe, mix_copied, gn)
                for kt in MIX_PARTS[part]:
                    for j in range(TPG):
                        last = pe.matmul(k.ps[32 * j:32 * j + 32, 6, 0:P], vh[:, u, kt, :],
                                         pt[:, j, gs % 2, kt, :], start=kt == 0, stop=kt == QT - 1)
                if part == len(MIX_PARTS) - 1:
                    last.then_inc(mixed, 1)

            def turn_mix(i, gs):
                gn = i * GB + gs
                pe.wait_ge(mix_copied, gn + 1)
                wait(pe, weighted, gn)
                pe.transpose(k.ps[:, 7, 0:P], mix[:, gs % 2, :], k.ident[:, :]).then_inc(mix_turned, 1)

            def step(i, s, due):
                if s < TB and not (i is NB or (i is NB - 1 and s >= TB - 2)):
                    scores(i, s + 2)
                if due(s - 1):
                    turn(i, s - 1)
                gs = s // TPG - 1
                if s % TPG and due(gs * TPG):
                    mix_part(i, gs, s % TPG - 1)
                if s % TPG == 1 and due((gs - 1) * TPG):
                    turn_mix(i, gs - 1)

            scores(0, 0)
            scores(0, 1)
            steps(pe, step)

        @block.vector
        def _(dve):
            def weight(i, gs):
                gn = i * GB + gs
                u, half = divmod(gs % GB, QT // TPG)
                dve.wait_ge(exp_done, (gn + 1) * TPG)
                wait(dve, weighted, gn - 1)
                dve.reciprocal(inv[:, gs % 2, :], sums[:, gs % 4, :]).then_inc(inverted, 1)
                dve.wait_ge(inverted, gn + 1)
                dve.wait_ge(mix_turned, gn + 1)
                dve.tensor_tensor(
                    attn[:, u * QT + half * TPG:u * QT + (half + 1) * TPG, bass.ds((i + gs // GB) * HD, HD)],
                    k.ps[:, 7, 0:P].rearrange("p (t d) -> p t d", d=32)[:, :, 0:HD],
                    inv[:, gs % 2, :].unsqueeze(2).to_broadcast([P, TPG, HD]), ALU.mult).then_inc(weighted, 1)

            def clip(i, s):
                n = i * TB + s
                dve.wait_ge(scored, n + 1)
                wait(dve, peaked, n - 1)
                dve.tensor_scalar(sc[:, s % 2, :], k.ps[:, 2 * (s % 2):2 * (s % 2) + 2, :].rearrange("p a n -> p (a n)"),
                                  -CLAMP, CLAMP, ALU.max, ALU.min).then_inc(clipped, 1)

            def fade(i, s):
                n = i * TB + s
                dve.wait_ge(clipped, n + 1)
                wait(dve, p_turned, n - 3)
                wait(dve, shifted, n - 7)
                off = (QT - 1 - s % QT) * P
                dve.nop(nofuse=True)
                dve.tensor_tensor_reduce(out=pr[:, s % 4, :], in0=sc[:, s % 2, :], in1=decay[:, off:off + S],
                                         scale=1.0, scalar=-3.0e38, op0=ALU.mult, op1=ALU.max,
                                         accum_out=peak[:, s % 8:s % 8 + 1]).then_inc(peaked, 1)

            def step(i, s, due):
                if not (i is NB or (i is NB - 1 and s == TB - 1)):
                    clip(i, s + 1)
                if i is not NB:
                    fade(i, s)
                gs = s // TPG - 2
                if s % TPG == 2 and due(gs * TPG):
                    weight(i, gs)

            clip(0, 0)
            steps(dve, step)

        @block.scalar
        def _(act):
            def copy_out(i, s):
                n = i * TB + s
                act.wait_ge(p_turned, n + 1)
                wait(act, mixed, i * GB + s // TPG - 1)
                act.activation(pt[:, s % 4, (s // TPG) % 2, :, :].rearrange("p t n -> p (t n)"),
                               k.ps[:, 4:6, :].rearrange("p a n -> p (a n)"), ACT.Copy).then_inc(pt_done, 1)

            def copy_mix(i, gs):
                gn = i * GB + gs
                act.wait_ge(mixed, gn + 1)
                wait(act, mix_turned, gn - 1)
                act.activation(mix[:, gs % 2, :], k.ps[:, 6, 0:P], ACT.Copy).then_inc(mix_copied, 1)

            def step(i, s, due):
                if i is not NB:
                    n = i * TB + s
                    act.wait_ge(shifted, n + 1)
                    wait(act, inverted, i * GB + s // TPG - 3)
                    act.activation(pr[:, s % 4, :], pr[:, s % 4, :], ACT.Exp, bias=shift[:, s % 8:s % 8 + 1],
                                   accum_out=sums[:, (s // TPG) % 4, s % 4:s % 4 + 1]).then_inc(exp_done, 1)
                if due(s - 1):
                    copy_out(i, s - 1)
                gs = s // TPG - 2
                if s % TPG == 0 and due(gs * TPG):
                    copy_mix(i, gs)
            steps(act, step)


def cross_attention(k, attn, wq, wk, wv, bq, bk, bv, mask, fill, ctx_t):
    nc = k.nc
    k.next_block()
    loaded, own_sem = k.sem("loaded"), k.sem("own")
    kv_ready, operands_done = k.sem("kv_ready"), k.sem("operands_done")
    q_ready, q_done = k.sem("q_ready"), k.sem("q_done")
    scored, peaked, shifted = k.sem("scored"), k.sem("peaked"), k.sem("shifted")
    exp_done, p_turned, pt_done, mixed = k.sem("exp_done"), k.sem("p_turned"), k.sem("pt_done"), k.sem("mixed")
    floored, inverted, weighted = k.sem("floored"), k.sem("inverted"), k.sem("weighted")
    HB = 4
    NBK = H // HB
    V1 = HD + 1
    scale = 1.0 / 4.0
    with ExitStack() as c, nc.Block() as block:
        sid = k.block
        ctx_sb = k.sb(c, f"ctx{sid}", [P, KD, B * C])
        bq_sb = k.sb(c, f"bq{sid}", [P, KD])
        bk_sb = k.sb(c, f"bk{sid}", [P, KD])
        bv_sb = k.sb(c, f"bv{sid}", [C, D])
        mask_sb = k.sb(c, f"mask{sid}", [P, B * C], mask.dtype)
        hidden = k.sb(c, f"hidden{sid}", [P, B * C])
        keep = k.sb(c, f"keep{sid}", [P, B * C])
        hidden4 = k.sb(c, f"hidden4{sid}", [3, B, HB, C], BF16)
        fill_sb = k.sb(c, f"fill{sid}", [3, P])
        fill_b = k.sb(c, f"fillb{sid}", [3, P], BF16)
        kt = k.sb(c, f"kt{sid}", [P, KD, B * C])
        kbd = k.sb(c, f"kbd{sid}", [P, B, KD, HP, C])
        va = k.sb(c, f"va{sid}", [C, B, H, V1])
        qt = k.sb(c, f"qt{sid}", [P, KD, T])
        pr = k.sb(c, f"pr{sid}", [P, 2, H, C])
        peak = k.sb(c, f"peak{sid}", [P, 2, H])
        pt = k.sb(c, f"pt{sid}", [C, 2, H, P])
        inv = k.sb(c, f"inv{sid}", [P, 2, H])

        @block.sync
        def _(sp):
            sp.dma_start(ctx_sb[:, :, :], ctx_t.rearrange("(k p) n -> p k n", p=P)).then_inc(loaded, 16)
            sp.dma_start(bq_sb[:, :], bq).then_inc(loaded, 16)
            sp.dma_start(bk_sb[:, :], bk).then_inc(loaded, 16)
            sp.dma_start(bv_sb[:, :], bv.partition_broadcast(C)).then_inc(loaded, 16)
            sp.dma_start(mask_sb[:, :], mask.partition_broadcast(P)).then_inc(loaded, 16)
            sp.dma_start(fill_sb[:, :], fill).then_inc(loaded, 16)

        @block.tensor
        def _(pe):
            pe.wait_ge(loaded, 6 * 16)
            for m in range(KD):
                for kd in range(KD):
                    pe.matmul(k.ps[:, 4 + m, 0:B * C], wk[:, kd, m * P:(m + 1) * P], ctx_sb[:, kd, :],
                              start=kd == 0, stop=kd == KD - 1)
            for b in range(B):
                for kd in range(KD):
                    last = pe.matmul(k.ps[0:C, 6 + b, 0:D], ctx_sb[:, kd, b * C:(b + 1) * C], wv[:, kd, :],
                                     start=kd == 0, stop=kd == KD - 1)
            last.then_inc(kv_ready, 1)
            for g in range(NG):
                for m in range(KD):
                    n = KD * g + m
                    wait(pe, q_done, n - 3)
                    for kd in range(KD):
                        last = pe.matmul(k.ps[:, n % 4, :], wq[:, kd, m * P:(m + 1) * P],
                                         k.xt[:, kd, g * G:(g + 1) * G], start=kd == 0, stop=kd == KD - 1)
                    last.then_inc(q_ready, 1)
            pe.wait_ge(operands_done, 1)
            pe.wait_ge(q_done, KD * NG)

            def scores(t):
                b = t // QT
                wait(pe, shifted, t)
                for a in range(NBK):
                    kd, half = divmod(a, NBK // KD)
                    rhs = kbd[:, b, kd, half * HB:(half + 1) * HB, :].rearrange("p h n -> p (h n)")
                    pe.matmul(k.ps[:, a, 0:HB * C], qt[:, kd, t * P:(t + 1) * P], rhs, start=True, stop=False)
                    last = pe.matmul(k.ps[:, a, 0:HB * C], fill_b[:, :],
                                     hidden4[:, b, :, :].rearrange("p h n -> p (h n)"), start=False, stop=True)
                last.then_inc(scored, 1)

            scores(0)
            for t in range(NT):
                b = t // QT
                pe.wait_ge(exp_done, t + 1)
                for a in range(NBK):
                    n = NBK * t + a
                    wait(pe, pt_done, n - 2)
                    for h in range(HB):
                        last = pe.transpose(k.ps[0:C, 4 + n % 3, h * P:(h + 1) * P], pr[:, t % 2, a * HB + h, :],
                                            k.ident[:, :])
                    last.then_inc(p_turned, 1)
                if t + 1 < NT:
                    scores(t + 1)
                wait(pe, weighted, t)
                for h in range(H):
                    if h % HB == 0:
                        pe.wait_ge(pt_done, NBK * t + h // HB + 1)
                    last = pe.matmul(k.ps[:, 7, h * V1:(h + 1) * V1], pt[:, t % 2, h, :], va[:, b, h, :],
                                     start=True, stop=True)
                last.then_inc(mixed, 1)

        @block.vector
        def _(dve):
            own = Steps(dve, own_sem)
            dve.wait_ge(loaded, 6 * 16)
            own.did(dve.tensor_scalar(hidden[:, :], mask_sb[:, :], 0.0, None, ALU.is_equal))
            own.did(dve.memset(va[:, :, :, :], 1.0))
            own.did(dve.tensor_copy(fill_b[:, :], fill_sb[:, :]))
            own.wait()
            own.did(dve.tensor_scalar(keep[:, :], hidden[:, :], -1.0, 1.0, ALU.mult, ALU.add))
            for b in range(B):
                for h in range(HB):
                    own.did(dve.tensor_copy(hidden4[:, b, h, :], hidden[0:3, b * C:(b + 1) * C]))
            dve.wait_ge(kv_ready, 1)
            for m in range(KD):
                own.did(dve.tensor_scalar(kt[:, m, :], k.ps[:, 4 + m, 0:B * C], bk_sb[:, m:m + 1], scale,
                                          ALU.add, ALU.mult))
            own.wait()
            for m in range(KD):
                own.did(dve.tensor_tensor(kt[:, m, :], kt[:, m, :], keep[:, :], ALU.mult))
            own.wait()
            for b in range(B):
                own.did(dve.tensor_tensor(va[:, b, :, 0:HD], k.ps[0:C, 6 + b, 0:D].rearrange("p (h d) -> p h d", d=HD),
                                          bv_sb[:, :].rearrange("p (h d) -> p h d", d=HD), ALU.add))
                for m in range(KD):
                    for h in range(HP):
                        last = dve.tensor_scalar(kbd[:, b, m, h, :], kt[:, m, b * C:(b + 1) * C],
                                                 k.hmask[:, h:h + 1], None, ALU.mult)
                        if not (b == B - 1 and m == KD - 1 and h == HP - 1):
                            own.did(last)
            own.wait()
            last.then_inc(operands_done, 1)

            def weight(t):
                dve.wait_ge(mixed, t + 1)
                o = k.ps[:, 7, 0:H * V1].rearrange("p (h d) -> p h d", d=V1)
                dve.reciprocal(inv[:, t % 2, :], o[:, :, HD]).then_inc(inverted, 1)
                dve.wait_ge(inverted, t + 1)
                dve.tensor_tensor(attn[:, t, :].rearrange("p (h d) -> p h d", d=HD), o[:, :, 0:HD],
                                  inv[:, t % 2, :].unsqueeze(2).to_broadcast([P, H, HD]), ALU.mult).then_inc(weighted, 1)

            for t in range(NT):
                dve.wait_ge(scored, t + 1)
                s = k.ps[:, 0:NBK, 0:HB * C].rearrange("p a (h n) -> p a h n", n=C)
                dve.tensor_reduce(peak[:, t % 2, :].rearrange("p (a h) -> p a h", h=HB), s, AX, ALU.max).then_inc(peaked, 1)
                dve.wait_ge(peaked, t + 1)
                wait(dve, p_turned, NBK * (t - 1))
                dve.tensor_tensor(pr[:, t % 2, :, :].rearrange("p (a h) n -> p a h n", h=HB), s,
                                  peak[:, t % 2, :].rearrange("p (a h) -> p a h", h=HB).unsqueeze(3)
                                  .to_broadcast([P, NBK, HB, C]), ALU.subtract).then_inc(shifted, 1)
                if t > 0:
                    weight(t - 1)
            weight(NT - 1)

        @block.scalar
        def _(act):
            act.wait_ge(loaded, 6 * 16)
            for n in range(KD * NG):
                g, m = divmod(n, KD)
                act.wait_ge(q_ready, n + 1)
                act.activation(qt[:, m, g * G:(g + 1) * G], k.ps[:, n % 4, :], ACT.Identity,
                               bias=bq_sb[:, m:m + 1]).then_inc(q_done, 1)
            for t in range(NT):
                act.wait_ge(shifted, t + 1)
                act.activation(pr[:, t % 2, :, :].rearrange("p h n -> p (h n)"),
                               pr[:, t % 2, :, :].rearrange("p h n -> p (h n)"), ACT.Exp).then_inc(exp_done, 1)
                for a in range(NBK):
                    n = NBK * t + a
                    act.wait_ge(p_turned, n + 1)
                    wait(act, mixed, t - 1)
                    act.activation(pt[:, t % 2, a * HB:(a + 1) * HB, :].rearrange("p h n -> p (h n)"),
                                   k.ps[0:C, 4 + n % 3, :], ACT.Copy).then_inc(pt_done, 1)


def quantise_weights(k, raws, quants, winvs, sources, banks):
    nc = k.nc
    k.next_block()
    own_sem, loaded, summed, totalled = k.sem("own"), [k.sem(f"loaded{i}") for i in range(2)], k.sem("summed"), k.sem("totalled")
    with ExitStack() as c, nc.Block() as block:
        ones = k.sb(c, "ones_pp", [P, P])
        raw = [k.sb(c, f"raw{i}", [P, F * KD]) for i in range(2)]
        tmp = [k.sb(c, f"rawtmp{i}", [P, F * KD]) for i in range(2)]
        part = k.sb(c, "abs_sums", [P, 2])
        mean = k.sb(c, "abs_mean", [P, 2])
        wsc = k.sb(c, "w_scale", [P, 2])

        @block.sync
        def _(sp):
            for i, (src, kt) in enumerate(sources):
                sp.dma_start(raw[i][:, :].rearrange("p (k n) -> p k n", k=kt),
                             src.rearrange("(k p) n -> p k n", p=P)).then_inc(loaded[i], 16)

        @block.tensor
        def _(pe):
            pe.wait_ge(summed, 3)
            pe.matmul(k.ps[:, 0, 0:2], ones[:, :], part[:, :], start=True, stop=True).then_inc(totalled, 1)

        @block.scalar
        def _(act):
            for i in range(2):
                act.wait_ge(loaded[i], 16)
                act.activation(tmp[i][:, :], raw[i][:, :], ACT.Abs, accum_out=part[:, i:i + 1]).then_inc(summed, 1)

        @block.vector
        def _(dve):
            own = Steps(dve, own_sem)
            dve.memset(ones[:, :], 1.0).then_inc(summed, 1)
            dve.wait_ge(totalled, 1)
            own.did(dve.tensor_scalar(mean[:, :], k.ps[:, 0, 0:2], 1.0 / (F * D), 1e-5, ALU.mult, ALU.max))
            own.wait()
            own.did(dve.reciprocal(wsc[:, :], mean[:, :]))
            own.wait()
            own.did(dve.reciprocal(winvs[:, :], wsc[:, :]))
            for i in range(2):
                own.did(dve.tensor_scalar(tmp[i][:, :], raw[i][:, :], wsc[:, i:i + 1], ROUND, ALU.mult, ALU.add))
                own.wait()
                own.did(dve.tensor_scalar(raw[i][:, :], tmp[i][:, :], -ROUND, -1.0, ALU.add, ALU.max))
                own.wait()
                own.did(dve.tensor_scalar(quants[i], raw[i][:, :], 1.0, None, ALU.min))
            own.wait()


def ternary_ffn(k, w1q, w2q, winv, b1, b2):
    nc = k.nc
    k.next_block()
    loaded, biased = k.sem("loaded"), k.sem("biased")
    own_sem, act_own = k.sem("own"), k.sem("act_own")
    var_ready, std_ready = k.sem("var_ready"), k.sem("std_ready")
    squared, rms_ready = k.sem("squared"), k.sem("rms_ready")
    xq_ready, x_turned, xqt_done, up_ready, pre_ready, gelu_done = (
        k.sem("xq_ready"), k.sem("x_turned"), k.sem("xqt_done"), k.sem("up_ready"), k.sem("pre_ready"), k.sem("gelu_done"))
    h_squared, h_rms = k.sem("h_squared"), k.sem("h_rms")
    hq_ready, h_turned, hqt_done, down_ready, added = (
        k.sem("hq_ready"), k.sem("h_turned"), k.sem("hqt_done"), k.sem("down_ready"), k.sem("added"))
    NF = F // 512
    with ExitStack() as c, nc.Block() as block:
        st = k.sb(c, "f_st", [P, NT, 6])
        mv = k.sb(c, "f_mv", [P, NT, 2])
        sm = k.sb(c, "f_small", [P, 12, NT])
        b1b = k.sb(c, "f_b1", [P, F])
        b2b = k.sb(c, "f_b2", [P, D])
        y = k.sb(c, "f_y", [P, NT, D])
        scr = k.sb(c, "f_scr", [P, 2, F])
        xr = k.sb(c, "f_xr", [P, 2, D])
        xq = k.sb(c, "f_xq", [P, 2, D], BF16)
        identb = k.sb(c, "f_identb", [P, P], BF16)
        xqt = k.sb(c, "f_xqt", [P, 2, KD, P], BF16)
        pre = k.sb(c, "f_pre", [P, 2, F])
        hh = k.sb(c, "f_h", [P, NT, F])
        hq = k.sb(c, "f_hq", [P, 2, F], BF16)
        hqt = k.sb(c, "f_hqt", [P, 2, FT, P], BF16)
        fin = k.sb(c, "f_fin", [P, 2, D])
        var, std, rstd, t1, ss, rms, peak, scl, comb, xinv = (sm[:, i, :] for i in range(10))
        ss2, peak2 = sm[:, 10, :], sm[:, 11, :]
        psb = k.ps[:, :, :].rearrange("p a n -> p (a n)").bitcast(BF16).rearrange("p (a n) -> p a n", a=8)

        @block.sync
        def _(sp):
            sp.dma_start(b1b[:, :], b1.partition_broadcast(P)).then_inc(loaded, 16)
            sp.dma_start(b2b[:, :], b2.partition_broadcast(P)).then_inc(loaded, 16)

        def root(own, out, s, v, r, tmp, raw):
            own.did(own.eng.reciprocal(r, raw))
            own.wait()
            own.did(own.eng.tensor_tensor(tmp, v, r, ALU.mult))
            own.wait()
            own.did(own.eng.tensor_tensor(s, tmp, raw, ALU.add))
            own.wait()
            own.did(own.eng.tensor_scalar(tmp, s, 0.5, None, ALU.mult))
            own.wait()
            own.did(own.eng.reciprocal(out, tmp))
            own.wait()

        def quant_scales(own, peak_, rms_, winv_):
            dve = own.eng
            own.did(dve.tensor_tensor(t1, peak_, rms_, ALU.mult))
            own.wait()
            own.did(dve.tensor_scalar(t1, t1, 1e-5, None, ALU.max))
            own.wait()
            own.did(dve.reciprocal(scl, t1))
            own.wait()
            own.did(dve.tensor_scalar(scl, scl, 127.0, None, ALU.mult))
            own.wait()
            own.did(dve.reciprocal(xinv, scl))
            own.wait()
            own.did(dve.tensor_scalar(xinv, xinv, winv_, None, ALU.mult))
            own.wait()

        @block.vector
        def _(dve):
            own = Steps(dve, own_sem)
            for t in range(NT):
                own.did(dve.bn_stats(st[:, t, :], k.x[:, t, :]))
            own.did(dve.tensor_copy(identb[:, :], k.ident[:, :]))
            own.wait()
            for t in range(NT):
                own.did(dve.bn_aggr(mv[:, t, :], st[:, t, :]))
            own.wait()
            dve.tensor_scalar(var, mv[:, :, 1], LN_EPS, None, ALU.add).then_inc(var_ready, 1)
            dve.wait_ge(std_ready, 1)
            root(own, rstd, ss, var, scl, t1, std)
            for t in range(NT):
                own.did(dve.tensor_scalar(y[:, t, :], k.x[:, t, :], mv[:, t, 0:1], rstd[:, t:t + 1],
                                          ALU.subtract, ALU.mult))
            own.wait()
            for t in range(NT):
                own.did(dve.tensor_tensor_reduce(out=scr[:, t % 2, 0:D], in0=y[:, t, :], in1=y[:, t, :], scale=1.0,
                                                 scalar=0.0, op0=ALU.mult, op1=ALU.add, accum_out=ss[:, t:t + 1]))
                own.did(dve.tensor_reduce(peak[:, t:t + 1], y[:, t, :], AX, ALU.max, apply_absolute_value=True))
                own.wait()
            dve.tensor_scalar(var, ss, 1.0 / D, LN_EPS, ALU.mult, ALU.add).then_inc(squared, 1)
            dve.wait_ge(rms_ready, 1)
            root(own, rms, ss, var, scl, t1, std)
            quant_scales(own, peak, rms, winv[:, 0:1])

            def quantise_x(t):
                wait(dve, x_turned, t - 1)
                own.did(dve.tensor_scalar(xr[:, t % 2, :], y[:, t, :], rms[:, t:t + 1], scl[:, t:t + 1],
                                          ALU.mult, ALU.mult))
                own.wait()
                dve.tensor_scalar(xq[:, t % 2, :], xr[:, t % 2, :], ROUND, -ROUND, ALU.add, ALU.add).then_inc(xq_ready, 1)

            quantise_x(0)
            for t in range(NT):
                if t + 1 < NT:
                    quantise_x(t + 1)
                if t == 0:
                    dve.wait_ge(loaded, 32)
                dve.wait_ge(up_ready, t + 1)
                wait(dve, gelu_done, t - 1)
                dve.scalar_tensor_tensor(out=pre[:, t % 2, :], in0=k.ps[:, 2 + 2 * (t % 2):4 + 2 * (t % 2), :].rearrange("p a n -> p (a n)"),
                                         scalar=xinv[:, t:t + 1], in1=b1b[:, :], op0=ALU.mult, op1=ALU.add).then_inc(pre_ready, 1)
                if t > 0:
                    dve.wait_ge(gelu_done, t)
                    own.did(dve.tensor_reduce(peak2[:, t - 1:t], hh[:, t - 1, :], AX, ALU.max, apply_absolute_value=True))
            dve.wait_ge(gelu_done, NT)
            own.did(dve.tensor_reduce(peak2[:, NT - 1:NT], hh[:, NT - 1, :], AX, ALU.max, apply_absolute_value=True))
            own.wait()
            dve.wait_ge(h_squared, NT)
            dve.tensor_scalar(var, ss2, 1.0 / F, LN_EPS, ALU.mult, ALU.add).then_inc(squared, 1)
            dve.wait_ge(rms_ready, 2)
            root(own, rms, ss, var, scl, t1, std)
            quant_scales(own, peak2, rms, winv[:, 1:2])

            def quantise_h(t):
                wait(dve, h_turned, 1 * (t - 1))
                own.did(dve.tensor_scalar(pre[:, t % 2, :], hh[:, t, :], rms[:, t:t + 1], scl[:, t:t + 1],
                                          ALU.mult, ALU.mult))
                own.wait()
                dve.tensor_scalar(hq[:, t % 2, :], pre[:, t % 2, :], ROUND, -ROUND, ALU.add, ALU.add).then_inc(hq_ready, 1)

            for t in range(NT):
                own.did(dve.tensor_tensor(k.x[:, t, :], k.x[:, t, :], b2b[:, :], ALU.add))
            own.wait()
            quantise_h(0)
            for t in range(NT):
                if t + 1 < NT:
                    quantise_h(t + 1)
                dve.wait_ge(down_ready, t + 1)
                dve.scalar_tensor_tensor(out=k.x[:, t, :], in0=k.ps[:, 6 + t % 2, 0:D], scalar=xinv[:, t:t + 1],
                                         in1=k.x[:, t, :], op0=ALU.mult, op1=ALU.add).then_inc(added, 1)

        @block.scalar
        def _(act):
            act.wait_ge(var_ready, 1)
            act.activation(std, var, ACT.Sqrt).then_inc(std_ready, 1)
            act.wait_ge(squared, 1)
            act.activation(std, var, ACT.Sqrt).then_inc(rms_ready, 1)

            def copy_x(t):
                act.wait_ge(x_turned, t + 1)
                wait(act, up_ready, t - 1)
                act.activation(xqt[:, t % 2, :, :].rearrange("p k n -> p (k n)"), psb[:, t % 2, 0:KD * P],
                               ACT.Copy).then_inc(xqt_done, 1)
            copy_x(0)
            for t in range(NT):
                if t + 1 < NT:
                    copy_x(t + 1)
                act.wait_ge(pre_ready, t + 1)
                act.activation(hh[:, t, :], pre[:, t % 2, :], ACT.Gelu).then_inc(gelu_done, 1)
                act.wait_ge(gelu_done, t + 1)
                wait(act, h_squared, t - 1)
                act.activation(scr[:, t % 2, :], hh[:, t, :], ACT.Square, accum_out=ss2[:, t:t + 1]).then_inc(h_squared, 1)
            act.wait_ge(squared, 2)
            act.activation(std, var, ACT.Sqrt).then_inc(rms_ready, 1)
            for t in range(NT):
                act.wait_ge(h_turned, t + 1)
                wait(act, down_ready, t - 1)
                act.activation(hqt[:, t % 2, :, :].rearrange("p k n -> p (k n)"),
                               psb[:, 2 + t % 2, :], ACT.Copy).then_inc(hqt_done, 1)

        @block.tensor
        def _(pe):
            def turn_x(t):
                pe.wait_ge(xq_ready, t + 1)
                wait(pe, xqt_done, t - 1)
                for kd in range(KD):
                    last = pe.transpose(psb[:, t % 2, kd * P:(kd + 1) * P], xq[:, t % 2, kd * P:(kd + 1) * P], identb[:, :])
                last.then_inc(x_turned, 1)

            turn_x(0)
            for t in range(NT):
                if t + 1 < NT:
                    turn_x(t + 1)
                pe.wait_ge(xqt_done, t + 1)
                wait(pe, pre_ready, t - 1)
                for n in range(NF):
                    for kd in range(KD):
                        last = pe.matmul(k.ps[:, 2 + 2 * (t % 2) + n, :], xqt[:, t % 2, kd, :],
                                         w1q[:, kd, n * 512:(n + 1) * 512], start=kd == 0, stop=kd == KD - 1)
                last.then_inc(up_ready, 1)
            pe.wait_ge(pre_ready, NT)

            def turn_h(t):
                pe.wait_ge(hq_ready, t + 1)
                wait(pe, hqt_done, t - 1)
                for f in range(FT):
                    last = pe.transpose(psb[:, 2 + t % 2, f * P:(f + 1) * P], hq[:, t % 2, f * P:(f + 1) * P], identb[:, :])
                last.then_inc(h_turned, 1)

            turn_h(0)
            for t in range(NT):
                if t + 1 < NT:
                    turn_h(t + 1)
                pe.wait_ge(hqt_done, t + 1)
                wait(pe, added, t - 1)
                for f in range(FT):
                    last = pe.matmul(k.ps[:, 6 + t % 2, 0:D], hqt[:, t % 2, f, :], w2q[:, f, :],
                                     start=f == 0, stop=f == FT - 1)
                last.then_inc(down_ready, 1)


def feature_attention(k, attn, wq, wk, wv, bq, bk, bv, random_matrix):
    nc = k.nc
    k.next_block()
    loaded, own_sem, operands_done = k.sem("loaded"), k.sem("own"), k.sem("operands_done")
    proj_ready, proj_done = k.sem("proj_ready"), k.sem("proj_done")
    v_ready, v_done = k.sem("v_ready"), k.sem("v_done")
    x_ready, low_ready, exp_done, feat_done = k.sem("x_ready"), k.sem("low_ready"), k.sem("exp_done"), k.sem("feat_done")
    kv_used, kv_ready, kv_done = k.sem("kv_used"), k.sem("kv_ready"), k.sem("kv_done")
    mixed, floored, inverted, weighted = k.sem("mixed"), k.sem("floored"), k.sem("inverted"), k.sem("weighted")
    V1 = HD + 1
    PAIRS = H // 2
    PW = 2 * V1
    FLOOR = 1e-6 * 256.0
    KP = NT * KD
    QP = NG * PAIRS
    with ExitStack() as c, nc.Block() as block:
        bq_sb = k.sb(c, "l_bq", [P, KD])
        bk_sb = k.sb(c, "l_bk", [P, KD])
        bv_sb = k.sb(c, "l_bv", [P, D])
        r8 = k.sb(c, "l_r8", [P, M])
        rbd = k.sb(c, "l_rbd", [P, HP, M])
        pj = k.sb(c, "l_pj", [P, 2, KD, G])
        va = k.sb(c, "l_va", [P, NT, H, V1])
        low = k.sb(c, "l_low", [P, 4, 512])
        kp = k.sb(c, "l_kp", [P, 2, KD, 512])
        qp = k.sb(c, "l_qp", [P, 2, PAIRS, G])
        kv = k.sb(c, "l_kv", [P, B, PAIRS, PW])
        den = k.sb(c, "l_den", [P, 2, H])
        inv = k.sb(c, "l_inv", [P, 2, H])

        @block.sync
        def _(sp):
            sp.dma_start(bq_sb[:, :], bq).then_inc(loaded, 16)
            sp.dma_start(bk_sb[:, :], bk).then_inc(loaded, 16)
            sp.dma_start(bv_sb[:, :], bv.partition_broadcast(P)).then_inc(loaded, 16)
            for h in range(HP):
                sp.dma_start(r8[h * HD:(h + 1) * HD, :], random_matrix).then_inc(loaded, 16)

        @block.tensor
        def _(pe):
            def project(n, w):
                g, m = divmod(n % (KD * NG), KD)
                wait(pe, proj_done, n - 1)
                for kd in range(KD):
                    last = pe.matmul(k.ps[:, 4 + m, :], w[:, kd, m * P:(m + 1) * P],
                                     k.xt[:, kd, g * G:(g + 1) * G], start=kd == 0, stop=kd == KD - 1)
                last.then_inc(proj_ready, 1)

            def key_value(t):
                b, q = divmod(t, QT)
                pe.wait_ge(feat_done, KD * (t + 1))
                if q == 0:
                    wait(pe, kv_done, b)
                for p in range(PAIRS):
                    kd, r = divmod(p, PAIRS // KD)
                    last = pe.matmul(k.ps[:, 7, p * PW:(p + 1) * PW], kp[:, t % 2, kd, r * P:(r + 1) * P],
                                     va[:, t, 2 * p:2 * p + 2, :].rearrange("p h d -> p (h d)"),
                                     start=q == 0 and p == 0, stop=q == QT - 1, skip_group_check=True)
                last.then_inc(kv_used, 1)

            pe.wait_ge(loaded, 16 * (3 + HP))
            for m in range(KD):
                project(m, wk)
            pe.wait_ge(operands_done, 1)
            for g in range(NG):
                for j in range(TPG):
                    t = g * TPG + j
                    wait(pe, v_done, t)
                    for kd in range(KD):
                        last = pe.matmul(k.ps[:, 6, 0:D], k.xt[:, kd, t * P:(t + 1) * P], wv[:, kd, :],
                                         start=kd == 0, stop=kd == KD - 1)
                    last.then_inc(v_ready, 1)
                    if j == 0:
                        pe.wait_ge(proj_done, KD * (g + 1))
                    for kd in range(KD):
                        n = KD * t + kd
                        wait(pe, feat_done, n - 3)
                        pe.matmul(k.ps[:, n % 4, :], pj[:, g % 2, kd, j * P:(j + 1) * P],
                                  rbd[:, :, :].rearrange("p h m -> p (h m)"), start=True, stop=True).then_inc(x_ready, 1)
                    if t > 0:
                        wait(pe, v_done, t)
                        key_value(t - 1)
                if g + 1 < NG:
                    for m in range(KD):
                        project(KD * (g + 1) + m, wk)
                else:
                    for m in range(KD):
                        project(KD * NG + m, wq)
            def mix(t):
                b = t // QT
                wait(pe, weighted, t)
                if t == 0:
                    pe.wait_ge(kv_done, B)
                g, j = divmod(t, TPG)
                pe.wait_ge(feat_done, KP + PAIRS * (g + 1))
                for p in range(PAIRS):
                    last = pe.matmul(k.ps[:, 7, p * PW:(p + 1) * PW], qp[:, g % 2, p, j * P:(j + 1) * P],
                                     kv[:, b, p, :], start=True, stop=True)
                last.then_inc(mixed, 1)

            for g in range(NG):
                pe.wait_ge(proj_done, KD * (NG + g + 1))
                for p in range(PAIRS):
                    kd, r = divmod(p, PAIRS // KD)
                    n = KP + PAIRS * g + p
                    wait(pe, feat_done, n - 3)
                    pe.matmul(k.ps[:, n % 4, :], rbd[:, 2 * r:2 * r + 2, :].rearrange("p h m -> p (h m)"),
                              pj[:, g % 2, kd, :], start=True, stop=True).then_inc(x_ready, 1)
                    if g == 0 and p == 0:
                        pe.wait_ge(v_done, NT)
                        key_value(NT - 1)
                    if g > 0 and p % 2 == 1:
                        mix((g - 1) * TPG + p // 2)
                if g + 1 < NG:
                    for m in range(KD):
                        project(KD * (NG + g + 1) + m, wq)
            for j in range(TPG):
                mix((NG - 1) * TPG + j)

        @block.scalar
        def _(act):
            def copy_proj(n):
                g, m = divmod(n, KD)
                act.wait_ge(proj_ready, n + 1)
                if 2 <= g < NG:
                    act.wait_ge(x_ready, KD * TPG * (g - 1))
                elif g >= NG:
                    act.wait_ge(x_ready, KP - KD * TPG if g == NG else (KP if g == NG + 1 else KP + PAIRS * (g - NG - 1)))
                bias = bk_sb if g < NG else bq_sb
                act.activation(pj[:, g % 2, m, :], k.ps[:, 4 + m, :], ACT.Identity, bias=bias[:, m:m + 1]).then_inc(proj_done, 1)

            act.wait_ge(loaded, 16 * (3 + HP))
            for m in range(KD):
                copy_proj(m)
            for n in range(KP + QP):
                act.wait_ge(low_ready, n + 1)
                act.activation(low[:, n % 4, :], low[:, n % 4, :], ACT.Exp).then_inc(exp_done, 1)
                if n % (KD * TPG) == KD * TPG - 1 and (n + 1) // (KD * TPG) < 2 * NG:
                    for m in range(KD):
                        copy_proj(KD * ((n + 1) // (KD * TPG)) + m)

        @block.vector
        def _(dve):
            own = Steps(dve, own_sem)
            own.did(dve.memset(va[:, :, :, :], 1.0))
            own.did(dve.memset(kv[:, :, :, :], 0.0))
            dve.wait_ge(loaded, 16 * (3 + HP))
            for h in range(HP):
                last = dve.tensor_scalar(rbd[:, h, :], r8[:, :], k.hmask[:, h:h + 1], None, ALU.mult)
                if h < HP - 1:
                    own.did(last)
            own.wait()
            last.then_inc(operands_done, 1)

            def lower(n):
                dve.wait_ge(x_ready, n + 1)
                wait(dve, feat_done, n - 3)
                dve.tensor_scalar(low[:, n % 4, :], k.ps[:, n % 4, :], 0.0, None, ALU.min).then_inc(low_ready, 1)

            def feature(n):
                dve.wait_ge(exp_done, n + 1)
                if n < KP:
                    t, kd = divmod(n, KD)
                    wait(dve, kv_used, t - 1)
                    dst = kp[:, t % 2, kd, :]
                else:
                    g, p = divmod(n - KP, PAIRS)
                    wait(dve, mixed, TPG * (g - 1))
                    dst = qp[:, g % 2, p, :]
                dve.scalar_tensor_tensor(out=dst, in0=k.ps[:, n % 4, :], scalar=0.0, in1=low[:, n % 4, :],
                                         op0=ALU.max, op1=ALU.add).then_inc(feat_done, 1)

            def copy_v(t):
                dve.wait_ge(v_ready, t + 1)
                dve.tensor_tensor(va[:, t, :, 0:HD], k.ps[:, 6, 0:D].rearrange("p (h d) -> p h d", d=HD),
                                  bv_sb[:, :].rearrange("p (h d) -> p h d", d=HD), ALU.add).then_inc(v_done, 1)

            def copy_kv(b):
                dve.wait_ge(kv_used, QT * (b + 1))
                src = k.ps[:, 7, 0:PAIRS * PW].rearrange("p (a n) -> p a n", n=PW)
                own.did(dve.tensor_copy(kv[0:64, b, :, 0:V1], src[0:64, :, 0:V1]))
                dve.tensor_copy(kv[64:P, b, :, V1:PW], src[64:P, :, V1:PW]).then_inc(kv_done, 1)
                own.wait()

            def weight(t):
                dve.wait_ge(mixed, t + 1)
                o = k.ps[:, 7, 0:H * V1].rearrange("p (h d) -> p h d", d=V1)
                dve.tensor_scalar(den[:, t % 2, :], o[:, :, HD], FLOOR, None, ALU.max).then_inc(floored, 1)
                dve.wait_ge(floored, t + 1)
                dve.reciprocal(inv[:, t % 2, :], den[:, t % 2, :]).then_inc(inverted, 1)
                dve.wait_ge(inverted, t + 1)
                dve.tensor_tensor(attn[:, t, :].rearrange("p (h d) -> p h d", d=HD), o[:, :, 0:HD],
                                  inv[:, t % 2, :].unsqueeze(2).to_broadcast([P, H, HD]), ALU.mult).then_inc(weighted, 1)

            copy_v(0)
            lower(0)
            for n in range(1, KP + QP + 1):
                if n < KP + QP:
                    if n < KP and n % KD == 0:
                        copy_v(n // KD)
                    lower(n)
                feature(n - 1)
                done = n
                if done == KD * QT + 2:
                    copy_kv(0)
                if done == KP + 1:
                    copy_kv(1)
                g, p = divmod(done - KP - 1, PAIRS)
                if done - KP - 1 >= PAIRS and p % 2 == 1 and p // 2 < TPG and g <= NG - 1:
                    weight((g - 1) * TPG + p // 2)
            for j in range(TPG):
                weight((NG - 1) * TPG + j)


def route(k, cw, wg, bg, b2):
    nc = k.nc
    k.next_block()
    loaded, own_sem, gated, cw_done = k.sem("loaded"), k.sem("own"), k.sem("gated"), k.sem("cw_done")
    exp_ready, exp_done, turned, turned_done = k.sem("exp_ready"), k.sem("exp_done"), k.sem("turned"), k.sem("turned_done")
    b2_ready, b2_added = k.sem("b2_ready"), k.sem("b2_added")
    with ExitStack() as c, nc.Block() as block:
        wg_sb = k.sb(c, "wg", [P, KD, E])
        bg_sb = k.sb(c, "bg", [P, E])
        b2_sb = k.sb(c, "b2", [E, D])
        iota = k.sb(c, "iota", [P, E])
        logit = k.sb(c, "logit", [P, NT, E])
        prob = k.sb(c, "prob", [P, NT, E])
        m1 = k.sb(c, "gate_max", [P, NT])
        ssum = k.sb(c, "gate_sum", [P, NT])
        inv = k.sb(c, "gate_inv", [P, NT])
        best = k.sb(c, "best", [P, NT, 8])
        best_at = k.sb(c, "best_at", [P, NT, 8], U32)
        at = k.sb(c, "at_f", [P, NT, 8])
        hot = k.sb(c, "hot", [P, 2, NT, E])
        cwt = k.sb(c, "cwt", [E, NT, P])

        def wide(a):
            return a.unsqueeze(2).to_broadcast([P, NT, E])

        @block.sync
        def _(sp):
            sp.dma_start(wg_sb[:, :, :], wg.rearrange("(k p) n -> p k n", p=P)).then_inc(loaded, 16)
            sp.dma_start(bg_sb[:, :], bg.partition_broadcast(P)).then_inc(loaded, 16)
            sp.dma_start(b2_sb[:, :], b2).then_inc(loaded, 16)
            sp.dma_start(iota[:, :], k.iota_in).then_inc(loaded, 16)

        @block.tensor
        def _(pe):
            pe.wait_ge(loaded, 64)
            for t in range(NT):
                for kd in range(KD):
                    last = pe.matmul(k.ps[:, 0, t * E:(t + 1) * E], k.xt[:, kd, t * P:(t + 1) * P], wg_sb[:, kd, :],
                                     start=kd == 0, stop=kd == KD - 1)
            last.then_inc(gated, 1)
            pe.wait_ge(cw_done, 1)
            for g in range(NG):
                for j in range(TPG):
                    last = pe.transpose(k.ps[0:E, 1 + g, j * P:(j + 1) * P], cw[:, g * TPG + j, :], k.ident[:, :])
                last.then_inc(turned, 1)
            for t in range(NT):
                pe.wait_ge(turned_done, t // TPG + 1)
                wait(pe, b2_added, t - 1)
                pe.matmul(k.ps[:, 5 + t % 2, 0:D], cwt[:, t, :], b2_sb[:, :], start=True, stop=True).then_inc(b2_ready, 1)

        @block.scalar
        def _(act):
            act.wait_ge(exp_ready, 1)
            act.activation(prob[:, :, :].rearrange("p t e -> p (t e)"), logit[:, :, :].rearrange("p t e -> p (t e)"),
                           ACT.Exp).then_inc(exp_done, 1)
            for g in range(NG):
                act.wait_ge(turned, g + 1)
                act.activation(cwt[:, g * TPG:(g + 1) * TPG, :].rearrange("p t n -> p (t n)"), k.ps[0:E, 1 + g, :],
                               ACT.Copy).then_inc(turned_done, 1)

        @block.vector
        def _(dve):
            own = Steps(dve, own_sem)

            def step(ins):
                own.did(ins)
                own.wait()

            dve.wait_ge(loaded, 64)
            dve.wait_ge(gated, 1)
            step(dve.tensor_tensor(logit[:, :, :], k.ps[:, 0, 0:NT * E].rearrange("p (t e) -> p t e", e=E),
                                   bg_sb[:, :].unsqueeze(1).to_broadcast([P, NT, E]), ALU.add))
            step(dve.tensor_reduce(m1[:, :], logit[:, :, :], AX, ALU.max))
            dve.tensor_tensor(logit[:, :, :], logit[:, :, :], wide(m1[:, :]), ALU.subtract).then_inc(exp_ready, 1)
            dve.wait_ge(exp_done, 1)
            step(dve.tensor_reduce(ssum[:, :], prob[:, :, :], AX, ALU.add))
            step(dve.reciprocal(inv[:, :], ssum[:, :]))
            step(dve.tensor_tensor(prob[:, :, :], prob[:, :, :], wide(inv[:, :]), ALU.mult))
            for t in range(NT):
                own.did(dve.max(best[:, t, :], prob[:, t, :]))
            own.wait()
            for t in range(NT):
                own.did(dve.max_index(best_at[:, t, :], best[:, t, :], prob[:, t, :]))
            own.wait()
            own.did(dve.tensor_copy(at[:, :, :], best_at[:, :, :]))
            step(dve.tensor_tensor(ssum[:, :], best[:, :, 0], best[:, :, 1], ALU.add))
            step(dve.tensor_scalar(ssum[:, :], ssum[:, :], 1e-8, None, ALU.add))
            step(dve.reciprocal(inv[:, :], ssum[:, :]))
            for r in range(2):
                step(dve.tensor_tensor(m1[:, :], best[:, :, r], inv[:, :], ALU.mult))
                step(dve.tensor_tensor(hot[:, r, :, :], iota[:, :].unsqueeze(1).to_broadcast([P, NT, E]),
                                       wide(at[:, :, r]), ALU.is_equal))
                step(dve.tensor_tensor(hot[:, r, :, :], hot[:, r, :, :], wide(m1[:, :]), ALU.mult))
            dve.tensor_tensor(cw[:, :, :], hot[:, 0, :, :], hot[:, 1, :, :], ALU.add).then_inc(cw_done, 1)
            for t in range(NT):
                dve.wait_ge(b2_ready, t + 1)
                dve.tensor_tensor(k.x[:, t, :], k.x[:, t, :], k.ps[:, 5 + t % 2, 0:D], ALU.add).then_inc(b2_added, 1)


def experts(k, cw, w1, b1, w2):
    nc = k.nc
    k.next_block()
    w_in = [k.sem(f"w_in{u}") for u in range(2)]
    pre_ready, h_done, used, y_ready, added, picked = (
        k.sem("pre_ready"), k.sem("h_done"), k.sem("used"), k.sem("y_ready"), k.sem("added"), k.sem("picked"))
    GE = NG
    BG = 2 * GE
    with ExitStack() as c, nc.Block() as block:
        w1_sb = k.sb(c, "e_w1", [P, 2, KD, F])
        w2_sb = k.sb(c, "e_w2", [P, 2, FT, D])
        b1_sb = k.sb(c, "e_b1", [P, 2, FT])
        cwu = k.sb(c, "e_cw", [P, 2, NT])
        ht = k.sb(c, "e_ht", [P, 2, FT, G])

        def bodies(eng, body):
            body(0, True, False)
            with eng.Fori(1, E // 2 - 1) as i:
                body(i, False, False)
            body(E // 2 - 1, False, True)

        @block.sync
        def _(sp):
            def body(i, first, last):
                for u in range(2):
                    if not first:
                        sp.wait_ge(y_ready, (i - 1) * 2 * NT + (u + 1) * NT)
                    e = i * 2 + u
                    sp.dma_start(w1_sb[:, u, :, :], w1[bass.ds(e, 1)].rearrange("a (k p) n -> p (a k) n", p=P)).then_inc(w_in[u], 16)
                    sp.dma_start(b1_sb[:, u, :], b1[bass.ds(e, 1)].rearrange("a p k -> p (a k)")).then_inc(w_in[u], 16)
                    sp.dma_start(w2_sb[:, u, :, :], w2[bass.ds(e, 1)].rearrange("a (k p) n -> p (a k) n", p=P)).then_inc(w_in[u], 16)
            bodies(sp, body)

        @block.tensor
        def _(pe):
            def up(i, s):
                u, g = divmod(s % BG, GE)
                if g == 0:
                    pe.wait_ge(w_in[u], (i + s // BG + 1) * 48)
                for f in range(FT):
                    wait(pe, h_done, i * BG * FT + s * FT + f - 3)
                    for kd in range(KD):
                        last = pe.matmul(k.ps[:, f % 4, :], w1_sb[:, u, kd, f * P:(f + 1) * P],
                                         k.xt[:, kd, g * G:(g + 1) * G], start=kd == 0, stop=kd == KD - 1)
                    last.then_inc(pre_ready, 1)

            def down(i, s):
                u, g = divmod(s, GE)
                pe.wait_ge(h_done, (i * BG + s + 1) * FT)
                for j in range(TPG):
                    wait(pe, added, (i * BG + s) * TPG + j - 3)
                    for f in range(FT):
                        last = pe.matmul(k.ps[:, 4 + j, 0:D], ht[:, s % 2, f, j * P:(j + 1) * P], w2_sb[:, u, f, :],
                                         start=f == 0, stop=f == FT - 1)
                    last.then_inc(y_ready, 1)

            up(0, 0)

            def body(i, first, last):
                for s in range(BG):
                    if not (last and s == BG - 1):
                        up(i, s + 1)
                    down(i, s)
            bodies(pe, body)

        @block.scalar
        def _(act):
            def body(i, first, last):
                for s in range(BG):
                    u, g = divmod(s, GE)
                    if g == 0:
                        act.wait_ge(w_in[u], (i + 1) * 48)
                    for f in range(FT):
                        act.wait_ge(pre_ready, (i * BG + s) * FT + f + 1)
                        if f == 0:
                            wait(act, y_ready, (i * BG + s - 1) * TPG)
                        act.activation(ht[:, s % 2, f, :], k.ps[:, f % 4, :], ACT.Gelu_apprx_tanh,
                                       bias=b1_sb[:, u, f:f + 1]).then_inc(h_done, 1)
            bodies(act, body)

        @block.vector
        def _(dve):
            def body(i, first, last):
                for u in range(2):
                    wait(dve, added, (i * 2 + u - 1) * NT)
                    dve.tensor_copy(cwu[:, u, :], cw[:, :, bass.ds(i * 2 + u, 1)].rearrange("p t a -> p (t a)")).then_inc(picked, 1)
                    dve.wait_ge(picked, i * 2 + u + 1)
                    for t in range(NT):
                        n = (i * 2 + u) * NT + t
                        dve.wait_ge(y_ready, n + 1)
                        wait(dve, added, n - NT + 1)
                        dve.scalar_tensor_tensor(out=k.x[:, t, :], in0=k.ps[:, 4 + t % TPG, 0:D], scalar=cwu[:, u, t:t + 1],
                                                 in1=k.x[:, t, :], op0=ALU.mult, op1=ALU.add).then_inc(added, 1)
            bodies(dve, body)


INS = ["x", "L0_attn_W_down_kv", "L0_attn_W_up_k", "L0_attn_W_up_v", "L0_attn_Wq", "L0_attn_Wo",
       "L0_xattn_bq", "L0_xattn_bk", "L0_xattn_bv", "L0_xattn_bo", "L0_ffn_b1", "L0_ffn_b2",
       "L1_attn_Wq", "L1_attn_bq", "L1_attn_Wk", "L1_attn_bk", "L1_attn_Wv", "L1_attn_bv", "L1_attn_Wo", "L1_attn_bo",
       "L1_attn_random_matrix", "L1_xattn_bq", "L1_xattn_bk", "L1_xattn_bv", "L1_xattn_bo",
       "L1_ffn_Wg", "L1_ffn_bg", "L1_ffn_W1", "L1_ffn_b1", "L1_ffn_W2", "L1_ffn_b2"]
TURNED = {"wk_t": "L0_attn_Wk", "wv_t": "L0_attn_Wv", "x0q": "L0_xattn_Wq", "x0k": "L0_xattn_Wk", "x0v": "L0_xattn_Wv",
          "x0o": "L0_xattn_Wo", "x1q": "L1_xattn_Wq", "x1k": "L1_xattn_Wk", "x1v": "L1_xattn_Wv", "x1o": "L1_xattn_Wo",
          "w1_t": "L0_ffn_w1", "w2_t": "L0_ffn_w2"}
SQUARE = ["L0_attn_Wq", "L0_attn_Wo", "wk_t", "wv_t", "x0q", "x0k", "x0v", "x0o",
          "L1_attn_Wq", "L1_attn_Wk", "L1_attn_Wv", "L1_attn_Wo", "x1q", "x1k", "x1v", "x1o"]


def program(nc, d, out, upto=99):
    with ExitStack() as ctx:
        k = Core(nc)
        k.x = k.sb(ctx, "x", [P, NT, D])
        k.xt = k.sb(ctx, "xt", [P, KD, T])
        attn = k.sb(ctx, "attn", [P, NT, D])
        k.ident = k.sb(ctx, "ident", [P, P])
        k.hmask = k.sb(ctx, "hmask", [P, HP])
        k.iota_in = d["c_iota"]
        k.ps = ctx.enter_context(nc.psum_tensor("banks", [P, 8, 512], F32))
        k.w = {name: k.sb(ctx, name, [P, KD, D]) for name in SQUARE}
        q_scratch = nc.dram_tensor("q_parts", (3, B * D, S), BF16).ap()
        k_scratch = nc.dram_tensor("k_parts", (3, B * D, S), BF16).ap()
        w = k.w
        with ExitStack() as c:
            k.wd = k.sb(c, "wd", [P, KD, L])
            k.wuk = k.sb(c, "wuk", [L, D])
            k.wuv = k.sb(c, "wuv", [L, D])
            k.decay = k.sb(c, "decay", [P, (2 * QT - 1) * P])
            v_heads = k.sb(c, "v_heads", [P, B * H, QT, HD])
            load_constants(k, d)
            if upto >= 1:
                normalise(k)
                latent_projections(k, v_heads, q_scratch, k_scratch)
                latent_attention(k, v_heads, attn, k.decay, q_scratch, k_scratch)
                project_out(k, w["L0_attn_Wo"], None, attn)
        if upto >= 2:
            normalise(k)
            cross_attention(k, attn, w["x0q"], w["x0k"], w["x0v"], d["L0_xattn_bq"], d["L0_xattn_bk"], d["L0_xattn_bv"],
                            d["c_mask0"], d["c_fill0"], d["c_ctx_t"])
            project_out(k, w["x0o"], d["L0_xattn_bo"], attn)
        if upto >= 3:
            with ExitStack() as c:
                w1q = k.sb(c, "w1q", [P, KD, F], BF16)
                w2q = k.sb(c, "w2q", [P, FT, D], BF16)
                winv = k.sb(c, "winv", [P, 2])
                quantise_weights(k, None, [w1q[:, :, :].rearrange("p k n -> p (k n)"), w2q[:, :, :].rearrange("p k n -> p (k n)")],
                                 winv, [(d["w1_t"], KD), (d["w2_t"], FT)], None)
                ternary_ffn(k, w1q, w2q, winv, d["L0_ffn_b1"], d["L0_ffn_b2"])
        if upto >= 4:
            normalise(k)
            feature_attention(k, attn, w["L1_attn_Wq"], w["L1_attn_Wk"], w["L1_attn_Wv"],
                              d["L1_attn_bq"], d["L1_attn_bk"], d["L1_attn_bv"], d["L1_attn_random_matrix"])
            project_out(k, w["L1_attn_Wo"], d["L1_attn_bo"], attn)
        if upto >= 5:
            normalise(k)
            cross_attention(k, attn, w["x1q"], w["x1k"], w["x1v"], d["L1_xattn_bq"], d["L1_xattn_bk"], d["L1_xattn_bv"],
                            d["c_mask1"], d["c_fill1"], d["c_ctx_t"])
            project_out(k, w["x1o"], d["L1_xattn_bo"], attn)
        if upto >= 6:
            normalise(k)
            with ExitStack() as c:
                cw = k.sb(c, "cw", [P, NT, E])
                route(k, cw, d["L1_ffn_Wg"], d["L1_ffn_bg"], d["L1_ffn_b2"])
                experts(k, cw, d["L1_ffn_W1"], d["L1_ffn_b1"], d["L1_ffn_W2"])
        k.next_block()
        stored = k.sem("stored")
        with nc.Block() as block:
            @block.sync
            def _(sp):
                sp.dma_start(out.rearrange("b (t p) n -> p (b t) n", p=P), k.x[:, :, :]).then_inc(stored, 16)
                sp.wait_ge(stored, 16)


COLUMNS = ["L0_xattn_bq", "L0_xattn_bk", "L1_attn_bq", "L1_attn_bk", "L1_xattn_bq", "L1_xattn_bk", "L1_ffn_b1"]


def split3(v):
    rows = []
    for _ in range(3):
        m, e = np.frexp(v)
        part = np.trunc(m * 256.0) / 256.0 * 2.0 ** e
        rows.append(part)
        v = v - part
    assert v == 0
    return np.repeat(np.array(rows, np.float32)[:, None], P, axis=1)


def layout(inputs):
    a = {n: np.ascontiguousarray(inputs[n]) for n in INS}
    for n, src in TURNED.items():
        a[n] = np.ascontiguousarray(np.swapaxes(np.asarray(inputs[src]), -1, -2))
    for n in COLUMNS:
        b = np.asarray(inputs[n])
        a[n] = np.ascontiguousarray(np.swapaxes(b.reshape(b.shape[:-1] + (-1, P)), -1, -2))
    a["c_ctx_t"] = np.ascontiguousarray(np.asarray(inputs["ctx_1024"]).reshape(B * C, D).T)
    a["c_mask0"] = np.ascontiguousarray(inputs["mask_BxS2_bf1"]).view(np.uint8).reshape(B * C)
    a["c_mask1"] = np.ascontiguousarray(inputs["mask_Bx1x1xS2_ik0"]).reshape(B * C)
    a["c_fill0"], a["c_fill1"] = split3(-1e8), split3(-1e9)
    a["c_ident"] = np.eye(P, dtype=np.float32)
    a["c_hmask"] = (np.arange(P)[:, None] // HD == np.arange(HP)[None, :]).astype(np.float32)
    a["c_iota"] = np.repeat(np.arange(E, dtype=np.float32)[None, :], P, axis=0)
    width = (2 * QT - 1) * P
    a["c_decay"] = np.exp(-DECAY * np.abs(np.arange(P)[:, None] + (QT - 1) * P - np.arange(width)[None, :])).astype(np.float32)
    return a


def kernel(**inputs):
    import concourse.bacc as bacc
    from concourse.bass_utils import run_bass_kernel_spmd

    nc = bacc.Bacc("TRN2", target_bir_lowering=False, num_devices=1)
    arrays = layout(inputs)
    d = {n: nc.dram_tensor(f"in_{n}", a.shape, mybir.dt.from_np(a.dtype), kind="ExternalInput").ap()
         for n, a in arrays.items()}
    out = nc.dram_tensor("out_0", (B, S, D), F32, kind="ExternalOutput").ap()
    program(nc, d, out)
    got = run_bass_kernel_spmd(nc, [{f"in_{n}": a for n, a in arrays.items()}], core_ids=[0])
    return got.results[0]["out_0"]
```

```python
from contextlib import ExitStack

import numpy as np

import concourse.bass as bass
from concourse import mybir

F32 = mybir.dt.float32
F32R = mybir.dt.float32r
BF16 = mybir.dt.bfloat16
U32 = mybir.dt.uint32
U8 = mybir.dt.uint8
I32 = mybir.dt.int32
ALU = mybir.AluOpType
ACT = mybir.ActivationFunctionType
AX = mybir.AxisListType.X

P = 128
B, S, D, H = 2, 1024, 256, 16
HD = D // H
T = B * S
KD = D // P
HP = P // HD
NT = T // P
TPG = 4
NG = NT // TPG
G = TPG * P
QT = S // P
C = 77
L = 64
F = 1024
FT = F // P
M = 64
E = 8
SLOT_TILES = 2 * NT + E - 1
IOTA = 40
LN_EPS = 1e-5
CLAMP = 10000.0
DECAY = 0.01 * 0.01
ROUND = 1.5 * 2.0 ** 23


def wait(eng, sem, value):
    if isinstance(value, int) and value <= 0:
        return
    eng.wait_ge(sem, value)


class Steps:

    def __init__(self, eng, sem, start=0):
        self.eng, self.sem, self.n = eng, sem, start

    def did(self, ins):
        ins.then_inc(self.sem, 1)
        self.n += 1

    def wait(self):
        self.eng.wait_ge(self.sem, self.n)


class Core:

    def __init__(self, nc):
        self.nc, self.block = nc, 0
        self.sems, self.zeroed = [], []

    def sb(self, ctx, name, shape, dt=F32):
        return ctx.enter_context(self.nc.sbuf_tensor(f"{name}_sb", list(shape), dt))

    def sem(self, name):
        self.sems.append(self.nc.alloc_semaphore(name=f"b{self.block}_{name}"))
        return self.sems[-1]

    def next_block(self):
        for s in self.zeroed:
            self.nc.release_semaphore(s)
        for s in self.sems:
            self.nc.gpsimd.sem_clear(s)
        self.sems, self.zeroed = [], self.sems
        self.block += 1


def load_constants(k, d):
    nc = k.nc
    k.next_block()
    x_in, small_in, weights_in, zeros_set = k.sem("x_in"), k.sem("small_in"), k.sem("weights_in"), k.sem("zeros_set")
    with nc.Block() as block:
        @block.gpsimd
        def _(pool):
            pool.memset(k.zeros[:, :], 0.0).then_inc(zeros_set, 1)
            pool.wait_ge(zeros_set, 1)
            pool.wait_ge(x_in, 16)
            pool.dma_start(k.slots_x.rearrange("(t p) n -> p t n", p=P),
                           k.zeros[:, :].unsqueeze(1).to_broadcast([P, SLOT_TILES, D])).then_inc(k.slots_zeroed, 16)

        @block.sync
        def _(sp):
            sp.dma_start(k.x[:, :, :], d["x"].rearrange("b (t p) n -> p (b t) n", p=P)).then_inc(x_in, 16)
            sp.dma_start(k.ident[:, :], d["c_ident"]).then_inc(small_in, 16)
            sp.dma_start(k.hmask[:, :], d["c_hmask"]).then_inc(small_in, 16)
            sp.dma_start(k.wd[:, :, :], d["L0_attn_W_down_kv"].rearrange("(k p) n -> p k n", p=P)).then_inc(small_in, 16)
            sp.dma_start(k.wuk[:, :], d["L0_attn_W_up_k"]).then_inc(small_in, 16)
            sp.dma_start(k.wuv[:, :], d["L0_attn_W_up_v"]).then_inc(small_in, 16)
            sp.wait_ge(x_in, 16)
            sp.dma_start(k.decay[:, :], d["c_decay"]).then_inc(small_in, 16)
            sp.wait_ge(small_in, 6 * 16)

        @block.scalar
        def _(act):
            for name, w in k.w.items():
                act.dma_start(w[:, :, :], d[name].rearrange("(k p) n -> p k n", p=P)).then_inc(weights_in, 16)
            act.wait_ge(weights_in, 16 * len(k.w))


def normalise(k, keep=None):
    nc = k.nc
    k.next_block()
    dve_own, var_ready, std_ready = k.sem("dve_own"), k.sem("var_ready"), k.sem("std_ready")
    xn_ready, turned, xt_done = k.sem("xn_ready"), k.sem("turned"), k.sem("xt_done")
    with ExitStack() as c, nc.Block() as block:
        sid = k.block
        st = k.sb(c, f"st{sid}", [P, NT, 6])
        mv = k.sb(c, f"mv{sid}", [P, NT, 2])
        var = k.sb(c, f"var{sid}", [P, NT])
        std = k.sb(c, f"std{sid}", [P, NT])
        std2 = k.sb(c, f"std2{sid}", [P, NT])
        rstd = k.sb(c, f"rstd{sid}", [P, NT])
        if keep is None:
            ring = k.sb(c, f"xn{sid}", [P, 2 * TPG, D])

        def xn(t):
            return ring[:, t % (2 * TPG), :] if keep is None else keep[:, t, :]

        @block.vector
        def _(dve):
            own = Steps(dve, dve_own)
            for t in range(NT):
                own.did(dve.bn_stats(st[:, t, :], k.x[:, t, :]))
            own.wait()
            for t in range(NT):
                own.did(dve.bn_aggr(mv[:, t, :], st[:, t, :]))
            own.wait()
            dve.tensor_scalar(var[:, :], mv[:, :, 1], LN_EPS, None, ALU.add).then_inc(var_ready, 1)
            dve.wait_ge(std_ready, 1)
            own.did(dve.reciprocal(rstd[:, :], std[:, :]))
            own.wait()
            own.did(dve.tensor_tensor(std2[:, :], var[:, :], rstd[:, :], ALU.mult))
            own.wait()
            own.did(dve.tensor_tensor(std[:, :], std2[:, :], std[:, :], ALU.add))
            own.wait()
            own.did(dve.tensor_scalar(std2[:, :], std[:, :], 0.5, None, ALU.mult))
            own.wait()
            own.did(dve.reciprocal(rstd[:, :], std2[:, :]))
            own.wait()
            for t in range(NT):
                g, j = divmod(t, TPG)
                if j == 0:
                    wait(dve, turned, g - 1)
                dve.tensor_scalar(xn(t), k.x[:, t, :], mv[:, t, 0:1], rstd[:, t:t + 1],
                                  ALU.subtract, ALU.mult).then_inc(xn_ready, 1)

        @block.scalar
        def _(act):
            act.wait_ge(var_ready, 1)
            act.activation(std[:, :], var[:, :], ACT.Sqrt).then_inc(std_ready, 1)
            for g in range(NG):
                act.wait_ge(turned, g + 1)
                for kd in range(KD):
                    act.activation(k.xt[:, kd, g * G:(g + 1) * G], k.ps[:, 2 * (g % 2) + kd, :],
                                   ACT.Copy).then_inc(xt_done, 1)

        @block.tensor
        def _(pe):
            for g in range(NG):
                wait(pe, xt_done, KD * (g - 1))
                for j in range(TPG):
                    pe.wait_ge(xn_ready, g * TPG + j + 1)
                    for kd in range(KD):
                        last = pe.transpose(k.ps[:, 2 * (g % 2) + kd, j * P:(j + 1) * P],
                                            xn(g * TPG + j)[:, kd * P:(kd + 1) * P], k.ident[:, :])
                last.then_inc(turned, 1)


def project_out(k, w, bias, attn):
    nc = k.nc
    k.next_block()
    bias_in, biased = k.sem("bias_in"), k.sem("biased")
    turned, at_done = k.sem("turned"), k.sem("at_done")
    out_ready, added = k.sem("out_ready"), k.sem("added")
    with ExitStack() as c, nc.Block() as block:
        sid = k.block
        at = k.sb(c, f"at{sid}", [P, KD, 2, G])
        bb = k.sb(c, f"bb{sid}", [P, D])

        @block.sync
        def _(sp):
            if bias is not None:
                sp.dma_start(bb[:, :], bias.partition_broadcast(P)).then_inc(bias_in, 16)

        @block.gpsimd
        def _(pool):
            if bias is not None:
                pool.wait_ge(bias_in, 16)
                for t in range(NT):
                    pool.tensor_tensor(k.x[:, t, :], k.x[:, t, :], bb[:, :], ALU.add).then_inc(biased, 1)

        @block.tensor
        def _(pe):
            for g in range(NG):
                wait(pe, at_done, KD * (g - 1))
                for j in range(TPG):
                    for kd in range(KD):
                        last = pe.transpose(k.ps[:, 2 * (g % 2) + kd, j * P:(j + 1) * P],
                                            attn[:, g * TPG + j, kd * P:(kd + 1) * P], k.ident[:, :])
                last.then_inc(turned, 1)
                for j in range(TPG):
                    t = g * TPG + j
                    if j == 0:
                        pe.wait_ge(at_done, KD * (g + 1))
                    wait(pe, added, t - TPG + 1)
                    for kd in range(KD):
                        last = pe.matmul(k.ps[:, 4 + j, 0:D], at[:, kd, g % 2, j * P:(j + 1) * P], w[:, kd, :],
                                         start=kd == 0, stop=kd == KD - 1)
                    last.then_inc(out_ready, 1)

        @block.scalar
        def _(act):
            for g in range(NG):
                act.wait_ge(turned, g + 1)
                wait(act, out_ready, (g - 1) * TPG)
                for kd in range(KD):
                    act.activation(at[:, kd, g % 2, :], k.ps[:, 2 * (g % 2) + kd, :], ACT.Copy).then_inc(at_done, 1)

        @block.vector
        def _(dve):
            for t in range(NT):
                if bias is not None:
                    dve.wait_ge(biased, t + 1)
                dve.wait_ge(out_ready, t + 1)
                dve.tensor_tensor(k.x[:, t, :], k.x[:, t, :], k.ps[:, 4 + t % TPG, 0:D], ALU.add).then_inc(added, 1)


def latent_projections(k, v_heads, q_scratch, k_scratch):
    nc = k.nc
    k.next_block()
    wsum_ready, wkv_ready, wkv_done = k.sem("wsum_ready"), k.sem("wkv_ready"), k.sem("wkv_done")
    lat_ready, lat_done = k.sem("lat_ready"), k.sem("lat_done")
    qk_ready, part1_done, rest1_done, part2_done, part3_done = (
        k.sem("qk_ready"), k.sem("part1_done"), k.sem("rest1_done"), k.sem("part2_done"), k.sem("part3_done"))
    v_ready, v_done = k.sem("v_ready"), k.sem("v_done")
    bound_own, largest_ready, largest_turned = k.sem("bound_own"), k.sem("largest_ready"), k.sem("largest_turned")
    stored = [k.sem(f"stored{s}") for s in range(4)]
    scale = 1.0 / 16.0
    NP = NG * 2 * KD
    with ExitStack() as c, nc.Block() as block:
        wsum = k.sb(c, "wsum", [P, KD, D])
        wkv = k.sb(c, "wkv", [P, KD, L])
        lat = k.sb(c, "lat", [L, T])
        parts = k.sb(c, "parts", [P, 4, 3, G], BF16)
        rest = k.sb(c, "rest", [P, 4, G])
        largest = k.sb(c, "largest", [P, NP])
        sides = k.sb(c, "sides", [P, 2])
        side_max = k.sb(c, "side_max", [1, 2])
        bound = k.sb(c, "bound", [1, 1])

        @block.tensor
        def _(pe):
            pe.wait_ge(wsum_ready, 1)
            for m in range(KD):
                for kd in range(KD):
                    last = pe.matmul(k.ps[:, 7, m * L:(m + 1) * L], wsum[:, kd, m * P:(m + 1) * P], k.wd[:, kd, :],
                                     start=kd == 0, stop=kd == KD - 1)
            last.then_inc(wkv_ready, 1)
            pe.wait_ge(wkv_done, 1)
            for g in range(NG):
                rows = slice(g * G, (g + 1) * G)
                wait(pe, lat_done, g)
                for kd in range(KD):
                    last = pe.matmul(k.ps[0:L, 4, :], wkv[:, kd, :], k.xt[:, kd, rows], start=kd == 0, stop=kd == KD - 1)
                last.then_inc(lat_ready, 1)
                for m in range(KD):
                    n = 4 * g + m
                    wait(pe, rest1_done, n - 3)
                    wait(pe, part1_done, n - 3)
                    for kd in range(KD):
                        last = pe.matmul(k.ps[:, m, :], k.w["L0_attn_Wq"][:, kd, m * P:(m + 1) * P],
                                         k.xt[:, kd, rows], start=kd == 0, stop=kd == KD - 1)
                    last.then_inc(qk_ready, 1)
                pe.wait_ge(lat_done, g + 1)
                for m in range(KD):
                    n = 4 * g + 2 + m
                    wait(pe, rest1_done, n - 3)
                    wait(pe, part1_done, n - 3)
                    pe.matmul(k.ps[:, 2 + m, :], k.wuk[:, m * P:(m + 1) * P], lat[:, rows],
                              start=True, stop=True).then_inc(qk_ready, 1)
                for j in range(TPG):
                    t = g * TPG + j
                    wait(pe, v_done, t - 1)
                    pe.matmul(k.ps[:, 5 + t % 2, 0:D], lat[:, t * P:(t + 1) * P], k.wuv[:, :],
                              start=True, stop=True).then_inc(v_ready, 1)
            pe.wait_ge(largest_ready, 1)
            for side in range(2):
                last = pe.transpose(k.ps[0:1, 7, side * P:(side + 1) * P], sides[:, side:side + 1], k.ident[:, :])
            last.then_inc(largest_turned, 1)

        @block.vector
        def _(dve):
            own = Steps(dve, bound_own)
            dve.tensor_tensor(wsum[:, :, :], k.w["wk_t"][:, :, :], k.w["wv_t"][:, :, :], ALU.add).then_inc(wsum_ready, 1)
            dve.wait_ge(wkv_ready, 1)
            dve.tensor_copy(wkv[:, :, :], k.ps[:, 7, 0:KD * L].rearrange("p (m n) -> p m n", m=KD)).then_inc(wkv_done, 1)
            for n in range(NP):
                s = n % 4
                f = scale if s < 2 else 1.0
                dve.wait_ge(part1_done, n + 1)
                dve.scalar_tensor_tensor(out=rest[:, s, :], in0=k.ps[:, s, :], scalar=f, in1=parts[:, s, 0, :],
                                         op0=ALU.mult, op1=ALU.subtract).then_inc(rest1_done, 1)
                dve.wait_ge(part2_done, n + 1)
                own.did(dve.tensor_reduce(largest[:, n:n + 1], parts[:, s, 0, :], AX, ALU.max, apply_absolute_value=True))
                dve.tensor_tensor(parts[:, s, 2, :], rest[:, s, :], parts[:, s, 1, :],
                                  ALU.subtract).then_inc(part3_done, 1)

            own.wait()
            by_piece = largest[:, :].rearrange("p (g a m) -> p g a m", a=2, m=KD)
            for side in range(2):
                ins = dve.tensor_reduce(sides[:, side:side + 1], by_piece[:, :, side, :], mybir.AxisListType.XY, ALU.max)
                if side == 0:
                    own.did(ins)
                    own.wait()
            ins.then_inc(largest_ready, 1)
            dve.wait_ge(largest_turned, 1)
            own.did(dve.tensor_reduce(side_max[:, :], k.ps[0:1, 7, 0:2 * P].rearrange("p (a n) -> p a n", a=2), AX, ALU.max))
            own.wait()
            own.did(dve.tensor_tensor(bound[:, :], side_max[:, 0:1], side_max[:, 1:2], ALU.mult))
            own.wait()
            own.did(dve.tensor_scalar(k.inside[:, :], bound[:, :], 0.9 * CLAMP / HD, None, ALU.is_lt))
            own.wait()

        @block.scalar
        def _(act):
            for n in range(NP):
                g, s = divmod(n, 4)
                if s == 0:
                    act.wait_ge(lat_ready, g + 1)
                    act.activation(lat[:, g * G:(g + 1) * G], k.ps[0:L, 4, :], ACT.Copy).then_inc(lat_done, 1)
                act.wait_ge(qk_ready, n + 1)
                wait(act, stored[s], 16 * g)
                act.activation(parts[:, s, 0, :], k.ps[:, s, :], ACT.Copy,
                               scale=scale if s < 2 else 1.0).then_inc(part1_done, 1)
                act.wait_ge(rest1_done, n + 1)
                act.activation(parts[:, s, 1, :], rest[:, s, :], ACT.Copy).then_inc(part2_done, 1)
                if s == 3:
                    for t in range(g * TPG, (g + 1) * TPG):
                        b, q = divmod(t, QT)
                        act.wait_ge(v_ready, t + 1)
                        act.activation(v_heads[:, b * H:(b + 1) * H, q, :],
                                       k.ps[:, 5 + t % 2, 0:D].rearrange("p (h d) -> p h d", d=HD),
                                       ACT.Copy).then_inc(v_done, 1)

        @block.sync
        def _(sp):
            for n in range(NP):
                g, s = divmod(n, 4)
                b, half = divmod(g, 2)
                m = s % 2
                scratch = q_scratch if s < 2 else k_scratch
                sp.wait_ge(part3_done, n + 1)
                sp.dma_start(scratch[:, b * D + m * P:b * D + (m + 1) * P, half * G:(half + 1) * G]
                             .rearrange("c p n -> p c n"), parts[:, s, :, :]).then_inc(stored[s], 16)
            for s in range(4):
                sp.wait_ge(stored[s], 16 * NG)


def latent_attention(k, v_heads, attn, decay, q_scratch, k_scratch):
    nc = k.nc
    k.next_block()
    stack_in = [k.sem(f"stack_in{u}") for u in range(2)]
    scored, clipped, peaked, shifted = (
        k.sem("scored"), k.sem("clipped"), k.sem("peaked"), k.sem("shifted"))
    exp_done, v_staged = k.sem("exp_done"), k.sem("v_staged")
    p_turned = [k.sem(f"p_turned{u}") for u in range(2)]
    pt_done = [k.sem(f"pt_done{u}") for u in range(2)]
    mixed, mix_copied, mix_turned, inverted, weighted = (
        k.sem("mixed"), k.sem("mix_copied"), k.sem("mix_turned"), k.sem("inverted"), k.sem("weighted"))
    zeroed = k.sem("zeroed")
    BODY = B
    NB = H
    TB = BODY * QT
    GB = TB // TPG
    LAG = 3
    TRAIL = 2 * TPG
    MIX_PARTS = [range(0, 3), range(3, 6), range(6, QT)]
    with ExitStack() as c, nc.Block() as block:
        qs = k.sb(c, "q_stack", [96, BODY, S], BF16)
        ks = k.sb(c, "k_stack", [96, BODY, S], BF16)
        vh = k.sb(c, "v_head", [P, BODY, QT, 32])
        sc = k.sb(c, "clipped_scores", [P, S])
        pr = k.sb(c, "probs", [P, 4, S])
        peak = k.sb(c, "peak", [P, 8])
        shift = k.sb(c, "shift", [P, 8])
        minus = k.sb(c, "minus", [P, 1])
        sums = k.sb(c, "sums", [P, 4, TPG])
        inv = k.sb(c, "inv", [P, 2, TPG])
        pt = k.sb(c, "probs_t", [P, TPG, 2, QT, P])
        mix = k.sb(c, "mix", [P, 2, P])

        def bodies(eng, body):
            body(0, True, False)
            with eng.Fori(1, NB - 1) as i:
                body(i, False, False)
            body(NB - 1, False, True)

        def steps(eng, step):
            for s in range(TB):
                step(0, s, lambda tile: tile >= 0)
            with eng.Fori(1, NB - 1) as i:
                for s in range(TB):
                    step(i, s, lambda tile: True)
            for s in range(TB):
                step(NB - 1, s, lambda tile: True)
            for s in range(TRAIL):
                step(NB, s, lambda tile: tile < 0)

        def copy_half(eng, i, s, half):
            n = i * TB + s
            eng.wait_ge(p_turned[half], n + 1)
            wait(eng, mixed, i * GB + s // TPG - 1)
            dst = pt[:, s % 4, (s // TPG) % 2, half * TPG:(half + 1) * TPG, :].rearrange("p t n -> p (t n)")
            if eng is nc.vector:
                ins = eng.tensor_copy(dst, k.ps[:, 4 + half, :])
            else:
                ins = eng.activation(dst, k.ps[:, 4 + half, :], ACT.Copy)
            ins.then_inc(pt_done[half], 1)

        @block.sync
        def _(sp):
            def body(i, first, last):
                for u in range(BODY):
                    wait(sp, scored, (i - 1) * TB + (u + 1) * QT if not first else 0)
                    for stack, scratch, order in ((qs, q_scratch, "q"), (ks, k_scratch, "k")):
                        row = 0
                        for r in range(3):
                            n = 3 - r
                            src = scratch[:, bass.ds(i * HD + u * D, HD), :]
                            if order == "q":
                                for x in range(n):
                                    sp.dma_start(stack[row + x * HD:row + (x + 1) * HD, u, :],
                                                 src[r:r + 1].rearrange("c p n -> (c p) n")).then_inc(stack_in[u], 16)
                            else:
                                for x in range(n):
                                    sp.dma_start(stack[row + x * HD:row + (x + 1) * HD, u, :],
                                                 src[x:x + 1].rearrange("c p n -> (c p) n")).then_inc(stack_in[u], 16)
                            row += n * HD
            bodies(sp, body)

        @block.gpsimd
        def _(pool):
            pool.memset(vh[:, :, :, :], 0.0).then_inc(zeroed, 1)
            pool.memset(minus[:, :], -1.0).then_inc(zeroed, 1)
            pool.wait_ge(zeroed, 2)

            def body(i, first, last):
                for s in range(TB):
                    u, q = divmod(s, QT)
                    n = i * TB + s
                    if q == 0:
                        wait(pool, mixed, i * GB - GB + (u + 1) * (QT // TPG) if not first else 0)
                        pool.tensor_copy(vh[:, u, :, 0:HD], v_heads[:, bass.ds(i + u * H, 1), :, :]
                                         .rearrange("p a t d -> p (a t) d")).then_inc(v_staged, 1)
                    pool.wait_ge(peaked, n + 1)
                    wait(pool, exp_done, n - 7)
                    pool.tensor_tensor(shift[:, s % 8:s % 8 + 1], peak[:, s % 8:s % 8 + 1], minus[:, :],
                                       ALU.mult).then_inc(shifted, 1)
            bodies(pool, body)

        @block.tensor
        def _(pe):
            def scores(i, s):
                n = i * TB + s
                u, q = divmod(s % TB, QT)
                if q == 0:
                    pe.wait_ge(stack_in[u], (i + s // TB + 1) * 12 * 16)
                wait(pe, peaked, n - 1)
                for half in range(2):
                    last = pe.matmul(k.ps[:, 2 * (s % 2) + half, :], qs[:, u, q * P:(q + 1) * P],
                                     ks[:, u, half * 512:(half + 1) * 512], start=True, stop=True)
                last.then_inc(scored, 1)

            def turn(i, s):
                n = i * TB + s
                pe.wait_ge(exp_done, n + 1)
                for half in range(2):
                    wait(pe, pt_done[half], n)
                    for j in range(TPG):
                        last = pe.transpose(k.ps[:, 4 + half, j * P:(j + 1) * P],
                                            pr[:, s % 4, (half * TPG + j) * P:(half * TPG + j + 1) * P], k.ident[:, :])
                    last.then_inc(p_turned[half], 1)

            def mix_part(i, gs, part):
                gn = i * GB + gs
                u = gs % GB // (QT // TPG)
                if part == 0:
                    for half in range(2):
                        pe.wait_ge(pt_done[half], (gn + 1) * TPG)
                    pe.wait_ge(v_staged, i * BODY + gs // (QT // TPG) + 1)
                    wait(pe, mix_copied, gn)
                for kt in MIX_PARTS[part]:
                    for j in range(TPG):
                        last = pe.matmul(k.ps[32 * j:32 * j + 32, 6, 0:P], vh[:, u, kt, :],
                                         pt[:, j, gs % 2, kt, :], start=kt == 0, stop=kt == QT - 1)
                if part == len(MIX_PARTS) - 1:
                    last.then_inc(mixed, 1)

            def turn_mix(i, gs):
                gn = i * GB + gs
                pe.wait_ge(mix_copied, gn + 1)
                wait(pe, weighted, gn)
                pe.transpose(k.ps[:, 7, 0:P], mix[:, gs % 2, :], k.ident[:, :]).then_inc(mix_turned, 1)

            def step(i, s, due):
                if due(s - LAG):
                    turn(i, s - LAG)
                if s < TB and not (i is NB or (i is NB - 1 and s >= TB - 2)):
                    scores(i, s + 2)
                gs, part = divmod(s - TPG - LAG, TPG)
                if part < len(MIX_PARTS) and due(gs * TPG):
                    mix_part(i, gs, part)
                gs = s // TPG - 2
                if s % TPG == 2 and due(gs * TPG):
                    turn_mix(i, gs)

            scores(0, 0)
            scores(0, 1)
            steps(pe, step)

        @block.vector
        def _(dve):
            def weight(i, gs):
                gn = i * GB + gs
                u, half = divmod(gs % GB, QT // TPG)
                dve.wait_ge(exp_done, (gn + 1) * TPG)
                wait(dve, weighted, gn - 1)
                dve.reciprocal(inv[:, gs % 2, :], sums[:, gs % 4, :]).then_inc(inverted, 1)
                dve.wait_ge(inverted, gn + 1)
                dve.wait_ge(mix_turned, gn + 1)
                dve.tensor_tensor(
                    attn[:, u * QT + half * TPG:u * QT + (half + 1) * TPG, bass.ds((i + gs // GB) * HD, HD)],
                    k.ps[:, 7, 0:P].rearrange("p (t d) -> p t d", d=32)[:, :, 0:HD],
                    inv[:, gs % 2, :].unsqueeze(2).to_broadcast([P, TPG, HD]), ALU.mult).then_inc(weighted, 1)

            def clip(i, s):
                n = i * TB + s
                dve.wait_ge(scored, n + 1)
                wait(dve, peaked, n)
                dve.tensor_scalar(sc[:, :], k.ps[:, 2 * (s % 2):2 * (s % 2) + 2, :].rearrange("p a n -> p (a n)"),
                                  -CLAMP, CLAMP, ALU.max, ALU.min).then_inc(clipped, 1)
                dve.wait_ge(clipped, n + 1)

            def fade(i, s, scores):
                n = i * TB + s
                wait(dve, p_turned[1], n - 3)
                wait(dve, shifted, n - 7)
                off = (QT - 1 - s % QT) * P
                dve.nop(nofuse=True)
                dve.tensor_tensor_reduce(out=pr[:, s % 4, :], in0=scores, in1=decay[:, off:off + S],
                                         scale=1.0, scalar=-3.0e38, op0=ALU.mult, op1=ALU.max,
                                         accum_out=peak[:, s % 8:s % 8 + 1]).then_inc(peaked, 1)

            def trailing(i, s, due):
                if s % 2 == 1 and due(s - LAG):
                    copy_half(dve, i, s - LAG, 1)
                gs = s // TPG - 2
                if s % TPG == 3 and due(gs * TPG):
                    weight(i, gs)

            def clipping_step(i, s, due):
                if i is not NB:
                    clip(i, s)
                    fade(i, s, sc[:, :])
                trailing(i, s, due)

            def step(i, s, due):
                if i is not NB:
                    dve.wait_ge(scored, i * TB + s + 1)
                    fade(i, s, k.ps[:, 2 * (s % 2):2 * (s % 2) + 2, :].rearrange("p a n -> p (a n)"))
                trailing(i, s, due)

            inside = dve.value_load(k.inside[0:1, 0:1], min_val=0, max_val=1)
            with dve.If(inside > 0):
                steps(dve, step)
            with dve.Else():
                steps(dve, clipping_step)

        @block.scalar
        def _(act):
            def copy_mix(i, gs):
                gn = i * GB + gs
                act.wait_ge(mixed, gn + 1)
                wait(act, mix_turned, gn - 1)
                act.activation(mix[:, gs % 2, :], k.ps[:, 6, 0:P], ACT.Copy).then_inc(mix_copied, 1)

            def step(i, s, due):
                if due(s - LAG):
                    copy_half(act, i, s - LAG, 0)
                    if s % 2 == 0:
                        copy_half(act, i, s - LAG, 1)
                if i is not NB:
                    n = i * TB + s
                    act.wait_ge(shifted, n + 1)
                    wait(act, inverted, i * GB + s // TPG - 3)
                    act.activation(pr[:, s % 4, :], pr[:, s % 4, :], ACT.Exp, bias=shift[:, s % 8:s % 8 + 1],
                                   accum_out=sums[:, (s // TPG) % 4, s % 4:s % 4 + 1]).then_inc(exp_done, 1)
                gs = s // TPG - 2
                if s % TPG == 1 and due(gs * TPG):
                    copy_mix(i, gs)
            steps(act, step)


def cross_attention(k, attn, wq, wk, wv, bq, bk, bv, mask, fill, ctx_t):
    nc = k.nc
    k.next_block()
    loaded, own_sem = k.sem("loaded"), k.sem("own")
    kv_ready, operands_done = k.sem("kv_ready"), k.sem("operands_done")
    q_ready, q_done = k.sem("q_ready"), k.sem("q_done")
    scored, peaked, shifted = k.sem("scored"), k.sem("peaked"), k.sem("shifted")
    exp_done, p_turned, pt_done, mixed = k.sem("exp_done"), k.sem("p_turned"), k.sem("pt_done"), k.sem("mixed")
    floored, inverted, weighted = k.sem("floored"), k.sem("inverted"), k.sem("weighted")
    HB = 4
    NBK = H // HB
    V1 = HD + 1
    scale = 1.0 / 4.0
    with ExitStack() as c, nc.Block() as block:
        sid = k.block
        ctx_sb = k.sb(c, f"ctx{sid}", [P, KD, B * C])
        bq_sb = k.sb(c, f"bq{sid}", [P, KD])
        bk_sb = k.sb(c, f"bk{sid}", [P, KD])
        bv_sb = k.sb(c, f"bv{sid}", [C, D])
        mask_sb = k.sb(c, f"mask{sid}", [P, B * C], mask.dtype)
        hidden = k.sb(c, f"hidden{sid}", [P, B * C])
        keep = k.sb(c, f"keep{sid}", [P, B * C])
        hidden4 = k.sb(c, f"hidden4{sid}", [3, B, HB, C], BF16)
        fill_sb = k.sb(c, f"fill{sid}", [3, P])
        fill_b = k.sb(c, f"fillb{sid}", [3, P], BF16)
        kt = k.sb(c, f"kt{sid}", [P, KD, B * C])
        kbd = k.sb(c, f"kbd{sid}", [P, B, KD, HP, C])
        va = k.sb(c, f"va{sid}", [C, B, H, V1])
        qt = k.sb(c, f"qt{sid}", [P, KD, T])
        pr = k.sb(c, f"pr{sid}", [P, 2, H, C])
        peak = k.sb(c, f"peak{sid}", [P, 2, H])
        pt = k.sb(c, f"pt{sid}", [C, 2, H, P])
        inv = k.sb(c, f"inv{sid}", [P, 2, H])

        @block.sync
        def _(sp):
            sp.dma_start(ctx_sb[:, :, :], ctx_t.rearrange("(k p) n -> p k n", p=P)).then_inc(loaded, 16)
            sp.dma_start(bq_sb[:, :], bq).then_inc(loaded, 16)
            sp.dma_start(bk_sb[:, :], bk).then_inc(loaded, 16)
            sp.dma_start(bv_sb[:, :], bv.partition_broadcast(C)).then_inc(loaded, 16)
            sp.dma_start(mask_sb[:, :], mask.partition_broadcast(P)).then_inc(loaded, 16)
            sp.dma_start(fill_sb[:, :], fill).then_inc(loaded, 16)

        @block.tensor
        def _(pe):
            pe.wait_ge(loaded, 6 * 16)
            for m in range(KD):
                for kd in range(KD):
                    pe.matmul(k.ps[:, 4 + m, 0:B * C], wk[:, kd, m * P:(m + 1) * P], ctx_sb[:, kd, :],
                              start=kd == 0, stop=kd == KD - 1)
            for b in range(B):
                for kd in range(KD):
                    last = pe.matmul(k.ps[0:C, 6 + b, 0:D], ctx_sb[:, kd, b * C:(b + 1) * C], wv[:, kd, :],
                                     start=kd == 0, stop=kd == KD - 1)
            last.then_inc(kv_ready, 1)
            for g in range(NG):
                for m in range(KD):
                    n = KD * g + m
                    wait(pe, q_done, n - 3)
                    for kd in range(KD):
                        last = pe.matmul(k.ps[:, n % 4, :], wq[:, kd, m * P:(m + 1) * P],
                                         k.xt[:, kd, g * G:(g + 1) * G], start=kd == 0, stop=kd == KD - 1)
                    last.then_inc(q_ready, 1)
            pe.wait_ge(operands_done, 1)
            pe.wait_ge(q_done, KD * NG)

            def scores(t):
                b = t // QT
                wait(pe, shifted, t)
                for a in range(NBK):
                    kd, half = divmod(a, NBK // KD)
                    rhs = kbd[:, b, kd, half * HB:(half + 1) * HB, :].rearrange("p h n -> p (h n)")
                    pe.matmul(k.ps[:, a, 0:HB * C], qt[:, kd, t * P:(t + 1) * P], rhs, start=True, stop=False)
                    last = pe.matmul(k.ps[:, a, 0:HB * C], fill_b[:, :],
                                     hidden4[:, b, :, :].rearrange("p h n -> p (h n)"), start=False, stop=True)
                last.then_inc(scored, 1)

            scores(0)
            for t in range(NT):
                b = t // QT
                pe.wait_ge(exp_done, t + 1)
                for a in range(NBK):
                    n = NBK * t + a
                    wait(pe, pt_done, n - 2)
                    for h in range(HB):
                        last = pe.transpose(k.ps[0:C, 4 + n % 3, h * P:(h + 1) * P], pr[:, t % 2, a * HB + h, :],
                                            k.ident[:, :])
                    last.then_inc(p_turned, 1)
                if t + 1 < NT:
                    scores(t + 1)
                wait(pe, weighted, t)
                for h in range(H):
                    if h % HB == 0:
                        pe.wait_ge(pt_done, NBK * t + h // HB + 1)
                    last = pe.matmul(k.ps[:, 7, h * V1:(h + 1) * V1], pt[:, t % 2, h, :], va[:, b, h, :],
                                     start=True, stop=True)
                last.then_inc(mixed, 1)

        @block.vector
        def _(dve):
            own = Steps(dve, own_sem)
            dve.wait_ge(loaded, 6 * 16)
            own.did(dve.tensor_scalar(hidden[:, :], mask_sb[:, :], 0.0, None, ALU.is_equal))
            own.did(dve.memset(va[:, :, :, :], 1.0))
            own.did(dve.tensor_copy(fill_b[:, :], fill_sb[:, :]))
            own.wait()
            own.did(dve.tensor_scalar(keep[:, :], hidden[:, :], -1.0, 1.0, ALU.mult, ALU.add))
            for b in range(B):
                for h in range(HB):
                    own.did(dve.tensor_copy(hidden4[:, b, h, :], hidden[0:3, b * C:(b + 1) * C]))
            dve.wait_ge(kv_ready, 1)
            for m in range(KD):
                own.did(dve.tensor_scalar(kt[:, m, :], k.ps[:, 4 + m, 0:B * C], bk_sb[:, m:m + 1], scale,
                                          ALU.add, ALU.mult))
            own.wait()
            for m in range(KD):
                own.did(dve.tensor_tensor(kt[:, m, :], kt[:, m, :], keep[:, :], ALU.mult))
            own.wait()
            for b in range(B):
                own.did(dve.tensor_tensor(va[:, b, :, 0:HD], k.ps[0:C, 6 + b, 0:D].rearrange("p (h d) -> p h d", d=HD),
                                          bv_sb[:, :].rearrange("p (h d) -> p h d", d=HD), ALU.add))
                for m in range(KD):
                    for h in range(HP):
                        last = dve.tensor_scalar(kbd[:, b, m, h, :], kt[:, m, b * C:(b + 1) * C],
                                                 k.hmask[:, h:h + 1], None, ALU.mult)
                        if not (b == B - 1 and m == KD - 1 and h == HP - 1):
                            own.did(last)
            own.wait()
            last.then_inc(operands_done, 1)

            def weight(t):
                dve.wait_ge(mixed, t + 1)
                o = k.ps[:, 7, 0:H * V1].rearrange("p (h d) -> p h d", d=V1)
                dve.reciprocal(inv[:, t % 2, :], o[:, :, HD]).then_inc(inverted, 1)
                dve.wait_ge(inverted, t + 1)
                dve.tensor_tensor(attn[:, t, :].rearrange("p (h d) -> p h d", d=HD), o[:, :, 0:HD],
                                  inv[:, t % 2, :].unsqueeze(2).to_broadcast([P, H, HD]), ALU.mult).then_inc(weighted, 1)

            for t in range(NT):
                dve.wait_ge(scored, t + 1)
                s = k.ps[:, 0:NBK, 0:HB * C].rearrange("p a (h n) -> p a h n", n=C)
                dve.tensor_reduce(peak[:, t % 2, :].rearrange("p (a h) -> p a h", h=HB), s, AX, ALU.max).then_inc(peaked, 1)
                dve.wait_ge(peaked, t + 1)
                wait(dve, p_turned, NBK * (t - 1))
                dve.tensor_tensor(pr[:, t % 2, :, :].rearrange("p (a h) n -> p a h n", h=HB), s,
                                  peak[:, t % 2, :].rearrange("p (a h) -> p a h", h=HB).unsqueeze(3)
                                  .to_broadcast([P, NBK, HB, C]), ALU.subtract).then_inc(shifted, 1)
                if t > 0:
                    weight(t - 1)
            weight(NT - 1)

        @block.scalar
        def _(act):
            act.wait_ge(loaded, 6 * 16)
            for n in range(KD * NG):
                g, m = divmod(n, KD)
                act.wait_ge(q_ready, n + 1)
                act.activation(qt[:, m, g * G:(g + 1) * G], k.ps[:, n % 4, :], ACT.Identity,
                               bias=bq_sb[:, m:m + 1]).then_inc(q_done, 1)
            for t in range(NT):
                act.wait_ge(shifted, t + 1)
                act.activation(pr[:, t % 2, :, :].rearrange("p h n -> p (h n)"),
                               pr[:, t % 2, :, :].rearrange("p h n -> p (h n)"), ACT.Exp).then_inc(exp_done, 1)
                for a in range(NBK):
                    n = NBK * t + a
                    act.wait_ge(p_turned, n + 1)
                    wait(act, mixed, t - 1)
                    act.activation(pt[:, t % 2, a * HB:(a + 1) * HB, :].rearrange("p h n -> p (h n)"),
                                   k.ps[0:C, 4 + n % 3, :], ACT.Copy).then_inc(pt_done, 1)


def quantise_weights(k, raws, quants, winvs, sources, banks):
    nc = k.nc
    k.next_block()
    own_sem, loaded, summed, totalled = k.sem("own"), [k.sem(f"loaded{i}") for i in range(2)], k.sem("summed"), k.sem("totalled")
    with ExitStack() as c, nc.Block() as block:
        ones = k.sb(c, "ones_pp", [P, P])
        raw = [k.sb(c, f"raw{i}", [P, F * KD]) for i in range(2)]
        tmp = [k.sb(c, f"rawtmp{i}", [P, F * KD]) for i in range(2)]
        part = k.sb(c, "abs_sums", [P, 2])
        mean = k.sb(c, "abs_mean", [P, 2])
        wsc = k.sb(c, "w_scale", [P, 2])

        @block.sync
        def _(sp):
            for i, (src, kt) in enumerate(sources):
                sp.dma_start(raw[i][:, :].rearrange("p (k n) -> p k n", k=kt),
                             src.rearrange("(k p) n -> p k n", p=P)).then_inc(loaded[i], 16)

        @block.tensor
        def _(pe):
            pe.wait_ge(summed, 3)
            pe.matmul(k.ps[:, 0, 0:2], ones[:, :], part[:, :], start=True, stop=True).then_inc(totalled, 1)

        @block.scalar
        def _(act):
            for i in range(2):
                act.wait_ge(loaded[i], 16)
                act.activation(tmp[i][:, :], raw[i][:, :], ACT.Abs, accum_out=part[:, i:i + 1]).then_inc(summed, 1)

        @block.vector
        def _(dve):
            own = Steps(dve, own_sem)
            dve.memset(ones[:, :], 1.0).then_inc(summed, 1)
            dve.wait_ge(totalled, 1)
            own.did(dve.tensor_scalar(mean[:, :], k.ps[:, 0, 0:2], 1.0 / (F * D), 1e-5, ALU.mult, ALU.max))
            own.wait()
            own.did(dve.reciprocal(wsc[:, :], mean[:, :]))
            own.wait()
            own.did(dve.reciprocal(winvs[:, :], wsc[:, :]))
            for i in range(2):
                own.did(dve.tensor_scalar(tmp[i][:, :], raw[i][:, :], wsc[:, i:i + 1], ROUND, ALU.mult, ALU.add))
                own.wait()
                own.did(dve.tensor_scalar(raw[i][:, :], tmp[i][:, :], -ROUND, -1.0, ALU.add, ALU.max))
                own.wait()
                own.did(dve.tensor_scalar(quants[i], raw[i][:, :], 1.0, None, ALU.min))
            own.wait()


def ternary_ffn(k, w1q, w2q, winv, b1, b2):
    nc = k.nc
    k.next_block()
    loaded, biased = k.sem("loaded"), k.sem("biased")
    own_sem, act_own = k.sem("own"), k.sem("act_own")
    var_ready, std_ready = k.sem("var_ready"), k.sem("std_ready")
    squared, rms_ready = k.sem("squared"), k.sem("rms_ready")
    xq_ready, x_turned, xqt_done, up_ready, pre_ready, gelu_done = (
        k.sem("xq_ready"), k.sem("x_turned"), k.sem("xqt_done"), k.sem("up_ready"), k.sem("pre_ready"), k.sem("gelu_done"))
    h_squared, h_rms = k.sem("h_squared"), k.sem("h_rms")
    hq_ready, h_turned, hqt_done, down_ready, added = (
        k.sem("hq_ready"), k.sem("h_turned"), k.sem("hqt_done"), k.sem("down_ready"), k.sem("added"))
    NF = F // 512
    with ExitStack() as c, nc.Block() as block:
        st = k.sb(c, "f_st", [P, NT, 6])
        mv = k.sb(c, "f_mv", [P, NT, 2])
        sm = k.sb(c, "f_small", [P, 12, NT])
        b1b = k.sb(c, "f_b1", [P, F])
        b2b = k.sb(c, "f_b2", [P, D])
        y = k.sb(c, "f_y", [P, NT, D])
        scr = k.sb(c, "f_scr", [P, 2, F])
        xr = k.sb(c, "f_xr", [P, 2, D])
        xq = k.sb(c, "f_xq", [P, 2, D], BF16)
        identb = k.sb(c, "f_identb", [P, P], BF16)
        xqt = k.sb(c, "f_xqt", [P, 2, KD, P], BF16)
        pre = k.sb(c, "f_pre", [P, 2, F])
        hh = k.sb(c, "f_h", [P, NT, F])
        hq = k.sb(c, "f_hq", [P, 2, F], BF16)
        hqt = k.sb(c, "f_hqt", [P, 2, FT, P], BF16)
        fin = k.sb(c, "f_fin", [P, 2, D])
        var, std, rstd, t1, ss, rms, peak, scl, comb, xinv = (sm[:, i, :] for i in range(10))
        ss2, peak2 = sm[:, 10, :], sm[:, 11, :]
        psb = k.ps[:, :, :].rearrange("p a n -> p (a n)").bitcast(BF16).rearrange("p (a n) -> p a n", a=8)

        @block.sync
        def _(sp):
            sp.dma_start(b1b[:, :], b1.partition_broadcast(P)).then_inc(loaded, 16)
            sp.dma_start(b2b[:, :], b2.partition_broadcast(P)).then_inc(loaded, 16)

        def root(own, out, s, v, r, tmp, raw):
            own.did(own.eng.reciprocal(r, raw))
            own.wait()
            own.did(own.eng.tensor_tensor(tmp, v, r, ALU.mult))
            own.wait()
            own.did(own.eng.tensor_tensor(s, tmp, raw, ALU.add))
            own.wait()
            own.did(own.eng.tensor_scalar(tmp, s, 0.5, None, ALU.mult))
            own.wait()
            own.did(own.eng.reciprocal(out, tmp))
            own.wait()

        def quant_scales(own, peak_, rms_, winv_):
            dve = own.eng
            own.did(dve.tensor_tensor(t1, peak_, rms_, ALU.mult))
            own.wait()
            own.did(dve.tensor_scalar(t1, t1, 1e-5, None, ALU.max))
            own.wait()
            own.did(dve.reciprocal(scl, t1))
            own.wait()
            own.did(dve.tensor_scalar(scl, scl, 127.0, None, ALU.mult))
            own.wait()
            own.did(dve.reciprocal(xinv, scl))
            own.wait()
            own.did(dve.tensor_scalar(xinv, xinv, winv_, None, ALU.mult))
            own.wait()

        @block.vector
        def _(dve):
            own = Steps(dve, own_sem)
            for t in range(NT):
                own.did(dve.bn_stats(st[:, t, :], k.x[:, t, :]))
            own.did(dve.tensor_copy(identb[:, :], k.ident[:, :]))
            own.wait()
            for t in range(NT):
                own.did(dve.bn_aggr(mv[:, t, :], st[:, t, :]))
            own.wait()
            dve.tensor_scalar(var, mv[:, :, 1], LN_EPS, None, ALU.add).then_inc(var_ready, 1)
            dve.wait_ge(std_ready, 1)
            root(own, rstd, ss, var, scl, t1, std)
            for t in range(NT):
                own.did(dve.tensor_scalar(y[:, t, :], k.x[:, t, :], mv[:, t, 0:1], rstd[:, t:t + 1],
                                          ALU.subtract, ALU.mult))
            own.wait()
            for t in range(NT):
                own.did(dve.tensor_tensor_reduce(out=scr[:, t % 2, 0:D], in0=y[:, t, :], in1=y[:, t, :], scale=1.0,
                                                 scalar=0.0, op0=ALU.mult, op1=ALU.add, accum_out=ss[:, t:t + 1]))
                own.did(dve.tensor_reduce(peak[:, t:t + 1], y[:, t, :], AX, ALU.max, apply_absolute_value=True))
                own.wait()
            dve.tensor_scalar(var, ss, 1.0 / D, LN_EPS, ALU.mult, ALU.add).then_inc(squared, 1)
            dve.wait_ge(rms_ready, 1)
            root(own, rms, ss, var, scl, t1, std)
            quant_scales(own, peak, rms, winv[:, 0:1])

            def quantise_x(t):
                wait(dve, x_turned, t - 1)
                own.did(dve.tensor_scalar(xr[:, t % 2, :], y[:, t, :], rms[:, t:t + 1], scl[:, t:t + 1],
                                          ALU.mult, ALU.mult))
                own.wait()
                dve.tensor_scalar(xq[:, t % 2, :], xr[:, t % 2, :], ROUND, -ROUND, ALU.add, ALU.add).then_inc(xq_ready, 1)

            quantise_x(0)
            for t in range(NT):
                if t + 1 < NT:
                    quantise_x(t + 1)
                if t == 0:
                    dve.wait_ge(loaded, 32)
                dve.wait_ge(up_ready, t + 1)
                wait(dve, gelu_done, t - 1)
                dve.scalar_tensor_tensor(out=pre[:, t % 2, :], in0=k.ps[:, 2 + 2 * (t % 2):4 + 2 * (t % 2), :].rearrange("p a n -> p (a n)"),
                                         scalar=xinv[:, t:t + 1], in1=b1b[:, :], op0=ALU.mult, op1=ALU.add).then_inc(pre_ready, 1)
                if t > 0:
                    dve.wait_ge(gelu_done, t)
                    own.did(dve.tensor_reduce(peak2[:, t - 1:t], hh[:, t - 1, :], AX, ALU.max, apply_absolute_value=True))
            dve.wait_ge(gelu_done, NT)
            own.did(dve.tensor_reduce(peak2[:, NT - 1:NT], hh[:, NT - 1, :], AX, ALU.max, apply_absolute_value=True))
            own.wait()
            dve.wait_ge(h_squared, NT)
            dve.tensor_scalar(var, ss2, 1.0 / F, LN_EPS, ALU.mult, ALU.add).then_inc(squared, 1)
            dve.wait_ge(rms_ready, 2)
            root(own, rms, ss, var, scl, t1, std)
            quant_scales(own, peak2, rms, winv[:, 1:2])

            def quantise_h(t):
                wait(dve, h_turned, 1 * (t - 1))
                own.did(dve.tensor_scalar(pre[:, t % 2, :], hh[:, t, :], rms[:, t:t + 1], scl[:, t:t + 1],
                                          ALU.mult, ALU.mult))
                own.wait()
                dve.tensor_scalar(hq[:, t % 2, :], pre[:, t % 2, :], ROUND, -ROUND, ALU.add, ALU.add).then_inc(hq_ready, 1)

            for t in range(NT):
                own.did(dve.tensor_tensor(k.x[:, t, :], k.x[:, t, :], b2b[:, :], ALU.add))
            own.wait()
            quantise_h(0)
            for t in range(NT):
                if t + 1 < NT:
                    quantise_h(t + 1)
                dve.wait_ge(down_ready, t + 1)
                dve.scalar_tensor_tensor(out=k.x[:, t, :], in0=k.ps[:, 6 + t % 2, 0:D], scalar=xinv[:, t:t + 1],
                                         in1=k.x[:, t, :], op0=ALU.mult, op1=ALU.add).then_inc(added, 1)

        @block.scalar
        def _(act):
            act.wait_ge(var_ready, 1)
            act.activation(std, var, ACT.Sqrt).then_inc(std_ready, 1)
            act.wait_ge(squared, 1)
            act.activation(std, var, ACT.Sqrt).then_inc(rms_ready, 1)

            def copy_x(t):
                act.wait_ge(x_turned, t + 1)
                wait(act, up_ready, t - 1)
                act.activation(xqt[:, t % 2, :, :].rearrange("p k n -> p (k n)"), psb[:, t % 2, 0:KD * P],
                               ACT.Copy).then_inc(xqt_done, 1)
            copy_x(0)
            for t in range(NT):
                if t + 1 < NT:
                    copy_x(t + 1)
                act.wait_ge(pre_ready, t + 1)
                act.activation(hh[:, t, :], pre[:, t % 2, :], ACT.Gelu).then_inc(gelu_done, 1)
                act.wait_ge(gelu_done, t + 1)
                wait(act, h_squared, t - 1)
                act.activation(scr[:, t % 2, :], hh[:, t, :], ACT.Square, accum_out=ss2[:, t:t + 1]).then_inc(h_squared, 1)
            act.wait_ge(squared, 2)
            act.activation(std, var, ACT.Sqrt).then_inc(rms_ready, 1)
            for t in range(NT):
                act.wait_ge(h_turned, t + 1)
                wait(act, down_ready, t - 1)
                act.activation(hqt[:, t % 2, :, :].rearrange("p k n -> p (k n)"),
                               psb[:, 2 + t % 2, :], ACT.Copy).then_inc(hqt_done, 1)

        @block.tensor
        def _(pe):
            def turn_x(t):
                pe.wait_ge(xq_ready, t + 1)
                wait(pe, xqt_done, t - 1)
                for kd in range(KD):
                    last = pe.transpose(psb[:, t % 2, kd * P:(kd + 1) * P], xq[:, t % 2, kd * P:(kd + 1) * P], identb[:, :])
                last.then_inc(x_turned, 1)

            turn_x(0)
            for t in range(NT):
                if t + 1 < NT:
                    turn_x(t + 1)
                pe.wait_ge(xqt_done, t + 1)
                wait(pe, pre_ready, t - 1)
                for n in range(NF):
                    for kd in range(KD):
                        last = pe.matmul(k.ps[:, 2 + 2 * (t % 2) + n, :], xqt[:, t % 2, kd, :],
                                         w1q[:, kd, n * 512:(n + 1) * 512], start=kd == 0, stop=kd == KD - 1)
                last.then_inc(up_ready, 1)
            pe.wait_ge(pre_ready, NT)

            def turn_h(t):
                pe.wait_ge(hq_ready, t + 1)
                wait(pe, hqt_done, t - 1)
                for f in range(FT):
                    last = pe.transpose(psb[:, 2 + t % 2, f * P:(f + 1) * P], hq[:, t % 2, f * P:(f + 1) * P], identb[:, :])
                last.then_inc(h_turned, 1)

            turn_h(0)
            for t in range(NT):
                if t + 1 < NT:
                    turn_h(t + 1)
                pe.wait_ge(hqt_done, t + 1)
                wait(pe, added, t - 1)
                for f in range(FT):
                    last = pe.matmul(k.ps[:, 6 + t % 2, 0:D], hqt[:, t % 2, f, :], w2q[:, f, :],
                                     start=f == 0, stop=f == FT - 1)
                last.then_inc(down_ready, 1)


def feature_attention(k, attn, wq, wk, wv, bq, bk, bv, random_matrix):
    nc = k.nc
    k.next_block()
    loaded, own_sem, operands_done = k.sem("loaded"), k.sem("own"), k.sem("operands_done")
    proj_ready, proj_done = k.sem("proj_ready"), k.sem("proj_done")
    v_ready, v_done = k.sem("v_ready"), k.sem("v_done")
    x_ready, low_ready, exp_done, feat_done = k.sem("x_ready"), k.sem("low_ready"), k.sem("exp_done"), k.sem("feat_done")
    kv_used, kv_ready, kv_done = k.sem("kv_used"), k.sem("kv_ready"), k.sem("kv_done")
    mixed, floored, inverted, weighted = k.sem("mixed"), k.sem("floored"), k.sem("inverted"), k.sem("weighted")
    V1 = HD + 1
    PAIRS = H // 2
    PW = 2 * V1
    FLOOR = 1e-6 * 256.0
    KP = NT * KD
    QP = NG * PAIRS
    with ExitStack() as c, nc.Block() as block:
        bq_sb = k.sb(c, "l_bq", [P, KD])
        bk_sb = k.sb(c, "l_bk", [P, KD])
        bv_sb = k.sb(c, "l_bv", [P, D])
        r8 = k.sb(c, "l_r8", [P, M])
        rbd = k.sb(c, "l_rbd", [P, HP, M])
        pj = k.sb(c, "l_pj", [P, 2, KD, G])
        va = k.sb(c, "l_va", [P, NT, H, V1])
        low = k.sb(c, "l_low", [P, 4, 512])
        kp = k.sb(c, "l_kp", [P, 2, KD, 512])
        qp = k.sb(c, "l_qp", [P, 2, PAIRS, G])
        kv = k.sb(c, "l_kv", [P, B, PAIRS, PW])
        den = k.sb(c, "l_den", [P, 2, H])
        inv = k.sb(c, "l_inv", [P, 2, H])

        @block.sync
        def _(sp):
            sp.dma_start(bq_sb[:, :], bq).then_inc(loaded, 16)
            sp.dma_start(bk_sb[:, :], bk).then_inc(loaded, 16)
            sp.dma_start(bv_sb[:, :], bv.partition_broadcast(P)).then_inc(loaded, 16)
            for h in range(HP):
                sp.dma_start(r8[h * HD:(h + 1) * HD, :], random_matrix).then_inc(loaded, 16)

        @block.tensor
        def _(pe):
            def project(n, w):
                g, m = divmod(n % (KD * NG), KD)
                wait(pe, proj_done, n - 1)
                for kd in range(KD):
                    last = pe.matmul(k.ps[:, 4 + m, :], w[:, kd, m * P:(m + 1) * P],
                                     k.xt[:, kd, g * G:(g + 1) * G], start=kd == 0, stop=kd == KD - 1)
                last.then_inc(proj_ready, 1)

            def key_value(t):
                b, q = divmod(t, QT)
                pe.wait_ge(feat_done, KD * (t + 1))
                if q == 0:
                    wait(pe, kv_done, b)
                for p in range(PAIRS):
                    kd, r = divmod(p, PAIRS // KD)
                    last = pe.matmul(k.ps[:, 7, p * PW:(p + 1) * PW], kp[:, t % 2, kd, r * P:(r + 1) * P],
                                     va[:, t, 2 * p:2 * p + 2, :].rearrange("p h d -> p (h d)"),
                                     start=q == 0 and p == 0, stop=q == QT - 1, skip_group_check=True)
                last.then_inc(kv_used, 1)

            pe.wait_ge(loaded, 16 * (3 + HP))
            for m in range(KD):
                project(m, wk)
            pe.wait_ge(operands_done, 1)
            for g in range(NG):
                for j in range(TPG):
                    t = g * TPG + j
                    wait(pe, v_done, t)
                    for kd in range(KD):
                        last = pe.matmul(k.ps[:, 6, 0:D], k.xt[:, kd, t * P:(t + 1) * P], wv[:, kd, :],
                                         start=kd == 0, stop=kd == KD - 1)
                    last.then_inc(v_ready, 1)
                    if j == 0:
                        pe.wait_ge(proj_done, KD * (g + 1))
                    for kd in range(KD):
                        n = KD * t + kd
                        wait(pe, feat_done, n - 3)
                        pe.matmul(k.ps[:, n % 4, :], pj[:, g % 2, kd, j * P:(j + 1) * P],
                                  rbd[:, :, :].rearrange("p h m -> p (h m)"), start=True, stop=True).then_inc(x_ready, 1)
                    if t > 0:
                        wait(pe, v_done, t)
                        key_value(t - 1)
                if g + 1 < NG:
                    for m in range(KD):
                        project(KD * (g + 1) + m, wk)
                else:
                    for m in range(KD):
                        project(KD * NG + m, wq)
            def mix(t):
                b = t // QT
                wait(pe, weighted, t)
                if t == 0:
                    pe.wait_ge(kv_done, B)
                g, j = divmod(t, TPG)
                pe.wait_ge(feat_done, KP + PAIRS * (g + 1))
                for p in range(PAIRS):
                    last = pe.matmul(k.ps[:, 7, p * PW:(p + 1) * PW], qp[:, g % 2, p, j * P:(j + 1) * P],
                                     kv[:, b, p, :], start=True, stop=True)
                last.then_inc(mixed, 1)

            for g in range(NG):
                pe.wait_ge(proj_done, KD * (NG + g + 1))
                for p in range(PAIRS):
                    kd, r = divmod(p, PAIRS // KD)
                    n = KP + PAIRS * g + p
                    wait(pe, feat_done, n - 3)
                    pe.matmul(k.ps[:, n % 4, :], rbd[:, 2 * r:2 * r + 2, :].rearrange("p h m -> p (h m)"),
                              pj[:, g % 2, kd, :], start=True, stop=True).then_inc(x_ready, 1)
                    if g == 0 and p == 0:
                        pe.wait_ge(v_done, NT)
                        key_value(NT - 1)
                    if g > 0 and p % 2 == 1:
                        mix((g - 1) * TPG + p // 2)
                if g + 1 < NG:
                    for m in range(KD):
                        project(KD * (NG + g + 1) + m, wq)
            for j in range(TPG):
                mix((NG - 1) * TPG + j)

        @block.scalar
        def _(act):
            def copy_proj(n):
                g, m = divmod(n, KD)
                act.wait_ge(proj_ready, n + 1)
                if 2 <= g < NG:
                    act.wait_ge(x_ready, KD * TPG * (g - 1))
                elif g >= NG:
                    act.wait_ge(x_ready, KP - KD * TPG if g == NG else (KP if g == NG + 1 else KP + PAIRS * (g - NG - 1)))
                bias = bk_sb if g < NG else bq_sb
                act.activation(pj[:, g % 2, m, :], k.ps[:, 4 + m, :], ACT.Identity, bias=bias[:, m:m + 1]).then_inc(proj_done, 1)

            act.wait_ge(loaded, 16 * (3 + HP))
            for m in range(KD):
                copy_proj(m)
            for n in range(KP + QP):
                act.wait_ge(low_ready, n + 1)
                act.activation(low[:, n % 4, :], low[:, n % 4, :], ACT.Exp).then_inc(exp_done, 1)
                if n % (KD * TPG) == KD * TPG - 1 and (n + 1) // (KD * TPG) < 2 * NG:
                    for m in range(KD):
                        copy_proj(KD * ((n + 1) // (KD * TPG)) + m)

        @block.vector
        def _(dve):
            own = Steps(dve, own_sem)
            own.did(dve.memset(va[:, :, :, :], 1.0))
            own.did(dve.memset(kv[:, :, :, :], 0.0))
            dve.wait_ge(loaded, 16 * (3 + HP))
            for h in range(HP):
                last = dve.tensor_scalar(rbd[:, h, :], r8[:, :], k.hmask[:, h:h + 1], None, ALU.mult)
                if h < HP - 1:
                    own.did(last)
            own.wait()
            last.then_inc(operands_done, 1)

            def lower(n):
                dve.wait_ge(x_ready, n + 1)
                wait(dve, feat_done, n - 3)
                dve.tensor_scalar(low[:, n % 4, :], k.ps[:, n % 4, :], 0.0, None, ALU.min).then_inc(low_ready, 1)

            def feature(n):
                dve.wait_ge(exp_done, n + 1)
                if n < KP:
                    t, kd = divmod(n, KD)
                    wait(dve, kv_used, t - 1)
                    dst = kp[:, t % 2, kd, :]
                else:
                    g, p = divmod(n - KP, PAIRS)
                    wait(dve, mixed, TPG * (g - 1))
                    dst = qp[:, g % 2, p, :]
                dve.scalar_tensor_tensor(out=dst, in0=k.ps[:, n % 4, :], scalar=0.0, in1=low[:, n % 4, :],
                                         op0=ALU.max, op1=ALU.add).then_inc(feat_done, 1)

            def copy_v(t):
                dve.wait_ge(v_ready, t + 1)
                dve.tensor_tensor(va[:, t, :, 0:HD], k.ps[:, 6, 0:D].rearrange("p (h d) -> p h d", d=HD),
                                  bv_sb[:, :].rearrange("p (h d) -> p h d", d=HD), ALU.add).then_inc(v_done, 1)

            def copy_kv(b):
                dve.wait_ge(kv_used, QT * (b + 1))
                src = k.ps[:, 7, 0:PAIRS * PW].rearrange("p (a n) -> p a n", n=PW)
                own.did(dve.tensor_copy(kv[0:64, b, :, 0:V1], src[0:64, :, 0:V1]))
                dve.tensor_copy(kv[64:P, b, :, V1:PW], src[64:P, :, V1:PW]).then_inc(kv_done, 1)
                own.wait()

            def weight(t):
                dve.wait_ge(mixed, t + 1)
                o = k.ps[:, 7, 0:H * V1].rearrange("p (h d) -> p h d", d=V1)
                dve.tensor_scalar(den[:, t % 2, :], o[:, :, HD], FLOOR, None, ALU.max).then_inc(floored, 1)
                dve.wait_ge(floored, t + 1)
                dve.reciprocal(inv[:, t % 2, :], den[:, t % 2, :]).then_inc(inverted, 1)
                dve.wait_ge(inverted, t + 1)
                dve.tensor_tensor(attn[:, t, :].rearrange("p (h d) -> p h d", d=HD), o[:, :, 0:HD],
                                  inv[:, t % 2, :].unsqueeze(2).to_broadcast([P, H, HD]), ALU.mult).then_inc(weighted, 1)

            copy_v(0)
            lower(0)
            for n in range(1, KP + QP + 1):
                if n < KP + QP:
                    if n < KP and n % KD == 0:
                        copy_v(n // KD)
                    lower(n)
                feature(n - 1)
                done = n
                if done == KD * QT + 2:
                    copy_kv(0)
                if done == KP + 1:
                    copy_kv(1)
                g, p = divmod(done - KP - 1, PAIRS)
                if done - KP - 1 >= PAIRS and p % 2 == 1 and p // 2 < TPG and g <= NG - 1:
                    weight((g - 1) * TPG + p // 2)
            for j in range(TPG):
                weight((NG - 1) * TPG + j)


def route(k, r, xn, scratch, wg, bg, b1, w1, w2, b2):
    nc = k.nc
    k.next_block()
    loaded, weights_in, own_sem, gated, cw_done = (
        k.sem("loaded"), k.sem("weights_in"), k.sem("own"), k.sem("gated"), k.sem("cw_done"))
    exp_ready, exp_done, turned, turned_done = k.sem("exp_ready"), k.sem("exp_done"), k.sem("turned"), k.sem("turned_done")
    b2_ready, b2_added = k.sem("b2_ready"), k.sem("b2_added")
    hot_done, ones_set, counted, placed, scattered = (
        k.sem("hot_done"), k.sem("ones_set"), k.sem("counted"), k.sem("placed"), k.sem("scattered"))
    b1_in, b1_split, b1_out = k.sem("b1_in"), k.sem("b1_split"), k.sem("b1_out")
    with ExitStack() as c, nc.Block() as block:
        wg_sb = k.sb(c, "wg", [P, KD, E])
        bg_sb = k.sb(c, "bg", [P, E])
        b2_sb = k.sb(c, "b2", [E, D])
        iota = k.sb(c, "iota", [P, IOTA])
        before = k.sb(c, "before", [P, P])
        ones = k.sb(c, "ones", [P, P])
        logit = k.sb(c, "logit", [P, NT, E])
        prob = k.sb(c, "prob", [P, NT, E])
        m1 = k.sb(c, "gate_max", [P, NT])
        ssum = k.sb(c, "gate_sum", [P, NT])
        inv = k.sb(c, "gate_inv", [P, NT])
        best = k.sb(c, "best", [P, NT, 8])
        best_at = k.sb(c, "best_at", [P, NT, 8], U32)
        at = k.sb(c, "at_f", [P, NT, 8])
        hot = k.sb(c, "hot", [P, 2, NT, E])
        both = k.sb(c, "both", [P, NT, E])
        cw = k.sb(c, "cw", [P, NT, E])
        weighed = k.sb(c, "weighed", [P, NT, E])
        upto = k.sb(c, "tokens_before", [P, NT + 1, E])
        total = k.sb(c, "tile_total", [P, NT, E])
        over = k.sb(c, "over", [P, E, NT])
        tiles = k.sb(c, "expert_tiles", [P, E])
        first = k.sb(c, "first_tile", [P, E])
        place = k.sb(c, "place", [P, NT, E])
        place_r = k.sb(c, "place_r", [P, 2, NT])
        owned = k.sb(c, "owned", [1, SLOT_TILES, E])
        owner = k.sb(c, "owner", [1, SLOT_TILES])
        cwt = k.sb(c, "cwt", [E, NT, P])
        b1_rows = k.sb(c, "b1_rows", [E, F])
        b1_pieces = k.sb(c, "b1_pieces", [E, 3, F], BF16)

        def wide(a):
            return a.unsqueeze(2).to_broadcast([P, NT, E])

        @block.sync
        def _(sp):
            sp.dma_start(wg_sb[:, :, :], wg.rearrange("(k p) n -> p k n", p=P)).then_inc(loaded, 16)
            sp.dma_start(bg_sb[:, :], bg.partition_broadcast(P)).then_inc(loaded, 16)
            sp.dma_start(b2_sb[:, :], b2).then_inc(loaded, 16)
            sp.dma_start(iota[:, :], k.iota_in).then_inc(loaded, 16)
            sp.dma_start(before[:, :], k.before_in).then_inc(loaded, 16)
            for e in range(E):
                sp.dma_start(r.w1[:, e, :, :], w1[e].rearrange("(k p) n -> p k n", p=P)).then_inc(weights_in, 16)
                sp.dma_start(r.w2[:, e, :, :], w2[e].rearrange("(k p) n -> p k n", p=P)).then_inc(weights_in, 16)
            sp.wait_ge(b1_split, 1)
            sp.dma_start(scratch.b1.rearrange("c e n -> e c n"), b1_pieces[:, :, :]).then_inc(b1_out, 16)
            sp.wait_ge(b1_out, 16)
            sp.wait_ge(weights_in, 2 * E * 16)

        @block.gpsimd
        def _(pool):
            pool.memset(ones[:, :], 1.0).then_inc(ones_set, 1)
            pool.wait_ge(k.slots_zeroed, 16)
            pool.wait_ge(placed, 1)
            for n in range(2 * NT):
                choice, t = divmod(n, NT)
                pool.indirect_dma_start(out=scratch.x[:, :], out_offset=bass.IndirectOffsetOnAxis(ap=r.slot[:, choice, t:t + 1], axis=0),
                                        in_=xn[:, t, :], in_offset=None).then_inc(scattered, 16)
            pool.wait_ge(scattered, 2 * NT * 16)

        @block.tensor
        def _(pe):
            pe.wait_ge(loaded, 80)
            for t in range(NT):
                for kd in range(KD):
                    last = pe.matmul(k.ps[:, 0, t * E:(t + 1) * E], k.xt[:, kd, t * P:(t + 1) * P], wg_sb[:, kd, :],
                                     start=kd == 0, stop=kd == KD - 1)
            last.then_inc(gated, 1)
            pe.wait_ge(hot_done, 1)
            pe.wait_ge(ones_set, 1)
            hs = both[:, :, :].rearrange("p t e -> p (t e)")
            pe.matmul(k.ps[:, 7, 0:NT * E], before[:, :], hs, start=True, stop=True)
            pe.matmul(k.ps[:, 7, NT * E:2 * NT * E], ones[:, :], hs, start=True, stop=True).then_inc(counted, 1)
            pe.wait_ge(cw_done, 1)
            for g in range(NG):
                for j in range(TPG):
                    last = pe.transpose(k.ps[0:E, 1 + g, j * P:(j + 1) * P], cw[:, g * TPG + j, :], k.ident[:, :])
                last.then_inc(turned, 1)
            for t in range(NT):
                pe.wait_ge(turned_done, t // TPG + 1)
                wait(pe, b2_added, t - 1)
                pe.matmul(k.ps[:, 5 + t % 2, 0:D], cwt[:, t, :], b2_sb[:, :], start=True, stop=True).then_inc(b2_ready, 1)

        @block.scalar
        def _(act):
            act.dma_start(b1_rows[:, :], b1).then_inc(b1_in, 16)
            act.wait_ge(exp_ready, 1)
            act.activation(prob[:, :, :].rearrange("p t e -> p (t e)"), logit[:, :, :].rearrange("p t e -> p (t e)"),
                           ACT.Exp).then_inc(exp_done, 1)
            for g in range(NG):
                act.wait_ge(turned, g + 1)
                act.activation(cwt[:, g * TPG:(g + 1) * TPG, :].rearrange("p t n -> p (t n)"), k.ps[0:E, 1 + g, :],
                               ACT.Copy).then_inc(turned_done, 1)

        @block.vector
        def _(dve):
            own = Steps(dve, own_sem)

            def step(ins):
                own.did(ins)
                own.wait()

            dve.wait_ge(b1_in, 16)
            for n in range(3):
                ins = dve.tensor_copy(b1_pieces[:, n, :], b1_rows[:, :])
                if n == 2:
                    ins.then_inc(b1_split, 1)
                else:
                    step(ins)
                    step(dve.tensor_tensor(b1_rows[:, :], b1_rows[:, :], b1_pieces[:, n, :], ALU.subtract))

            dve.wait_ge(loaded, 80)
            dve.wait_ge(gated, 1)
            step(dve.tensor_tensor(logit[:, :, :], k.ps[:, 0, 0:NT * E].rearrange("p (t e) -> p t e", e=E),
                                   bg_sb[:, :].unsqueeze(1).to_broadcast([P, NT, E]), ALU.add))
            step(dve.tensor_reduce(m1[:, :], logit[:, :, :], AX, ALU.max))
            dve.tensor_tensor(logit[:, :, :], logit[:, :, :], wide(m1[:, :]), ALU.subtract).then_inc(exp_ready, 1)
            dve.wait_ge(exp_done, 1)
            step(dve.tensor_reduce(ssum[:, :], prob[:, :, :], AX, ALU.add))
            step(dve.reciprocal(inv[:, :], ssum[:, :]))
            step(dve.tensor_tensor(prob[:, :, :], prob[:, :, :], wide(inv[:, :]), ALU.mult))
            for t in range(NT):
                own.did(dve.max(best[:, t, :], prob[:, t, :]))
            own.wait()
            for t in range(NT):
                own.did(dve.max_index(best_at[:, t, :], best[:, t, :], prob[:, t, :]))
            own.wait()
            step(dve.tensor_copy(at[:, :, :], best_at[:, :, :]))
            for n in range(2):
                own.did(dve.tensor_tensor(hot[:, n, :, :], iota[:, 0:E].unsqueeze(1).to_broadcast([P, NT, E]),
                                          wide(at[:, :, n]), ALU.is_equal))
            own.wait()
            dve.tensor_tensor(both[:, :, :], hot[:, 0, :, :], hot[:, 1, :, :], ALU.add).then_inc(hot_done, 1)
            own.did(dve.memset(upto[:, 0, :], 0.0))
            dve.wait_ge(counted, 1)
            step(dve.tensor_copy(total[:, :, :], k.ps[:, 7, NT * E:2 * NT * E].rearrange("p (t e) -> p t e", e=E)))
            for t in range(NT):
                step(dve.tensor_tensor(upto[:, t + 1, :], upto[:, t, :], total[:, t, :], ALU.add))
            step(dve.tensor_scalar(tiles[:, :], upto[:, NT, :], 1.0 / P, None, ALU.mult))
            step(dve.tensor_tensor(over[:, :, :], tiles[:, :].unsqueeze(2).to_broadcast([P, E, NT]),
                                   iota[:, 0:NT].unsqueeze(1).to_broadcast([P, E, NT]), ALU.is_gt))
            own.did(dve.memset(first[:, 0:1], 0.0))
            step(dve.tensor_reduce(tiles[:, :], over[:, :, :], AX, ALU.add))
            for e in range(1, E):
                step(dve.tensor_tensor(first[:, e:e + 1], first[:, e - 1:e], tiles[:, e - 1:e], ALU.add))
            step(dve.tensor_tensor(place[:, :, :], upto[:, 0:NT, :],
                                   k.ps[:, 7, 0:NT * E].rearrange("p (t e) -> p t e", e=E), ALU.add))
            step(dve.tensor_scalar(tiles[:, :], first[:, :], float(P), None, ALU.mult))
            step(dve.tensor_tensor(place[:, :, :], place[:, :, :], tiles[:, :].unsqueeze(1).to_broadcast([P, NT, E]), ALU.add))
            for n in range(2):
                step(dve.tensor_tensor(weighed[:, :, :], hot[:, n, :, :], place[:, :, :], ALU.mult))
                step(dve.tensor_reduce(place_r[:, n, :], weighed[:, :, :], AX, ALU.add))
            dve.tensor_copy(r.slot[:, :, :], place_r[:, :, :]).then_inc(placed, 1)
            step(dve.tensor_tensor(owned[:, :, :], iota[0:1, 0:SLOT_TILES].unsqueeze(2).to_broadcast([1, SLOT_TILES, E]),
                                   first[0:1, :].unsqueeze(1).to_broadcast([1, SLOT_TILES, E]), ALU.is_ge))
            step(dve.tensor_reduce(owner[:, :], owned[:, :, :], AX, ALU.add))
            step(dve.tensor_scalar(owner[:, :], owner[:, :], -1.0, None, ALU.add))
            own.did(dve.tensor_copy(r.owner[:, :], owner[:, :]))
            step(dve.tensor_tensor(ssum[:, :], best[:, :, 0], best[:, :, 1], ALU.add))
            step(dve.tensor_scalar(ssum[:, :], ssum[:, :], 1e-8, None, ALU.add))
            step(dve.reciprocal(inv[:, :], ssum[:, :]))
            for n in range(2):
                step(dve.tensor_tensor(r.weight[:, n, :], best[:, :, n], inv[:, :], ALU.mult))
                step(dve.tensor_tensor(hot[:, n, :, :], hot[:, n, :, :], wide(r.weight[:, n, :]), ALU.mult))
            dve.tensor_tensor(cw[:, :, :], hot[:, 0, :, :], hot[:, 1, :, :], ALU.add).then_inc(cw_done, 1)
            for t in range(NT):
                dve.wait_ge(b2_ready, t + 1)
                dve.tensor_tensor(k.x[:, t, :], k.x[:, t, :], k.ps[:, 5 + t % 2, 0:D], ALU.add).then_inc(b2_added, 1)


def experts(k, r, scratch):
    nc = k.nc
    k.next_block()
    x_in = [k.sem(f"x_in{u}") for u in range(2)]
    y_out = [k.sem(f"y_out{u}") for u in range(2)]
    ones_set, x_turned, x_copied = k.sem("ones_set"), k.sem("x_turned"), k.sem("x_copied")
    pre_ready, h_done, h_turned, ht_done = k.sem("pre_ready"), k.sem("h_done"), k.sem("h_turned"), k.sem("ht_done")
    y_ready, y_copied = k.sem("y_ready"), k.sem("y_copied")
    BODY = 2
    NB = (SLOT_TILES - 1) // BODY
    HALF = F // 2
    b1_in = k.sem("b1_in")
    with ExitStack() as c, nc.Block() as block:
        b1 = k.sb(c, "hidden_bias", [3, E * F], BF16)
        xs = k.sb(c, "slots_x", [P, 2, D])
        xst = k.sb(c, "slots_xt", [P, 2, KD, P])
        ys = k.sb(c, "slots_y", [P, 2, D])
        ones = k.sb(c, "one_rows", [3, P], BF16)
        h = k.xt[:, 0, :].rearrange("p (u n) -> p u n", u=2)
        ht = k.xt[:, 1, :].rearrange("p (u f n) -> p u f n", u=2, f=FT)

        def bodies(eng, step):
            for s in range(BODY):
                step(0, s)
            with eng.Fori(1, NB - 1) as i:
                for s in range(BODY):
                    step(i, s)
            for s in range(BODY):
                step(NB - 1, s)
            step(NB, 0)

        def exists(i, s):
            return not isinstance(i, int) or i * BODY + s < SLOT_TILES

        @block.sync
        def _(sp):
            def step(i, s):
                n = i * BODY + s
                wait(sp, x_turned, n - 1)
                sp.dma_start(xs[:, s, :], scratch.x[bass.ds(n * P, P), :]).then_inc(x_in[s], 16)
            sp.dma_start(b1[:, :], scratch.b1.rearrange("c e n -> c (e n)")).then_inc(b1_in, 16)
            bodies(sp, step)

        @block.tensor
        def _(pe):
            def turn_x(i, s):
                n = i * BODY + s
                u = s % 2
                pe.wait_ge(x_in[u], (i + s // BODY + 1) * 16)
                wait(pe, x_copied, n)
                for kd in range(KD):
                    last = pe.transpose(k.ps[:, 7, (u * KD + kd) * P:(u * KD + kd + 1) * P],
                                        xs[:, u, kd * P:(kd + 1) * P], k.ident[:, :])
                last.then_inc(x_turned, 1)

            def up(i, s, half):
                n = i * BODY + s
                u = s % 2
                if half == 0:
                    pe.wait_ge(x_copied, n + 1)
                    wait(pe, h_done, n - 1)
                    pe.nop(nofuse=True)
                e = pe.value_load(r.owner[0:1, bass.ds(n, 1)], min_val=0, max_val=E - 1)
                bank = k.ps[:, 2 * u + half, :]
                for kd in range(KD):
                    pe.matmul(bank, xst[:, u, kd, :],
                              r.w1[:, bass.ds(e, 1), kd, half * HALF:(half + 1) * HALF].rearrange("p a n -> p (a n)"),
                              start=kd == 0, stop=False)
                last = pe.matmul(bank, ones[:, :], b1[:, bass.ds(e * F + half * HALF, HALF)], start=False, stop=True)
                if half == 1:
                    last.then_inc(pre_ready, 1)

            def turn_h(i, s):
                n = i * BODY + s
                pe.wait_ge(h_done, n + 1)
                wait(pe, ht_done, n)
                for f in range(FT):
                    last = pe.transpose(k.ps[:, 4 + f // 4, (f % 4) * P:(f % 4 + 1) * P],
                                        h[:, s, f * P:(f + 1) * P], k.ident[:, :])
                last.then_inc(h_turned, 1)

            def down(i, s):
                n = i * BODY + s
                pe.wait_ge(ht_done, n + 1)
                wait(pe, y_copied, n)
                pe.nop(nofuse=True)
                e = pe.value_load(r.owner[0:1, bass.ds(n, 1)], min_val=0, max_val=E - 1)
                for f in range(FT):
                    last = pe.matmul(k.ps[:, 6, s * D:(s + 1) * D], ht[:, s, f, :],
                                     r.w2[:, bass.ds(e, 1), f, :].rearrange("p a n -> p (a n)"), start=f == 0, stop=f == FT - 1)
                last.then_inc(y_ready, 1)

            def step(i, s):
                if exists(i, s + 1):
                    up(i, s + 1, 0)
                turn_h(i, s)
                if exists(i, s + 1):
                    up(i, s + 1, 1)
                if exists(i, s + 2):
                    turn_x(i, s + 2)
                down(i, s)

            pe.wait_ge(ones_set, 1)
            pe.wait_ge(b1_in, 16)
            turn_x(0, 0)
            turn_x(0, 1)
            up(0, 0, 0)
            up(0, 0, 1)
            bodies(pe, step)

        @block.gpsimd
        def _(pool):
            pool.memset(ones[:, :], 1.0).then_inc(ones_set, 1)

        @block.scalar
        def _(act):
            def copy_x(i, s):
                n = i * BODY + s
                u = s % 2
                act.wait_ge(x_turned, n + 1)
                wait(act, pre_ready, n - 1)
                act.activation(xst[:, u, :, :].rearrange("p k n -> p (k n)"), k.ps[:, 7, u * D:(u + 1) * D],
                               ACT.Copy).then_inc(x_copied, 1)

            def hidden(i, s):
                n = i * BODY + s
                act.wait_ge(pre_ready, n + 1)
                wait(act, h_turned, n - 1)
                act.activation(h[:, s, :], k.ps[:, 2 * s:2 * s + 2, :].rearrange("p a n -> p (a n)"),
                               ACT.Gelu_apprx_tanh).then_inc(h_done, 1)

            def store(i, s):
                act.wait_ge(y_copied, i * BODY + s + 1)
                act.dma_start(scratch.y[bass.ds((i * BODY + s) * P, P), :], ys[:, s, :]).then_inc(y_out[s], 16)

            def step(i, s):
                hidden(i, s)
                if exists(i, s + 2):
                    copy_x(i, s + 2)
                store(i, s)

            copy_x(0, 0)
            copy_x(0, 1)
            bodies(act, step)

        @block.vector
        def _(dve):
            def step(i, s):
                n = i * BODY + s
                dve.wait_ge(h_turned, n + 1)
                wait(dve, y_ready, n - 1)
                dve.tensor_copy(ht[:, s, :, :].rearrange("p f n -> p (f n)"),
                                k.ps[:, 4:6, :].rearrange("p a n -> p (a n)")).then_inc(ht_done, 1)
                dve.wait_ge(y_ready, n + 1)
                if not (isinstance(i, int) and i == 0):
                    dve.wait_ge(y_out[s], i * 16)
                dve.tensor_copy(ys[:, s, :], k.ps[:, 6, s * D:(s + 1) * D]).then_inc(y_copied, 1)
            bodies(dve, step)
            for s in range(BODY):
                dve.wait_ge(y_out[s], (NB + (s == 0)) * 16)


def combine(k, r, scratch, out):
    nc = k.nc
    k.next_block()
    LANES = 8
    gathered = [k.sem(f"gathered{u}") for u in range(LANES)]
    added, stored = k.sem("added"), k.sem("stored")
    with ExitStack() as c, nc.Block() as block:
        rows = k.xt[:, :, :].rearrange("p k n -> p (k n)").rearrange("p (u n) -> p u n", n=D)

        @block.gpsimd
        def _(pool):
            for n in range(2 * NT):
                t, choice = divmod(n, 2)
                wait(pool, added, n - LANES + 1)
                pool.indirect_dma_start(out=rows[:, n % LANES, :], out_offset=None, in_=scratch.y[:, :],
                                        in_offset=bass.IndirectOffsetOnAxis(ap=r.slot[:, choice, t:t + 1], axis=0)
                                        ).then_inc(gathered[n % LANES], 16)

        @block.vector
        def _(dve):
            for n in range(2 * NT):
                t, choice = divmod(n, 2)
                dve.wait_ge(gathered[n % LANES], 16 * (n // LANES + 1))
                wait(dve, added, n)
                dve.scalar_tensor_tensor(out=k.x[:, t, :], in0=rows[:, n % LANES, :], scalar=r.weight[:, choice, t:t + 1],
                                         in1=k.x[:, t, :], op0=ALU.mult, op1=ALU.add).then_inc(added, 1)

        @block.sync
        def _(sp):
            for g in range(NG):
                sp.wait_ge(added, 2 * TPG * (g + 1))
                b, q = divmod(g * TPG, QT)
                sp.dma_start(out[b, q * P:(q + TPG) * P, :].rearrange("(t p) n -> p t n", p=P),
                             k.x[:, g * TPG:(g + 1) * TPG, :]).then_inc(stored, 16)
            sp.wait_ge(stored, NG * 16)


INS = ["x", "L0_attn_W_down_kv", "L0_attn_W_up_k", "L0_attn_W_up_v", "L0_attn_Wq", "L0_attn_Wo",
       "L0_xattn_bq", "L0_xattn_bk", "L0_xattn_bv", "L0_xattn_bo", "L0_ffn_b1", "L0_ffn_b2",
       "L1_attn_Wq", "L1_attn_bq", "L1_attn_Wk", "L1_attn_bk", "L1_attn_Wv", "L1_attn_bv", "L1_attn_Wo", "L1_attn_bo",
       "L1_attn_random_matrix", "L1_xattn_bq", "L1_xattn_bk", "L1_xattn_bv", "L1_xattn_bo",
       "L1_ffn_Wg", "L1_ffn_bg", "L1_ffn_W1", "L1_ffn_b1", "L1_ffn_W2", "L1_ffn_b2"]
TURNED = {"wk_t": "L0_attn_Wk", "wv_t": "L0_attn_Wv", "x0q": "L0_xattn_Wq", "x0k": "L0_xattn_Wk", "x0v": "L0_xattn_Wv",
          "x0o": "L0_xattn_Wo", "x1q": "L1_xattn_Wq", "x1k": "L1_xattn_Wk", "x1v": "L1_xattn_Wv", "x1o": "L1_xattn_Wo",
          "w1_t": "L0_ffn_w1", "w2_t": "L0_ffn_w2"}
SQUARE = ["L0_attn_Wq", "L0_attn_Wo", "wk_t", "wv_t", "x0q", "x0k", "x0v", "x0o",
          "L1_attn_Wq", "L1_attn_Wk", "L1_attn_Wv", "L1_attn_Wo", "x1q", "x1k", "x1v", "x1o"]


class Routing:
    pass


class Slots:
    pass


def program(nc, d, out, upto=99):
    with ExitStack() as ctx:
        k = Core(nc)
        k.x = k.sb(ctx, "x", [P, NT, D])
        k.xt = k.sb(ctx, "xt", [P, KD, T])
        attn = k.sb(ctx, "attn", [P, NT, D])
        k.ident = k.sb(ctx, "ident", [P, P])
        k.hmask = k.sb(ctx, "hmask", [P, HP])
        k.iota_in, k.before_in = d["c_iota"], d["c_before"]
        k.ps = ctx.enter_context(nc.psum_tensor("banks", [P, 8, 512], F32))
        k.zeros = k.sb(ctx, "zeros", [P, D])
        squares = ctx.enter_context(ExitStack())
        k.w = {name: k.sb(squares, name, [P, KD, D]) for name in SQUARE}
        k.slots_zeroed = nc.alloc_semaphore(name="slots_zeroed")
        k.slots_x = nc.dram_tensor("slots_x", (SLOT_TILES * P, D), F32).ap()
        q_scratch = nc.dram_tensor("q_parts", (3, B * D, S), BF16).ap()
        k_scratch = nc.dram_tensor("k_parts", (3, B * D, S), BF16).ap()
        w = k.w
        with ExitStack() as c:
            k.wd = k.sb(c, "wd", [P, KD, L])
            k.wuk = k.sb(c, "wuk", [L, D])
            k.wuv = k.sb(c, "wuv", [L, D])
            k.inside = k.sb(c, "inside", [1, 1], I32)
            k.decay = k.sb(c, "decay", [P, (2 * QT - 1) * P])
            v_heads = k.sb(c, "v_heads", [P, B * H, QT, HD])
            load_constants(k, d)
            if upto >= 1:
                normalise(k)
                latent_projections(k, v_heads, q_scratch, k_scratch)
                latent_attention(k, v_heads, attn, k.decay, q_scratch, k_scratch)
                project_out(k, w["L0_attn_Wo"], None, attn)
        if upto >= 2:
            normalise(k)
            cross_attention(k, attn, w["x0q"], w["x0k"], w["x0v"], d["L0_xattn_bq"], d["L0_xattn_bk"], d["L0_xattn_bv"],
                            d["c_mask0"], d["c_fill0"], d["c_ctx_t"])
            project_out(k, w["x0o"], d["L0_xattn_bo"], attn)
        if upto >= 3:
            with ExitStack() as c:
                w1q = k.sb(c, "w1q", [P, KD, F], BF16)
                w2q = k.sb(c, "w2q", [P, FT, D], BF16)
                winv = k.sb(c, "winv", [P, 2])
                quantise_weights(k, None, [w1q[:, :, :].rearrange("p k n -> p (k n)"), w2q[:, :, :].rearrange("p k n -> p (k n)")],
                                 winv, [(d["w1_t"], KD), (d["w2_t"], FT)], None)
                ternary_ffn(k, w1q, w2q, winv, d["L0_ffn_b1"], d["L0_ffn_b2"])
        if upto >= 4:
            normalise(k)
            feature_attention(k, attn, w["L1_attn_Wq"], w["L1_attn_Wk"], w["L1_attn_Wv"],
                              d["L1_attn_bq"], d["L1_attn_bk"], d["L1_attn_bv"], d["L1_attn_random_matrix"])
            project_out(k, w["L1_attn_Wo"], d["L1_attn_bo"], attn)
        if upto >= 5:
            normalise(k)
            cross_attention(k, attn, w["x1q"], w["x1k"], w["x1v"], d["L1_xattn_bq"], d["L1_xattn_bk"], d["L1_xattn_bv"],
                            d["c_mask1"], d["c_fill1"], d["c_ctx_t"])
            project_out(k, w["x1o"], d["L1_xattn_bo"], attn)
        squares.close()
        if upto >= 6:
            with ExitStack() as c:
                r = Routing()
                r.slot = k.sb(c, "slot", [P, 2, NT], U32)
                r.weight = k.sb(c, "choice_weight", [P, 2, NT])
                r.owner = k.sb(c, "tile_owner", [1, SLOT_TILES], I32)
                scratch = Slots()
                scratch.x = k.slots_x
                scratch.y = nc.dram_tensor("slots_y", (SLOT_TILES * P, D), F32).ap()
                scratch.b1 = nc.dram_tensor("b1_parts", (3, E, F), BF16).ap()
                r.w1 = k.sb(c, "experts_w1", [P, E, KD, F])
                r.w2 = k.sb(c, "experts_w2", [P, E, FT, D])
                normalise(k, keep=attn)
                route(k, r, attn, scratch, d["L1_ffn_Wg"], d["L1_ffn_bg"], d["L1_ffn_b1"], d["L1_ffn_W1"], d["L1_ffn_W2"],
                      d["L1_ffn_b2"])
                experts(k, r, scratch)
                combine(k, r, scratch, out)
        if upto < 6:
            k.next_block()
            stored = k.sem("stored")
            with nc.Block() as block:
                @block.sync
                def _(sp):
                    sp.dma_start(out.rearrange("b (t p) n -> p (b t) n", p=P), k.x[:, :, :]).then_inc(stored, 16)
                    sp.wait_ge(stored, 16)


COLUMNS = ["L0_xattn_bq", "L0_xattn_bk", "L1_attn_bq", "L1_attn_bk", "L1_xattn_bq", "L1_xattn_bk"]


def split3(v):
    rows = []
    for _ in range(3):
        m, e = np.frexp(v)
        part = np.trunc(m * 256.0) / 256.0 * 2.0 ** e
        rows.append(part)
        v = v - part
    assert v == 0
    return np.repeat(np.array(rows, np.float32)[:, None], P, axis=1)


def layout(inputs):
    a = {n: np.ascontiguousarray(inputs[n]) for n in INS}
    for n, src in TURNED.items():
        a[n] = np.ascontiguousarray(np.swapaxes(np.asarray(inputs[src]), -1, -2))
    for n in COLUMNS:
        b = np.asarray(inputs[n])
        a[n] = np.ascontiguousarray(np.swapaxes(b.reshape(b.shape[:-1] + (-1, P)), -1, -2))
    a["c_ctx_t"] = np.ascontiguousarray(np.asarray(inputs["ctx_1024"]).reshape(B * C, D).T)
    a["c_mask0"] = np.ascontiguousarray(inputs["mask_BxS2_bf1"]).view(np.uint8).reshape(B * C)
    a["c_mask1"] = np.ascontiguousarray(inputs["mask_Bx1x1xS2_ik0"]).reshape(B * C)
    a["c_fill0"], a["c_fill1"] = split3(-1e8), split3(-1e9)
    a["c_ident"] = np.eye(P, dtype=np.float32)
    a["c_hmask"] = (np.arange(P)[:, None] // HD == np.arange(HP)[None, :]).astype(np.float32)
    a["c_iota"] = np.repeat(np.arange(IOTA, dtype=np.float32)[None, :], P, axis=0)
    a["c_before"] = np.triu(np.ones((P, P), np.float32), 1)
    width = (2 * QT - 1) * P
    a["c_decay"] = np.exp(-DECAY * np.abs(np.arange(P)[:, None] + (QT - 1) * P - np.arange(width)[None, :])).astype(np.float32)
    return a


def kernel(**inputs):
    import concourse.bacc as bacc
    from concourse.bass_utils import run_bass_kernel_spmd

    nc = bacc.Bacc("TRN2", target_bir_lowering=False, num_devices=1)
    arrays = layout(inputs)
    d = {n: nc.dram_tensor(f"in_{n}", a.shape, mybir.dt.from_np(a.dtype), kind="ExternalInput").ap()
         for n, a in arrays.items()}
    out = nc.dram_tensor("out_0", (B, S, D), F32, kind="ExternalOutput").ap()
    program(nc, d, out)
    got = run_bass_kernel_spmd(nc, [{f"in_{n}": a for n, a in arrays.items()}], core_ids=[0])
    return got.results[0]["out_0"]
```

```python
from contextlib import ExitStack

import numpy as np

import concourse.bass as bass
from concourse import mybir

F32 = mybir.dt.float32
BF16 = mybir.dt.bfloat16
U32 = mybir.dt.uint32
I32 = mybir.dt.int32
ALU = mybir.AluOpType
ACT = mybir.ActivationFunctionType
AX = mybir.AxisListType.X

P = 128
B, S, D, H = 2, 1024, 256, 16
HD = D // H
T = B * S
KD = D // P
HP = P // HD
NT = T // P
TPG = 4
NG = NT // TPG
G = TPG * P
QT = S // P
C = 77
L = 64
F = 1024
FT = F // P
M = 64
E = 8
SLOT_TILES = 2 * NT + E - 1
SLOT = D + 2
IOTA = 40
LN_EPS = 1e-5
CLAMP = 10000.0
DECAY = 0.01 * 0.01
ROUND = 1.5 * 2.0 ** 23


def wait(eng, sem, value):
    if isinstance(value, int) and value <= 0:
        return
    eng.wait_ge(sem, value)


class Steps:

    def __init__(self, eng, sem, start=0):
        self.eng, self.sem, self.n = eng, sem, start

    def did(self, ins):
        ins.then_inc(self.sem, 1)
        self.n += 1

    def wait(self):
        self.eng.wait_ge(self.sem, self.n)


class Core:

    def __init__(self, nc):
        self.nc, self.block = nc, 0
        self.sems, self.zeroed = [], []

    def sb(self, ctx, name, shape, dt=F32):
        return ctx.enter_context(self.nc.sbuf_tensor(f"{name}_sb", list(shape), dt))

    def sem(self, name):
        self.sems.append(self.nc.alloc_semaphore(name=f"b{self.block}_{name}"))
        return self.sems[-1]

    def next_block(self):
        for s in self.zeroed:
            self.nc.release_semaphore(s)
        for s in self.sems:
            self.nc.gpsimd.sem_clear(s)
        self.sems, self.zeroed = [], self.sems
        self.block += 1


class Incoming:

    def __init__(self, nc, name, copies):
        self.done, self.copies, self.started = nc.alloc_semaphore(name=name), copies, False

    def start(self, eng):
        if not self.started:
            for dst, src in self.copies:
                eng.dma_start(dst, src).then_inc(self.done, 16)
        self.started = True

    def wait(self, eng):
        eng.wait_ge(self.done, 16 * len(self.copies))


def clear_slots(k, pool, zeros_set):
    pool.memset(k.zeros[:, :], 0.0).then_inc(zeros_set, 1)
    pool.wait_ge(zeros_set, 1)
    pool.dma_start(k.slots_x.rearrange("(t p) n -> p t n", p=P),
                   k.zeros[:, :].unsqueeze(1).to_broadcast([P, SLOT_TILES, SLOT])).then_inc(k.slots_zeroed, 16)


def square_weights(k, ctx, d, names):
    w = {n: k.sb(ctx, n, [P, KD, D]) for n in names}
    return w, [(w[n][:, :, :], d[n].rearrange("(k p) n -> p k n", p=P)) for n in names]


def load_tokens(k, d):
    nc = k.nc
    k.next_block()
    x_in, small_in = [k.sem(f"x_in{g}") for g in range(NG)], k.sem("small_in")
    with nc.Block() as block:
        @block.sync
        def _(sp):
            for g in range(NG):
                b, q = divmod(g * TPG, QT)
                sp.dma_start(k.x[:, g * TPG:(g + 1) * TPG, :],
                             d["x"][b, q * P:(q + TPG) * P, :].rearrange("(t p) n -> p t n", p=P)).then_inc(x_in[g], 16)
            sp.dma_start(k.ident[:, :], d["c_ident"]).then_inc(small_in, 16)
            sp.dma_start(k.hmask[:, :], d["c_hmask"]).then_inc(small_in, 16)
            sp.wait_ge(small_in, 2 * 16)

        @block.vector
        def _(dve):
            for t in range(NT):
                if t % TPG == 0:
                    dve.wait_ge(x_in[t // TPG], 16)
                dve.bn_stats(k.stats[:, t, :], k.x[:, t, :])
    k.stats_known = True


def normalise(k, loads, keep=None):
    nc = k.nc
    k.next_block()
    dve_own, var_ready, std_ready = k.sem("dve_own"), k.sem("var_ready"), k.sem("std_ready")
    xn_ready, turned, xt_done, loaded = k.sem("xn_ready"), k.sem("turned"), k.sem("xt_done"), k.sem("loaded")
    with ExitStack() as c, nc.Block() as block:
        sid = k.block
        mv = k.sb(c, f"mv{sid}", [P, NT, 2])
        var = k.sb(c, f"var{sid}", [P, NT])
        std = k.sb(c, f"std{sid}", [P, NT])
        std2 = k.sb(c, f"std2{sid}", [P, NT])
        rstd = k.sb(c, f"rstd{sid}", [P, NT])
        if keep is None:
            ring = k.sb(c, f"xn{sid}", [P, 2 * TPG, D])

        def xn(t):
            return ring[:, t % (2 * TPG), :] if keep is None else keep[:, t, 0:D]

        @block.sync
        def _(sp):
            for dst, src in loads:
                sp.dma_start(dst, src).then_inc(loaded, 16)
            wait(sp, loaded, 16 * len(loads))

        @block.vector
        def _(dve):
            own = Steps(dve, dve_own)
            if not k.stats_known:
                for t in range(NT):
                    own.did(dve.bn_stats(k.stats[:, t, :], k.x[:, t, :]))
                own.wait()
            for t in range(NT):
                own.did(dve.bn_aggr(mv[:, t, :], k.stats[:, t, :]))
            own.wait()
            dve.tensor_scalar(var[:, :], mv[:, :, 1], LN_EPS, None, ALU.add).then_inc(var_ready, 1)
            dve.wait_ge(std_ready, 1)
            own.did(dve.reciprocal(rstd[:, :], std[:, :]))
            own.wait()
            own.did(dve.tensor_tensor(std2[:, :], var[:, :], rstd[:, :], ALU.mult))
            own.wait()
            own.did(dve.tensor_tensor(std[:, :], std2[:, :], std[:, :], ALU.add))
            own.wait()
            own.did(dve.tensor_scalar(std2[:, :], std[:, :], 0.5, None, ALU.mult))
            own.wait()
            own.did(dve.reciprocal(rstd[:, :], std2[:, :]))
            own.wait()
            for t in range(NT):
                g, j = divmod(t, TPG)
                if j == 0:
                    wait(dve, turned, g - 1)
                dve.tensor_scalar(xn(t), k.x[:, t, :], mv[:, t, 0:1], rstd[:, t:t + 1],
                                  ALU.subtract, ALU.mult).then_inc(xn_ready, 1)

        @block.scalar
        def _(act):
            act.wait_ge(var_ready, 1)
            act.activation(std[:, :], var[:, :], ACT.Sqrt).then_inc(std_ready, 1)
            for g in range(NG):
                act.wait_ge(turned, g + 1)
                for kd in range(KD):
                    act.activation(k.xt[:, kd, g * G:(g + 1) * G], k.ps[:, 2 * (g % 2) + kd, :],
                                   ACT.Copy).then_inc(xt_done, 1)

        @block.tensor
        def _(pe):
            for g in range(NG):
                wait(pe, xt_done, KD * (g - 1))
                for j in range(TPG):
                    pe.wait_ge(xn_ready, g * TPG + j + 1)
                    for kd in range(KD):
                        last = pe.transpose(k.ps[:, 2 * (g % 2) + kd, j * P:(j + 1) * P],
                                            xn(g * TPG + j)[:, kd * P:(kd + 1) * P], k.ident[:, :])
                last.then_inc(turned, 1)


def project_out(k, w, bias, attn):
    nc = k.nc
    k.next_block()
    bias_in, biased = k.sem("bias_in"), k.sem("biased")
    turned, at_done = k.sem("turned"), k.sem("at_done")
    out_ready, added = k.sem("out_ready"), k.sem("added")
    with ExitStack() as c, nc.Block() as block:
        sid = k.block
        at = k.sb(c, f"at{sid}", [P, KD, 2, G])
        bb = k.sb(c, f"bb{sid}", [P, D])

        @block.sync
        def _(sp):
            if bias is not None:
                sp.dma_start(bb[:, :], bias.partition_broadcast(P)).then_inc(bias_in, 16)

        @block.gpsimd
        def _(pool):
            if bias is not None:
                pool.wait_ge(bias_in, 16)
                for t in range(NT):
                    pool.tensor_tensor(k.x[:, t, :], k.x[:, t, :], bb[:, :], ALU.add).then_inc(biased, 1)

        @block.tensor
        def _(pe):
            def turn(g):
                wait(pe, at_done, KD * (g - 1))
                for j in range(TPG):
                    for kd in range(KD):
                        last = pe.transpose(k.ps[:, 2 * (g % 2) + kd, j * P:(j + 1) * P],
                                            attn[:, g * TPG + j, kd * P:(kd + 1) * P], k.ident[:, :])
                last.then_inc(turned, 1)

            turn(0)
            for g in range(NG):
                if g + 1 < NG:
                    turn(g + 1)
                for j in range(TPG):
                    t = g * TPG + j
                    if j == 0:
                        pe.wait_ge(at_done, KD * (g + 1))
                    wait(pe, added, t - TPG + 1)
                    for kd in range(KD):
                        last = pe.matmul(k.ps[:, 4 + j, 0:D], at[:, kd, g % 2, j * P:(j + 1) * P], w[:, kd, :],
                                         start=kd == 0, stop=kd == KD - 1)
                    last.then_inc(out_ready, 1)

        @block.scalar
        def _(act):
            for g in range(NG):
                act.wait_ge(turned, g + 1)
                wait(act, out_ready, (g - 1) * TPG)
                for kd in range(KD):
                    act.activation(at[:, kd, g % 2, :], k.ps[:, 2 * (g % 2) + kd, :], ACT.Copy).then_inc(at_done, 1)

        @block.vector
        def _(dve):
            for t in range(NT):
                if bias is not None:
                    dve.wait_ge(biased, t + 1)
                dve.wait_ge(out_ready, t + 1)
                dve.tensor_tensor(k.x[:, t, :], k.x[:, t, :], k.ps[:, 4 + t % TPG, 0:D], ALU.add).then_inc(added, 1)
                if t > 0:
                    dve.wait_ge(added, t)
                    dve.bn_stats(k.stats[:, t - 1, :], k.x[:, t - 1, :])
            dve.wait_ge(added, NT)
            dve.bn_stats(k.stats[:, NT - 1, :], k.x[:, NT - 1, :])
        k.stats_known = True


def latent_projections(k, v_heads, q_scratch, k_scratch):
    nc = k.nc
    k.next_block()
    wsum_ready, wkv_ready, wkv_done = k.sem("wsum_ready"), k.sem("wkv_ready"), k.sem("wkv_done")
    lat_ready, lat_done = k.sem("lat_ready"), k.sem("lat_done")
    qk_ready, part1_done, rest1_done, part2_done, part3_done = (
        k.sem("qk_ready"), k.sem("part1_done"), k.sem("rest1_done"), k.sem("part2_done"), k.sem("part3_done"))
    v_ready, v_done = k.sem("v_ready"), k.sem("v_done")
    bound_own, largest_ready, largest_turned = k.sem("bound_own"), k.sem("largest_ready"), k.sem("largest_turned")
    stored = [k.sem(f"stored{s}") for s in range(4)]
    scale = 1.0 / 16.0
    NP = NG * 2 * KD
    with ExitStack() as c, nc.Block() as block:
        wsum = k.sb(c, "wsum", [P, KD, D])
        wkv = k.sb(c, "wkv", [P, KD, L])
        lat = k.sb(c, "lat", [L, T])
        parts = k.sb(c, "parts", [P, 4, 3, G], BF16)
        rest = k.sb(c, "rest", [P, 4, G])
        largest = k.sb(c, "largest", [P, NP])
        sides = k.sb(c, "sides", [P, 2])
        side_max = k.sb(c, "side_max", [1, 2])
        bound = k.sb(c, "bound", [1, 1])

        @block.tensor
        def _(pe):
            pe.wait_ge(wsum_ready, 1)
            for m in range(KD):
                for kd in range(KD):
                    last = pe.matmul(k.ps[:, 7, m * L:(m + 1) * L], wsum[:, kd, m * P:(m + 1) * P], k.wd[:, kd, :],
                                     start=kd == 0, stop=kd == KD - 1)
            last.then_inc(wkv_ready, 1)
            pe.wait_ge(wkv_done, 1)

            def latent(g):
                wait(pe, lat_done, g)
                for kd in range(KD):
                    last = pe.matmul(k.ps[0:L, 4, :], wkv[:, kd, :], k.xt[:, kd, g * G:(g + 1) * G],
                                     start=kd == 0, stop=kd == KD - 1)
                last.then_inc(lat_ready, 1)

            latent(0)
            for g in range(NG):
                rows = slice(g * G, (g + 1) * G)
                for m in range(KD):
                    n = 4 * g + m
                    wait(pe, rest1_done, n - 3)
                    for kd in range(KD):
                        last = pe.matmul(k.ps[:, m, :], k.w["L0_attn_Wq"][:, kd, m * P:(m + 1) * P],
                                         k.xt[:, kd, rows], start=kd == 0, stop=kd == KD - 1)
                    last.then_inc(qk_ready, 1)
                pe.wait_ge(lat_done, g + 1)
                for m in range(KD):
                    n = 4 * g + 2 + m
                    wait(pe, rest1_done, n - 3)
                    pe.matmul(k.ps[:, 2 + m, :], k.wuk[:, m * P:(m + 1) * P], lat[:, rows],
                              start=True, stop=True).then_inc(qk_ready, 1)
                if g + 1 < NG:
                    latent(g + 1)
                for j in range(TPG):
                    t = g * TPG + j
                    wait(pe, v_done, t - 1)
                    pe.matmul(k.ps[:, 5 + t % 2, 0:D], lat[:, t * P:(t + 1) * P], k.wuv[:, :],
                              start=True, stop=True).then_inc(v_ready, 1)
            pe.wait_ge(largest_ready, 1)
            for side in range(2):
                last = pe.transpose(k.ps[0:1, 7, side * P:(side + 1) * P], sides[:, side:side + 1], k.ident[:, :])
            last.then_inc(largest_turned, 1)

        @block.vector
        def _(dve):
            own = Steps(dve, bound_own)
            dve.tensor_tensor(wsum[:, :, :], k.w["wk_t"][:, :, :], k.w["wv_t"][:, :, :], ALU.add).then_inc(wsum_ready, 1)
            dve.wait_ge(wkv_ready, 1)
            dve.tensor_copy(wkv[:, :, :], k.ps[:, 7, 0:KD * L].rearrange("p (m n) -> p m n", m=KD)).then_inc(wkv_done, 1)
            for g in range(NG):
                for n in range(4 * g, 4 * g + 4):
                    s = n % 4
                    dve.wait_ge(part1_done, n + 1)
                    wait(dve, part2_done, n - 3)
                    wait(dve, part3_done, n - 3)
                    dve.scalar_tensor_tensor(out=rest[:, s, :], in0=k.ps[:, s, :], scalar=scale if s < 2 else 1.0,
                                             in1=parts[:, s, 0, :], op0=ALU.mult, op1=ALU.subtract).then_inc(rest1_done, 1)
                    own.did(dve.tensor_reduce(largest[:, n:n + 1], parts[:, s, 0, :], AX, ALU.max, apply_absolute_value=True))
                for n in range(4 * g, 4 * g + 4):
                    s = n % 4
                    dve.wait_ge(part2_done, n + 1)
                    dve.wait_ge(rest1_done, n + 1)
                    dve.tensor_tensor(parts[:, s, 2, :], rest[:, s, :], parts[:, s, 1, :],
                                      ALU.subtract).then_inc(part3_done, 1)

            own.wait()
            by_piece = largest[:, :].rearrange("p (g a m) -> p g a m", a=2, m=KD)
            for side in range(2):
                ins = dve.tensor_reduce(sides[:, side:side + 1], by_piece[:, :, side, :], mybir.AxisListType.XY, ALU.max)
                if side == 0:
                    own.did(ins)
                    own.wait()
            ins.then_inc(largest_ready, 1)
            dve.wait_ge(largest_turned, 1)
            own.did(dve.tensor_reduce(side_max[:, :], k.ps[0:1, 7, 0:2 * P].rearrange("p (a n) -> p a n", a=2), AX, ALU.max))
            own.wait()
            own.did(dve.tensor_tensor(bound[:, :], side_max[:, 0:1], side_max[:, 1:2], ALU.mult))
            own.wait()
            own.did(dve.tensor_scalar(k.inside[:, :], bound[:, :], 0.9 * CLAMP / HD, None, ALU.is_lt))
            own.wait()

        @block.scalar
        def _(act):
            def copy_latent(g):
                act.wait_ge(lat_ready, g + 1)
                act.activation(lat[:, g * G:(g + 1) * G], k.ps[0:L, 4, :], ACT.Copy).then_inc(lat_done, 1)

            copy_latent(0)
            for g in range(NG):
                for n in range(4 * g, 4 * g + 4):
                    s = n % 4
                    act.wait_ge(qk_ready, n + 1)
                    wait(act, stored[s], 16 * g)
                    act.activation(parts[:, s, 0, :], k.ps[:, s, :], ACT.Copy,
                                   scale=scale if s < 2 else 1.0).then_inc(part1_done, 1)
                if g + 1 < NG:
                    copy_latent(g + 1)
                for n in range(4 * g, 4 * g + 4):
                    s = n % 4
                    act.wait_ge(rest1_done, n + 1)
                    act.activation(parts[:, s, 1, :], rest[:, s, :], ACT.Copy).then_inc(part2_done, 1)
                for t in range(g * TPG, (g + 1) * TPG):
                    b, q = divmod(t, QT)
                    act.wait_ge(v_ready, t + 1)
                    act.activation(v_heads[:, b * H:(b + 1) * H, q, :],
                                   k.ps[:, 5 + t % 2, 0:D].rearrange("p (h d) -> p h d", d=HD),
                                   ACT.Copy).then_inc(v_done, 1)

        @block.sync
        def _(sp):
            for n in range(NP):
                g, s = divmod(n, 4)
                b, half = divmod(g, 2)
                m = s % 2
                scratch = q_scratch if s < 2 else k_scratch
                sp.wait_ge(part3_done, n + 1)
                sp.dma_start(scratch[:, b * D + m * P:b * D + (m + 1) * P, half * G:(half + 1) * G]
                             .rearrange("c p n -> p c n"), parts[:, s, :, :]).then_inc(stored[s], 16)
            for s in range(4):
                sp.wait_ge(stored[s], 16 * NG)


def latent_attention(k, v_heads, attn, decay, q_scratch, k_scratch):
    nc = k.nc
    k.next_block()
    stack_in = [k.sem(f"stack_in{u}") for u in range(2)]
    scored, clipped, peaked, shifted = (
        k.sem("scored"), k.sem("clipped"), k.sem("peaked"), k.sem("shifted"))
    exp_done, v_staged = k.sem("exp_done"), k.sem("v_staged")
    p_turned = [k.sem(f"p_turned{u}") for u in range(2)]
    pt_done = [k.sem(f"pt_done{u}") for u in range(2)]
    mixed, mix_copied, mix_turned, inverted, weighted = (
        k.sem("mixed"), k.sem("mix_copied"), k.sem("mix_turned"), k.sem("inverted"), k.sem("weighted"))
    zeroed, zeros_set = k.sem("zeroed"), k.sem("zeros_set")
    BODY = B
    NB = H
    TB = BODY * QT
    GB = TB // TPG
    LAG = 3
    TRAIL = 2 * TPG
    MIX_PARTS = [range(0, 3), range(3, 6), range(6, QT)]
    with ExitStack() as c, nc.Block() as block:
        qs = k.sb(c, "q_stack", [96, BODY, S], BF16)
        ks = k.sb(c, "k_stack", [96, BODY, S], BF16)
        vh = k.sb(c, "v_head", [P, BODY, QT, 32])
        sc = k.sb(c, "clipped_scores", [P, S])
        pr = k.sb(c, "probs", [P, 4, S])
        peak = k.sb(c, "peak", [P, 8])
        shift = k.sb(c, "shift", [P, 8])
        minus = k.sb(c, "minus", [P, 1])
        sums = k.sb(c, "sums", [P, 4, TPG])
        inv = k.sb(c, "inv", [P, 2, TPG])
        pt = k.sb(c, "probs_t", [P, TPG, 2, QT, P])
        mix = k.sb(c, "mix", [P, 2, P])

        def bodies(eng, body):
            body(0, True, False)
            with eng.Fori(1, NB - 1) as i:
                body(i, False, False)
            body(NB - 1, False, True)

        def steps(eng, step):
            for s in range(TB):
                step(0, s, lambda tile: tile >= 0)
            with eng.Fori(1, NB - 1) as i:
                for s in range(TB):
                    step(i, s, lambda tile: True)
            for s in range(TB):
                step(NB - 1, s, lambda tile: True)
            for s in range(TRAIL):
                step(NB, s, lambda tile: tile < 0)

        def copy_half(eng, i, s, half):
            n = i * TB + s
            eng.wait_ge(p_turned[half], n + 1)
            wait(eng, mixed, i * GB + s // TPG - 1)
            dst = pt[:, s % 4, (s // TPG) % 2, half * TPG:(half + 1) * TPG, :].rearrange("p t n -> p (t n)")
            if eng is nc.vector:
                ins = eng.tensor_copy(dst, k.ps[:, 4 + half, :])
            else:
                ins = eng.activation(dst, k.ps[:, 4 + half, :], ACT.Copy)
            ins.then_inc(pt_done[half], 1)

        @block.sync
        def _(sp):
            def body(i, first, last):
                for u in range(BODY):
                    wait(sp, scored, (i - 1) * TB + (u + 1) * QT if not first else 0)
                    for stack, scratch, order in ((qs, q_scratch, "q"), (ks, k_scratch, "k")):
                        row = 0
                        for r in range(3):
                            n = 3 - r
                            src = scratch[:, bass.ds(i * HD + u * D, HD), :]
                            if order == "q":
                                for x in range(n):
                                    sp.dma_start(stack[row + x * HD:row + (x + 1) * HD, u, :],
                                                 src[r:r + 1].rearrange("c p n -> (c p) n")).then_inc(stack_in[u], 16)
                            else:
                                for x in range(n):
                                    sp.dma_start(stack[row + x * HD:row + (x + 1) * HD, u, :],
                                                 src[x:x + 1].rearrange("c p n -> (c p) n")).then_inc(stack_in[u], 16)
                            row += n * HD
            bodies(sp, body)

        @block.gpsimd
        def _(pool):
            pool.memset(vh[:, :, :, :], 0.0).then_inc(zeroed, 1)
            pool.memset(minus[:, :], -1.0).then_inc(zeroed, 1)
            pool.wait_ge(zeroed, 2)

            def body(i, first, last):
                for s in range(TB):
                    u, q = divmod(s, QT)
                    n = i * TB + s
                    if q == 0:
                        wait(pool, mixed, i * GB - GB + (u + 1) * (QT // TPG) if not first else 0)
                        pool.tensor_copy(vh[:, u, :, 0:HD], v_heads[:, bass.ds(i + u * H, 1), :, :]
                                         .rearrange("p a t d -> p (a t) d")).then_inc(v_staged, 1)
                    pool.wait_ge(peaked, n + 1)
                    wait(pool, exp_done, n - 7)
                    pool.tensor_tensor(shift[:, s % 8:s % 8 + 1], peak[:, s % 8:s % 8 + 1], minus[:, :],
                                       ALU.mult).then_inc(shifted, 1)
            bodies(pool, body)
            clear_slots(k, pool, zeros_set)

        @block.tensor
        def _(pe):
            def scores(i, s):
                n = i * TB + s
                u, q = divmod(s % TB, QT)
                if q == 0:
                    pe.wait_ge(stack_in[u], (i + s // TB + 1) * 12 * 16)
                wait(pe, peaked, n - 1)
                for half in range(2):
                    last = pe.matmul(k.ps[:, 2 * (s % 2) + half, :], qs[:, u, q * P:(q + 1) * P],
                                     ks[:, u, half * 512:(half + 1) * 512], start=True, stop=True)
                last.then_inc(scored, 1)

            def turn(i, s):
                n = i * TB + s
                pe.wait_ge(exp_done, n + 1)
                for half in range(2):
                    wait(pe, pt_done[half], n)
                    for j in range(TPG):
                        last = pe.transpose(k.ps[:, 4 + half, j * P:(j + 1) * P],
                                            pr[:, s % 4, (half * TPG + j) * P:(half * TPG + j + 1) * P], k.ident[:, :])
                    last.then_inc(p_turned[half], 1)

            def mix_part(i, gs, part):
                gn = i * GB + gs
                u = gs % GB // (QT // TPG)
                if part == 0:
                    for half in range(2):
                        pe.wait_ge(pt_done[half], (gn + 1) * TPG)
                    pe.wait_ge(v_staged, i * BODY + gs // (QT // TPG) + 1)
                    wait(pe, mix_copied, gn)
                for kt in MIX_PARTS[part]:
                    for j in range(TPG):
                        last = pe.matmul(k.ps[32 * j:32 * j + 32, 6, 0:P], vh[:, u, kt, :],
                                         pt[:, j, gs % 2, kt, :], start=kt == 0, stop=kt == QT - 1)
                if part == len(MIX_PARTS) - 1:
                    last.then_inc(mixed, 1)

            def turn_mix(i, gs):
                gn = i * GB + gs
                pe.wait_ge(mix_copied, gn + 1)
                wait(pe, weighted, gn)
                pe.transpose(k.ps[:, 7, 0:P], mix[:, gs % 2, :], k.ident[:, :]).then_inc(mix_turned, 1)

            def step(i, s, due):
                if due(s - LAG):
                    turn(i, s - LAG)
                gs, part = divmod(s - TPG - LAG, TPG)
                if part < len(MIX_PARTS) and due(gs * TPG):
                    mix_part(i, gs, part)
                gs = s // TPG - 2
                if s % TPG == 2 and due(gs * TPG):
                    turn_mix(i, gs)
                if s < TB and not (i is NB or (i is NB - 1 and s >= TB - 2)):
                    scores(i, s + 2)

            scores(0, 0)
            scores(0, 1)
            steps(pe, step)

        @block.vector
        def _(dve):
            def weight(i, gs):
                gn = i * GB + gs
                u, half = divmod(gs % GB, QT // TPG)
                dve.wait_ge(exp_done, (gn + 1) * TPG)
                wait(dve, weighted, gn - 1)
                dve.reciprocal(inv[:, gs % 2, :], sums[:, gs % 4, :]).then_inc(inverted, 1)
                dve.wait_ge(inverted, gn + 1)
                dve.wait_ge(mix_turned, gn + 1)
                dve.tensor_tensor(
                    attn[:, u * QT + half * TPG:u * QT + (half + 1) * TPG, bass.ds((i + gs // GB) * HD, HD)],
                    k.ps[:, 7, 0:P].rearrange("p (t d) -> p t d", d=32)[:, :, 0:HD],
                    inv[:, gs % 2, :].unsqueeze(2).to_broadcast([P, TPG, HD]), ALU.mult).then_inc(weighted, 1)

            def clip(i, s):
                n = i * TB + s
                dve.wait_ge(scored, n + 1)
                wait(dve, peaked, n)
                dve.tensor_scalar(sc[:, :], k.ps[:, 2 * (s % 2):2 * (s % 2) + 2, :].rearrange("p a n -> p (a n)"),
                                  -CLAMP, CLAMP, ALU.max, ALU.min).then_inc(clipped, 1)
                dve.wait_ge(clipped, n + 1)

            def fade(i, s, scores):
                n = i * TB + s
                wait(dve, p_turned[1], n - 3)
                wait(dve, shifted, n - 7)
                off = (QT - 1 - s % QT) * P
                dve.nop(nofuse=True)
                dve.tensor_tensor_reduce(out=pr[:, s % 4, :], in0=scores, in1=decay[:, off:off + S],
                                         scale=1.0, scalar=-3.0e38, op0=ALU.mult, op1=ALU.max,
                                         accum_out=peak[:, s % 8:s % 8 + 1]).then_inc(peaked, 1)

            def trailing(i, s, due):
                if s % 2 == 1 and due(s - LAG):
                    copy_half(dve, i, s - LAG, 1)
                gs = s // TPG - 2
                if s % TPG == 3 and due(gs * TPG):
                    weight(i, gs)

            def clipping_step(i, s, due):
                if i is not NB:
                    clip(i, s)
                    fade(i, s, sc[:, :])
                trailing(i, s, due)

            def step(i, s, due):
                if i is not NB:
                    dve.wait_ge(scored, i * TB + s + 1)
                    fade(i, s, k.ps[:, 2 * (s % 2):2 * (s % 2) + 2, :].rearrange("p a n -> p (a n)"))
                trailing(i, s, due)

            inside = dve.value_load(k.inside[0:1, 0:1], min_val=0, max_val=1)
            with dve.If(inside > 0):
                steps(dve, step)
            with dve.Else():
                steps(dve, clipping_step)

        @block.scalar
        def _(act):
            def copy_mix(i, gs):
                gn = i * GB + gs
                act.wait_ge(mixed, gn + 1)
                wait(act, mix_turned, gn - 1)
                act.activation(mix[:, gs % 2, :], k.ps[:, 6, 0:P], ACT.Copy).then_inc(mix_copied, 1)

            def step(i, s, due):
                if due(s - LAG):
                    copy_half(act, i, s - LAG, 0)
                    if s % 2 == 0:
                        copy_half(act, i, s - LAG, 1)
                if i is not NB:
                    n = i * TB + s
                    act.wait_ge(shifted, n + 1)
                    wait(act, inverted, i * GB + s // TPG - 3)
                    act.activation(pr[:, s % 4, :], pr[:, s % 4, :], ACT.Exp, bias=shift[:, s % 8:s % 8 + 1],
                                   accum_out=sums[:, (s // TPG) % 4, s % 4:s % 4 + 1]).then_inc(exp_done, 1)
                gs = s // TPG - 2
                if s % TPG == 1 and due(gs * TPG):
                    copy_mix(i, gs)
            steps(act, step)


def context_operands(k, c, d, layer, mask, fill):
    sid = f"x{layer}"
    room = [k.sb(c, f"ctx{sid}", [P, KD, B * C]), k.sb(c, f"bq{sid}", [P, KD]), k.sb(c, f"bk{sid}", [P, KD]),
            k.sb(c, f"bv{sid}", [C, D]), k.sb(c, f"mask{sid}", [P, B * C], mask.dtype), k.sb(c, f"fill{sid}", [3, P])]
    sources = [d["c_ctx_t"].rearrange("(k p) n -> p k n", p=P), d[f"L{layer}_xattn_bq"], d[f"L{layer}_xattn_bk"],
               d[f"L{layer}_xattn_bv"].partition_broadcast(C), mask.partition_broadcast(P), fill]
    whole = [room[0][:, :, :]] + [a[:, :] for a in room[1:]]
    return room, list(zip(whole, sources))


def cross_attention(k, attn, wq, wk, wv, operands, later):
    nc = k.nc
    k.next_block()
    own_sem = k.sem("own")
    kv_ready, operands_done = k.sem("kv_ready"), k.sem("operands_done")
    q_ready, q_done = k.sem("q_ready"), k.sem("q_done")
    scored, shifted, exp_done = ([k.sem(f"{name}{u}") for u in range(2)] for name in ("scored", "shifted", "exp_done"))
    peaked, p_turned, pt_done, mixed = k.sem("peaked"), k.sem("p_turned"), k.sem("pt_done"), k.sem("mixed")
    mix_copied, mix_turned, inverted, weighted = k.sem("mix_copied"), k.sem("mix_turned"), k.sem("inverted"), k.sem("weighted")
    HB = 4
    NBK = H // HB
    HALF = NBK // 2
    VW = 32
    scale = 1.0 / 4.0
    with ExitStack() as c, nc.Block() as block:
        sid = k.block
        ctx_sb, bq_sb, bk_sb, bv_sb, mask_sb, fill_sb = operands
        hidden = k.sb(c, f"hidden{sid}", [P, B * C])
        keep = k.sb(c, f"keep{sid}", [P, B * C])
        hidden4 = k.sb(c, f"hidden4{sid}", [3, B, HB, C], BF16)
        fill_b = k.sb(c, f"fillb{sid}", [3, P], BF16)
        kt = k.sb(c, f"kt{sid}", [P, KD, B * C])
        kbd = k.sb(c, f"kbd{sid}", [P, B, KD, HP, C])
        va = k.sb(c, f"va{sid}", [C, B, H, VW])
        qt = k.sb(c, f"qt{sid}", [P, KD, T])
        pr = k.sb(c, f"pr{sid}", [P, 3, H, C])
        peak = k.sb(c, f"peak{sid}", [P, 2, H])
        pt = k.sb(c, f"pt{sid}", [C, 2, H, P])
        inv = k.sb(c, f"inv{sid}", [P, 2, H])
        mix = k.sb(c, f"mix{sid}", [P, NBK, P])

        @block.sync
        def _(sp):
            later.start(sp)

        @block.tensor
        def _(pe):
            for m in range(KD):
                for kd in range(KD):
                    pe.matmul(k.ps[:, 4 + m, 0:B * C], wk[:, kd, m * P:(m + 1) * P], ctx_sb[:, kd, :],
                              start=kd == 0, stop=kd == KD - 1)
            for b in range(B):
                for kd in range(KD):
                    last = pe.matmul(k.ps[0:C, 6 + b, 0:D], ctx_sb[:, kd, b * C:(b + 1) * C], wv[:, kd, :],
                                     start=kd == 0, stop=kd == KD - 1)
            last.then_inc(kv_ready, 1)
            for g in range(NG):
                for m in range(KD):
                    n = KD * g + m
                    wait(pe, q_done, n - 3)
                    for kd in range(KD):
                        last = pe.matmul(k.ps[:, n % 4, :], wq[:, kd, m * P:(m + 1) * P],
                                         k.xt[:, kd, g * G:(g + 1) * G], start=kd == 0, stop=kd == KD - 1)
                    last.then_inc(q_ready, 1)
            pe.wait_ge(operands_done, 1)
            pe.wait_ge(q_done, KD * NG)

            def scores(t, half):
                b = t // QT
                wait(pe, shifted[half], t)
                for a in range(half * HALF, (half + 1) * HALF):
                    kd, part = divmod(a, NBK // KD)
                    rhs = kbd[:, b, kd, part * HB:(part + 1) * HB, :].rearrange("p h n -> p (h n)")
                    pe.matmul(k.ps[:, a, 0:HB * C], qt[:, kd, t * P:(t + 1) * P], rhs, start=True, stop=False)
                    last = pe.matmul(k.ps[:, a, 0:HB * C], fill_b[:, :],
                                     hidden4[:, b, :, :].rearrange("p h n -> p (h n)"), start=False, stop=True)
                last.then_inc(scored[half], 1)

            def turn(t, a):
                n = NBK * t + a
                pe.wait_ge(exp_done[a // HALF], t + 1)
                wait(pe, pt_done, n - 1)
                for h in range(HB):
                    last = pe.transpose(k.ps[0:C, 4 + n % 2, h * P:(h + 1) * P], pr[:, t % 3, a * HB + h, :],
                                        k.ident[:, :])
                last.then_inc(p_turned, 1)

            def mix_values(t):
                pe.wait_ge(pt_done, NBK * (t + 1))
                wait(pe, mix_copied, t)
                for a in range(NBK):
                    for j in range(HB):
                        last = pe.matmul(k.ps[VW * j:VW * (j + 1), 6, a * P:(a + 1) * P], va[:, t // QT, a * HB + j, :],
                                         pt[:, t % 2, a * HB + j, :], start=True, stop=True)
                last.then_inc(mixed, 1)

            def turn_mix(t):
                pe.wait_ge(mix_copied, t + 1)
                wait(pe, weighted, t)
                for a in range(NBK):
                    last = pe.transpose(k.ps[:, 7, a * P:(a + 1) * P], mix[:, a, :], k.ident[:, :])
                last.then_inc(mix_turned, 1)

            for half in range(2):
                scores(0, half)
            for t in range(NT + 2):
                if t >= 2:
                    mix_values(t - 2)
                for a in range(NBK):
                    if 1 <= t <= NT:
                        turn(t - 1, a)
                    if t + 1 < NT and a in (1, 2):
                        scores(t + 1, a - 1)
                if t >= 2:
                    turn_mix(t - 2)

        @block.vector
        def _(dve):
            own = Steps(dve, own_sem)
            own.did(dve.tensor_scalar(hidden[:, :], mask_sb[:, :], 0.0, None, ALU.is_equal))
            own.did(dve.memset(va[:, :, :, :], 0.0))
            own.did(dve.tensor_copy(fill_b[:, :], fill_sb[:, :]))
            own.wait()
            own.did(dve.memset(va[:, :, :, HD:HD + 1], 1.0))
            own.did(dve.tensor_scalar(keep[:, :], hidden[:, :], -1.0, 1.0, ALU.mult, ALU.add))
            for b in range(B):
                for h in range(HB):
                    own.did(dve.tensor_copy(hidden4[:, b, h, :], hidden[0:3, b * C:(b + 1) * C]))
            dve.wait_ge(kv_ready, 1)
            for m in range(KD):
                own.did(dve.tensor_scalar(kt[:, m, :], k.ps[:, 4 + m, 0:B * C], bk_sb[:, m:m + 1], scale,
                                          ALU.add, ALU.mult))
            own.wait()
            for m in range(KD):
                own.did(dve.tensor_tensor(kt[:, m, :], kt[:, m, :], keep[:, :], ALU.mult))
            own.wait()
            for b in range(B):
                own.did(dve.tensor_tensor(va[:, b, :, 0:HD], k.ps[0:C, 6 + b, 0:D].rearrange("p (h d) -> p h d", d=HD),
                                          bv_sb[:, :].rearrange("p (h d) -> p h d", d=HD), ALU.add))
                for m in range(KD):
                    for h in range(HP):
                        last = dve.tensor_scalar(kbd[:, b, m, h, :], kt[:, m, b * C:(b + 1) * C],
                                                 k.hmask[:, h:h + 1], None, ALU.mult)
                        if not (b == B - 1 and m == KD - 1 and h == HP - 1):
                            own.did(last)
            own.wait()
            last.then_inc(operands_done, 1)

            def weight(t):
                dve.wait_ge(mix_turned, t + 1)
                o = k.ps[:, 7, :].rearrange("p (h d) -> p h d", d=VW)
                dve.reciprocal(inv[:, t % 2, :], o[:, :, HD]).then_inc(inverted, 1)
                dve.wait_ge(inverted, t + 1)
                dve.tensor_tensor(attn[:, t, 0:D].rearrange("p (h d) -> p h d", d=HD), o[:, :, 0:HD],
                                  inv[:, t % 2, :].unsqueeze(2).to_broadcast([P, H, HD]), ALU.mult).then_inc(weighted, 1)

            def shift(t, half):
                heads = slice(half * HALF * HB, (half + 1) * HALF * HB)
                dve.wait_ge(scored[half], t + 1)
                s = k.ps[:, half * HALF:(half + 1) * HALF, 0:HB * C].rearrange("p a (h n) -> p a h n", n=C)
                dve.tensor_reduce(peak[:, t % 2, heads].rearrange("p (a h) -> p a h", h=HB), s, AX, ALU.max).then_inc(peaked, 1)
                dve.wait_ge(peaked, 2 * t + half + 1)
                wait(dve, p_turned, NBK * (t - 2))
                dve.tensor_tensor(pr[:, t % 3, heads, :].rearrange("p (a h) n -> p a h n", h=HB), s,
                                  peak[:, t % 2, heads].rearrange("p (a h) -> p a h", h=HB).unsqueeze(3)
                                  .to_broadcast([P, HALF, HB, C]), ALU.subtract).then_inc(shifted[half], 1)

            for t in range(NT + 3):
                for half in range(2):
                    if t < NT:
                        shift(t, half)
                if t >= 3:
                    weight(t - 3)

        @block.scalar
        def _(act):
            def exponential(t, half):
                heads = slice(half * HALF * HB, (half + 1) * HALF * HB)
                act.wait_ge(shifted[half], t + 1)
                act.activation(pr[:, t % 3, heads, :].rearrange("p h n -> p (h n)"),
                               pr[:, t % 3, heads, :].rearrange("p h n -> p (h n)"), ACT.Exp).then_inc(exp_done[half], 1)

            def copy_turned(t, a):
                n = NBK * t + a
                act.wait_ge(p_turned, n + 1)
                wait(act, mixed, t - 1)
                act.activation(pt[:, t % 2, a * HB:(a + 1) * HB, :].rearrange("p h n -> p (h n)"),
                               k.ps[0:C, 4 + n % 2, :], ACT.Copy).then_inc(pt_done, 1)

            def copy_mix(t):
                act.wait_ge(mixed, t + 1)
                wait(act, mix_turned, t)
                act.activation(mix[:, :, :].rearrange("p a n -> p (a n)"), k.ps[:, 6, :], ACT.Copy).then_inc(mix_copied, 1)

            for n in range(KD * NG):
                g, m = divmod(n, KD)
                act.wait_ge(q_ready, n + 1)
                act.activation(qt[:, m, g * G:(g + 1) * G], k.ps[:, n % 4, :], ACT.Identity,
                               bias=bq_sb[:, m:m + 1]).then_inc(q_done, 1)
            for t in range(NT + 2):
                if t >= 2:
                    copy_mix(t - 2)
                for a in range(NBK):
                    if 1 <= t <= NT:
                        copy_turned(t - 1, a)
                    if t < NT and a % 2 == 1:
                        exponential(t, a // 2)


def quantise_weights(k, raws, quants, winvs):
    nc = k.nc
    k.next_block()
    own_sem, summed, totalled = k.sem("own"), k.sem("summed"), k.sem("totalled")
    with ExitStack() as c, nc.Block() as block:
        ones = k.sb(c, "ones_pp", [P, P])
        tmp = [k.sb(c, f"rawtmp{i}", [P, F * KD]) for i in range(2)]
        part = k.sb(c, "abs_sums", [P, 2])
        mean = k.sb(c, "abs_mean", [P, 2])
        wsc = k.sb(c, "w_scale", [P, 2])

        @block.sync
        def _(sp):
            raws.start(sp)

        @block.tensor
        def _(pe):
            pe.wait_ge(summed, 3)
            pe.matmul(k.ps[:, 0, 0:2], ones[:, :], part[:, :], start=True, stop=True).then_inc(totalled, 1)

        @block.scalar
        def _(act):
            raws.wait(act)
            for i in range(2):
                act.activation(tmp[i][:, :], raws.tiles[i][:, :], ACT.Abs, accum_out=part[:, i:i + 1]).then_inc(summed, 1)

        @block.vector
        def _(dve):
            own = Steps(dve, own_sem)
            dve.memset(ones[:, :], 1.0).then_inc(summed, 1)
            raws.wait(dve)
            dve.wait_ge(totalled, 1)
            own.did(dve.tensor_scalar(mean[:, :], k.ps[:, 0, 0:2], 1.0 / (F * D), 1e-5, ALU.mult, ALU.max))
            own.wait()
            own.did(dve.reciprocal(wsc[:, :], mean[:, :]))
            own.wait()
            own.did(dve.reciprocal(winvs[:, :], wsc[:, :]))
            for i in range(2):
                own.did(dve.tensor_scalar(tmp[i][:, :], raws.tiles[i][:, :], wsc[:, i:i + 1], ROUND, ALU.mult, ALU.add))
                own.wait()
                own.did(dve.tensor_scalar(raws.tiles[i][:, :], tmp[i][:, :], -ROUND, -1.0, ALU.add, ALU.max))
                own.wait()
                own.did(dve.tensor_scalar(quants[i], raws.tiles[i][:, :], 1.0, None, ALU.min))
            own.wait()


def ternary_ffn(k, w1q, w2q, winv, b1, b2):
    nc = k.nc
    k.next_block()
    loaded, own_sem = k.sem("loaded"), k.sem("own")
    var_ready, std_ready = k.sem("var_ready"), k.sem("std_ready")
    squared, rms_ready = k.sem("squared"), k.sem("rms_ready")
    xq_ready, x_turned, xqt_done, up_ready, pre_ready, gelu_done = (
        k.sem("xq_ready"), k.sem("x_turned"), k.sem("xqt_done"), k.sem("up_ready"), k.sem("pre_ready"), k.sem("gelu_done"))
    h_squared = k.sem("h_squared")
    hq_ready, h_turned, hqt_done, down_ready, added = (
        k.sem("hq_ready"), k.sem("h_turned"), k.sem("hqt_done"), k.sem("down_ready"), k.sem("added"))
    NF = F // 512
    normalised, x_squared = k.sem("normalised"), k.sem("x_squared")
    with ExitStack() as c, nc.Block() as block:
        mv = k.sb(c, "f_mv", [P, NT, 2])
        sm = k.sb(c, "f_small", [P, 11, NT])
        b1b = k.sb(c, "f_b1", [P, F])
        b2b = k.sb(c, "f_b2", [P, D])
        y = k.sb(c, "f_y", [P, NT, D])
        scr = k.sb(c, "f_scr", [P, 2, F])
        xr = k.sb(c, "f_xr", [P, 2, D])
        xq = k.sb(c, "f_xq", [P, 2, D], BF16)
        identb = k.sb(c, "f_identb", [P, P], BF16)
        xqt = k.sb(c, "f_xqt", [P, 2, KD, P], BF16)
        pre = k.sb(c, "f_pre", [P, 2, F])
        hh = k.sb(c, "f_h", [P, NT, F])
        hq = k.sb(c, "f_hq", [P, 2, F], BF16)
        hqt = k.sb(c, "f_hqt", [P, 2, FT, P], BF16)
        var, std, rstd, t1, ss, rms, peak, scl, xinv = (sm[:, i, :] for i in range(9))
        ss2, peak2 = sm[:, 9, :], sm[:, 10, :]
        psb = k.ps[:, :, :].rearrange("p a n -> p (a n)").bitcast(BF16).rearrange("p (a n) -> p a n", a=8)

        @block.sync
        def _(sp):
            sp.dma_start(b1b[:, :], b1.partition_broadcast(P)).then_inc(loaded, 16)
            sp.dma_start(b2b[:, :], b2.partition_broadcast(P)).then_inc(loaded, 16)

        def root(own, out, s, v, r, tmp, raw):
            own.did(own.eng.reciprocal(r, raw))
            own.wait()
            own.did(own.eng.tensor_tensor(tmp, v, r, ALU.mult))
            own.wait()
            own.did(own.eng.tensor_tensor(s, tmp, raw, ALU.add))
            own.wait()
            own.did(own.eng.tensor_scalar(tmp, s, 0.5, None, ALU.mult))
            own.wait()
            own.did(own.eng.reciprocal(out, tmp))
            own.wait()

        def quant_scales(own, peak_, rms_, winv_):
            dve = own.eng
            own.did(dve.tensor_tensor(t1, peak_, rms_, ALU.mult))
            own.wait()
            own.did(dve.tensor_scalar(t1, t1, 1e-5, None, ALU.max))
            own.wait()
            own.did(dve.reciprocal(scl, t1))
            own.wait()
            own.did(dve.tensor_scalar(scl, scl, 127.0, None, ALU.mult))
            own.wait()
            own.did(dve.reciprocal(xinv, scl))
            own.wait()
            own.did(dve.tensor_scalar(xinv, xinv, winv_, None, ALU.mult))
            own.wait()

        @block.vector
        def _(dve):
            own = Steps(dve, own_sem)
            if not k.stats_known:
                for t in range(NT):
                    own.did(dve.bn_stats(k.stats[:, t, :], k.x[:, t, :]))
            own.did(dve.tensor_copy(identb[:, :], k.ident[:, :]))
            own.wait()
            for t in range(NT):
                own.did(dve.bn_aggr(mv[:, t, :], k.stats[:, t, :]))
            own.wait()
            dve.tensor_scalar(var, mv[:, :, 1], LN_EPS, None, ALU.add).then_inc(var_ready, 1)
            dve.wait_ge(std_ready, 1)
            root(own, rstd, ss, var, scl, t1, std)
            for t in range(NT):
                dve.tensor_scalar(y[:, t, :], k.x[:, t, :], mv[:, t, 0:1], rstd[:, t:t + 1],
                                  ALU.subtract, ALU.mult).then_inc(normalised, 1)
            for t in range(NT):
                dve.wait_ge(normalised, t + 1)
                own.did(dve.tensor_reduce(peak[:, t:t + 1], y[:, t, :], AX, ALU.max, apply_absolute_value=True))
            own.wait()
            dve.wait_ge(x_squared, NT)
            dve.tensor_scalar(var, ss, 1.0 / D, LN_EPS, ALU.mult, ALU.add).then_inc(squared, 1)
            dve.wait_ge(rms_ready, 1)
            root(own, rms, ss, var, scl, t1, std)
            quant_scales(own, peak, rms, winv[:, 0:1])

            def quantise_x(t):
                wait(dve, x_turned, t - 1)
                own.did(dve.tensor_scalar(xr[:, t % 2, :], y[:, t, :], rms[:, t:t + 1], scl[:, t:t + 1],
                                          ALU.mult, ALU.mult))
                own.wait()
                dve.tensor_scalar(xq[:, t % 2, :], xr[:, t % 2, :], ROUND, -ROUND, ALU.add, ALU.add).then_inc(xq_ready, 1)

            quantise_x(0)
            quantise_x(1)
            dve.wait_ge(loaded, 32)
            for t in range(NT):
                dve.wait_ge(up_ready, t + 1)
                wait(dve, gelu_done, t - 1)
                dve.scalar_tensor_tensor(out=pre[:, t % 2, :], in0=k.ps[:, 2 + 2 * (t % 2):4 + 2 * (t % 2), :].rearrange("p a n -> p (a n)"),
                                         scalar=xinv[:, t:t + 1], in1=b1b[:, :], op0=ALU.mult, op1=ALU.add).then_inc(pre_ready, 1)
                if t + 2 < NT:
                    quantise_x(t + 2)
                if t > 0:
                    dve.wait_ge(gelu_done, t)
                    own.did(dve.tensor_reduce(peak2[:, t - 1:t], hh[:, t - 1, :], AX, ALU.max, apply_absolute_value=True))
            dve.wait_ge(gelu_done, NT)
            own.did(dve.tensor_reduce(peak2[:, NT - 1:NT], hh[:, NT - 1, :], AX, ALU.max, apply_absolute_value=True))
            own.wait()
            dve.wait_ge(h_squared, NT)
            dve.tensor_scalar(var, ss2, 1.0 / F, LN_EPS, ALU.mult, ALU.add).then_inc(squared, 1)
            dve.wait_ge(rms_ready, 2)
            root(own, rms, ss, var, scl, t1, std)
            quant_scales(own, peak2, rms, winv[:, 1:2])

            def quantise_h(t):
                wait(dve, h_turned, t - 1)
                own.did(dve.tensor_scalar(pre[:, t % 2, :], hh[:, t, :], rms[:, t:t + 1], scl[:, t:t + 1],
                                          ALU.mult, ALU.mult))
                own.wait()
                dve.tensor_scalar(hq[:, t % 2, :], pre[:, t % 2, :], ROUND, -ROUND, ALU.add, ALU.add).then_inc(hq_ready, 1)

            for t in range(NT):
                own.did(dve.tensor_tensor(k.x[:, t, :], k.x[:, t, :], b2b[:, :], ALU.add))
            own.wait()
            quantise_h(0)
            quantise_h(1)
            for t in range(NT):
                if t + 2 < NT:
                    quantise_h(t + 2)
                dve.wait_ge(down_ready, t + 1)
                dve.scalar_tensor_tensor(out=k.x[:, t, :], in0=k.ps[:, 6 + t % 2, 0:D], scalar=xinv[:, t:t + 1],
                                         in1=k.x[:, t, :], op0=ALU.mult, op1=ALU.add).then_inc(added, 1)

        @block.scalar
        def _(act):
            act.wait_ge(var_ready, 1)
            act.activation(std, var, ACT.Sqrt).then_inc(std_ready, 1)
            for t in range(NT):
                act.wait_ge(normalised, t + 1)
                wait(act, x_squared, t - 1)
                act.activation(scr[:, t % 2, 0:D], y[:, t, :], ACT.Square, accum_out=ss[:, t:t + 1]).then_inc(x_squared, 1)
            act.wait_ge(squared, 1)
            act.activation(std, var, ACT.Sqrt).then_inc(rms_ready, 1)

            def copy_x(t):
                act.wait_ge(x_turned, t + 1)
                wait(act, up_ready, t - 1)
                act.activation(xqt[:, t % 2, :, :].rearrange("p k n -> p (k n)"), psb[:, t % 2, 0:KD * P],
                               ACT.Copy).then_inc(xqt_done, 1)
            copy_x(0)
            for t in range(NT):
                if t + 1 < NT:
                    copy_x(t + 1)
                act.wait_ge(pre_ready, t + 1)
                act.activation(hh[:, t, :], pre[:, t % 2, :], ACT.Gelu).then_inc(gelu_done, 1)
                act.wait_ge(gelu_done, t + 1)
                wait(act, h_squared, t - 1)
                act.activation(scr[:, t % 2, :], hh[:, t, :], ACT.Square, accum_out=ss2[:, t:t + 1]).then_inc(h_squared, 1)
            act.wait_ge(squared, 2)
            act.activation(std, var, ACT.Sqrt).then_inc(rms_ready, 1)
            for t in range(NT):
                act.wait_ge(h_turned, t + 1)
                wait(act, down_ready, t - 1)
                act.activation(hqt[:, t % 2, :, :].rearrange("p k n -> p (k n)"),
                               psb[:, 2 + t % 2, :], ACT.Copy).then_inc(hqt_done, 1)

        @block.tensor
        def _(pe):
            def turn_x(t):
                pe.wait_ge(xq_ready, t + 1)
                wait(pe, xqt_done, t - 1)
                for kd in range(KD):
                    last = pe.transpose(psb[:, t % 2, kd * P:(kd + 1) * P], xq[:, t % 2, kd * P:(kd + 1) * P], identb[:, :])
                last.then_inc(x_turned, 1)

            turn_x(0)
            for t in range(NT):
                pe.wait_ge(xqt_done, t + 1)
                wait(pe, pre_ready, t - 1)
                for n in range(NF):
                    for kd in range(KD):
                        last = pe.matmul(k.ps[:, 2 + 2 * (t % 2) + n, :], xqt[:, t % 2, kd, :],
                                         w1q[:, kd, n * 512:(n + 1) * 512], start=kd == 0, stop=kd == KD - 1)
                last.then_inc(up_ready, 1)
                if t + 1 < NT:
                    turn_x(t + 1)
            pe.wait_ge(pre_ready, NT)

            def turn_h(t):
                pe.wait_ge(hq_ready, t + 1)
                wait(pe, hqt_done, t - 1)
                for f in range(FT):
                    last = pe.transpose(psb[:, 2 + t % 2, f * P:(f + 1) * P], hq[:, t % 2, f * P:(f + 1) * P], identb[:, :])
                last.then_inc(h_turned, 1)

            turn_h(0)
            turn_h(1)
            for t in range(NT):
                pe.wait_ge(hqt_done, t + 1)
                wait(pe, added, t - 1)
                for f in range(FT):
                    last = pe.matmul(k.ps[:, 6 + t % 2, 0:D], hqt[:, t % 2, f, :], w2q[:, f, :],
                                     start=f == 0, stop=f == FT - 1)
                last.then_inc(down_ready, 1)
                if t + 2 < NT:
                    turn_h(t + 2)
    k.stats_known = False


def feature_operands(k, c, d):
    room = [k.sb(c, "l_bq", [P, KD]), k.sb(c, "l_bk", [P, KD]), k.sb(c, "l_bv", [P, D]), k.sb(c, "l_r8", [P, M])]
    loads = [(room[0][:, :], d["L1_attn_bq"]), (room[1][:, :], d["L1_attn_bk"]),
             (room[2][:, :], d["L1_attn_bv"].partition_broadcast(P))]
    return room, loads + [(room[3][h * HD:(h + 1) * HD, :], d["L1_attn_random_matrix"]) for h in range(HP)]


def feature_attention(k, attn, wq, wk, wv, operands):
    nc = k.nc
    k.next_block()
    own_sem, operands_done = k.sem("own"), k.sem("operands_done")
    proj_ready, proj_done = k.sem("proj_ready"), k.sem("proj_done")
    v_ready, v_done = k.sem("v_ready"), k.sem("v_done")
    x_ready, low_ready, exp_done, feat_done = k.sem("x_ready"), k.sem("low_ready"), k.sem("exp_done"), k.sem("feat_done")
    kv_used, kv_done = k.sem("kv_used"), k.sem("kv_done")
    mixed, floored, inverted, weighted = k.sem("mixed"), k.sem("floored"), k.sem("inverted"), k.sem("weighted")
    V1 = HD + 1
    PAIRS = H // 2
    PW = 2 * V1
    FLOOR = 1e-6 * 256.0
    KP = NT * KD
    QP = NG * PAIRS
    with ExitStack() as c, nc.Block() as block:
        bq_sb, bk_sb, bv_sb, r8 = operands
        rbd = k.sb(c, "l_rbd", [P, HP, M])
        pj = k.sb(c, "l_pj", [P, 2, KD, G])
        va = k.sb(c, "l_va", [P, NT, H, V1])
        low = k.sb(c, "l_low", [P, 4, 512])
        kp = k.sb(c, "l_kp", [P, 3, KD, 512])
        qp = k.sb(c, "l_qp", [P, 2, PAIRS, G])
        kv = k.sb(c, "l_kv", [P, B, PAIRS, PW])
        den = k.sb(c, "l_den", [P, 2, H])
        inv = k.sb(c, "l_inv", [P, 2, H])

        @block.tensor
        def _(pe):
            def project(n, w):
                g, m = divmod(n % (KD * NG), KD)
                wait(pe, proj_done, n - 1)
                for kd in range(KD):
                    last = pe.matmul(k.ps[:, 4 + m, :], w[:, kd, m * P:(m + 1) * P],
                                     k.xt[:, kd, g * G:(g + 1) * G], start=kd == 0, stop=kd == KD - 1)
                last.then_inc(proj_ready, 1)

            def key_value(t):
                b, q = divmod(t, QT)
                pe.wait_ge(feat_done, KD * (t + 1))
                if q == 0:
                    wait(pe, kv_done, b)
                for p in range(PAIRS):
                    kd, r = divmod(p, PAIRS // KD)
                    last = pe.matmul(k.ps[:, 7, p * PW:(p + 1) * PW], kp[:, t % 3, kd, r * P:(r + 1) * P],
                                     va[:, t, 2 * p:2 * p + 2, :].rearrange("p h d -> p (h d)"),
                                     start=q == 0 and p == 0, stop=q == QT - 1, skip_group_check=True)
                last.then_inc(kv_used, 1)

            for m in range(KD):
                project(m, wk)
            pe.wait_ge(operands_done, 1)
            for g in range(NG):
                for j in range(TPG):
                    t = g * TPG + j
                    wait(pe, v_done, t)
                    for kd in range(KD):
                        last = pe.matmul(k.ps[:, 6, 0:D], k.xt[:, kd, t * P:(t + 1) * P], wv[:, kd, :],
                                         start=kd == 0, stop=kd == KD - 1)
                    last.then_inc(v_ready, 1)
                    if j == 0:
                        pe.wait_ge(proj_done, KD * (g + 1))
                    for kd in range(KD):
                        n = KD * t + kd
                        wait(pe, feat_done, n - 3)
                        pe.matmul(k.ps[:, n % 4, :], pj[:, g % 2, kd, j * P:(j + 1) * P],
                                  rbd[:, :, :].rearrange("p h m -> p (h m)"), start=True, stop=True).then_inc(x_ready, 1)
                    if t > 1:
                        wait(pe, v_done, t - 1)
                        key_value(t - 2)
                if g + 1 < NG:
                    for m in range(KD):
                        project(KD * (g + 1) + m, wk)
                else:
                    for m in range(KD):
                        project(KD * NG + m, wq)
            def mix(t):
                b = t // QT
                wait(pe, weighted, t - 1)
                if t == 0:
                    pe.wait_ge(kv_done, B)
                g, j = divmod(t, TPG)
                pe.wait_ge(feat_done, KP + PAIRS * (g + 1))
                for p in range(PAIRS):
                    last = pe.matmul(k.ps[:, 6 + t % 2, p * PW:(p + 1) * PW], qp[:, g % 2, p, j * P:(j + 1) * P],
                                     kv[:, b, p, :], start=True, stop=True)
                last.then_inc(mixed, 1)

            for g in range(NG):
                pe.wait_ge(proj_done, KD * (NG + g + 1))
                for p in range(PAIRS):
                    kd, r = divmod(p, PAIRS // KD)
                    n = KP + PAIRS * g + p
                    wait(pe, feat_done, n - 3)
                    pe.matmul(k.ps[:, n % 4, :], rbd[:, 2 * r:2 * r + 2, :].rearrange("p h m -> p (h m)"),
                              pj[:, g % 2, kd, :], start=True, stop=True).then_inc(x_ready, 1)
                    if g == 0 and p < 2:
                        pe.wait_ge(v_done, NT - 1 + p)
                        key_value(NT - 2 + p)
                    if g > 0 and p % 2 == 1:
                        mix((g - 1) * TPG + p // 2)
                if g + 1 < NG:
                    for m in range(KD):
                        project(KD * (NG + g + 1) + m, wq)
            for j in range(TPG):
                mix((NG - 1) * TPG + j)

        @block.scalar
        def _(act):
            def copy_proj(n):
                g, m = divmod(n, KD)
                act.wait_ge(proj_ready, n + 1)
                if 2 <= g < NG:
                    act.wait_ge(x_ready, KD * TPG * (g - 1))
                elif g >= NG:
                    act.wait_ge(x_ready, KP - KD * TPG if g == NG else (KP if g == NG + 1 else KP + PAIRS * (g - NG - 1)))
                bias = bk_sb if g < NG else bq_sb
                act.activation(pj[:, g % 2, m, :], k.ps[:, 4 + m, :], ACT.Identity, bias=bias[:, m:m + 1]).then_inc(proj_done, 1)

            for m in range(KD):
                copy_proj(m)
            for n in range(KP + QP):
                act.wait_ge(low_ready, n + 1)
                act.activation(low[:, n % 4, :], low[:, n % 4, :], ACT.Exp).then_inc(exp_done, 1)
                if n % (KD * TPG) == KD * TPG - 1 and (n + 1) // (KD * TPG) < 2 * NG:
                    for m in range(KD):
                        copy_proj(KD * ((n + 1) // (KD * TPG)) + m)

        @block.vector
        def _(dve):
            own = Steps(dve, own_sem)
            own.did(dve.memset(va[:, :, :, :], 1.0))
            own.did(dve.memset(kv[:, :, :, :], 0.0))
            for h in range(HP):
                last = dve.tensor_scalar(rbd[:, h, :], r8[:, :], k.hmask[:, h:h + 1], None, ALU.mult)
                if h < HP - 1:
                    own.did(last)
            own.wait()
            last.then_inc(operands_done, 1)

            def lower(n):
                dve.wait_ge(x_ready, n + 1)
                wait(dve, feat_done, n - 3)
                dve.tensor_scalar(low[:, n % 4, :], k.ps[:, n % 4, :], 0.0, None, ALU.min).then_inc(low_ready, 1)

            def feature(n):
                dve.wait_ge(exp_done, n + 1)
                if n < KP:
                    t, kd = divmod(n, KD)
                    wait(dve, kv_used, t - 2)
                    dst = kp[:, t % 3, kd, :]
                else:
                    g, p = divmod(n - KP, PAIRS)
                    wait(dve, mixed, TPG * (g - 1))
                    dst = qp[:, g % 2, p, :]
                dve.scalar_tensor_tensor(out=dst, in0=k.ps[:, n % 4, :], scalar=0.0, in1=low[:, n % 4, :],
                                         op0=ALU.max, op1=ALU.add).then_inc(feat_done, 1)

            def copy_v(t):
                dve.wait_ge(v_ready, t + 1)
                dve.tensor_tensor(va[:, t, :, 0:HD], k.ps[:, 6, 0:D].rearrange("p (h d) -> p h d", d=HD),
                                  bv_sb[:, :].rearrange("p (h d) -> p h d", d=HD), ALU.add).then_inc(v_done, 1)

            def copy_kv(b):
                dve.wait_ge(kv_used, QT * (b + 1))
                src = k.ps[:, 7, 0:PAIRS * PW].rearrange("p (a n) -> p a n", n=PW)
                own.did(dve.tensor_copy(kv[0:64, b, :, 0:V1], src[0:64, :, 0:V1]))
                dve.tensor_copy(kv[64:P, b, :, V1:PW], src[64:P, :, V1:PW]).then_inc(kv_done, 1)
                own.wait()

            def weight(t):
                dve.wait_ge(mixed, t + 1)
                o = k.ps[:, 6 + t % 2, 0:H * V1].rearrange("p (h d) -> p h d", d=V1)
                dve.tensor_scalar(den[:, t % 2, :], o[:, :, HD], FLOOR, None, ALU.max).then_inc(floored, 1)
                dve.wait_ge(floored, t + 1)
                dve.reciprocal(inv[:, t % 2, :], den[:, t % 2, :]).then_inc(inverted, 1)
                dve.wait_ge(inverted, t + 1)
                dve.tensor_tensor(attn[:, t, 0:D].rearrange("p (h d) -> p h d", d=HD), o[:, :, 0:HD],
                                  inv[:, t % 2, :].unsqueeze(2).to_broadcast([P, H, HD]), ALU.mult).then_inc(weighted, 1)

            copy_v(0)
            lower(0)
            for n in range(1, KP + QP + 1):
                if n < KP + QP:
                    if n < KP and n % KD == 0:
                        copy_v(n // KD)
                    lower(n)
                feature(n - 1)
                done = n
                if done == KD * (QT + 1) + 2:
                    copy_kv(0)
                if done == KP + 3:
                    copy_kv(1)
                g, p = divmod(done - KP - 1, PAIRS)
                if done - KP - 1 >= PAIRS and p % 2 == 1 and p // 2 < TPG and g <= NG - 1:
                    weight((g - 1) * TPG + p // 2)
            for j in range(TPG):
                weight((NG - 1) * TPG + j)


def route(k, r, xn, scratch, wg, bg, b1, w2, b2):
    nc = k.nc
    k.next_block()
    loaded, weights_in, own_sem, gated, cw_done = (
        k.sem("loaded"), k.sem("weights_in"), k.sem("own"), k.sem("gated"), k.sem("cw_done"))
    exp_ready, exp_done, turned, turned_done = k.sem("exp_ready"), k.sem("exp_done"), k.sem("turned"), k.sem("turned_done")
    b2_ready, b2_added = k.sem("b2_ready"), k.sem("b2_added")
    hot_done, ones_set, counted, placed, scattered = (
        k.sem("hot_done"), k.sem("ones_set"), k.sem("counted"), k.sem("placed"), k.sem("scattered"))
    numbered = k.sem("numbered")
    with ExitStack() as c, nc.Block() as block:
        wg_sb = k.sb(c, "wg", [P, KD, E])
        bg_sb = k.sb(c, "bg", [P, E])
        b2_sb = k.sb(c, "b2", [E, D])
        iota = k.sb(c, "iota", [P, IOTA])
        before = k.sb(c, "before", [P, P])
        numbers = k.sb(c, "numbers", [P, NT])
        ones = k.sb(c, "ones", [P, P])
        logit = k.sb(c, "logit", [P, NT, E])
        prob = k.sb(c, "prob", [P, NT, E])
        m1 = k.sb(c, "gate_max", [P, NT])
        ssum = k.sb(c, "gate_sum", [P, NT])
        inv = k.sb(c, "gate_inv", [P, NT])
        best = k.sb(c, "best", [P, NT, 8])
        best_at = k.sb(c, "best_at", [P, NT, 8], U32)
        at = k.sb(c, "at_f", [P, NT, 8])
        hot = k.sb(c, "hot", [P, 2, NT, E])
        both = k.sb(c, "both", [P, NT, E])
        cw = k.sb(c, "cw", [P, NT, E])
        weighed = k.sb(c, "weighed", [P, NT, E])
        upto = k.sb(c, "tokens_before", [P, NT + 1, E])
        total = k.sb(c, "tile_total", [P, NT, E])
        over = k.sb(c, "over", [P, E, NT])
        tiles = k.sb(c, "expert_tiles", [P, E])
        first = k.sb(c, "first_tile", [P, E])
        place = k.sb(c, "place", [P, NT, E])
        place_r = k.sb(c, "place_r", [P, 2, NT])
        owned = k.sb(c, "owned", [P, SLOT_TILES, E])
        owner = k.sb(c, "owner", [1, SLOT_TILES])
        cwt = k.sb(c, "cwt", [E, NT, P])

        def wide(a):
            return a.unsqueeze(2).to_broadcast([P, NT, E])

        @block.sync
        def _(sp):
            sp.dma_start(wg_sb[:, :, :], wg.rearrange("(k p) n -> p k n", p=P)).then_inc(loaded, 16)
            sp.dma_start(bg_sb[:, :], bg.partition_broadcast(P)).then_inc(loaded, 16)
            sp.dma_start(b2_sb[:, :], b2).then_inc(loaded, 16)
            sp.dma_start(iota[:, :], k.iota_in).then_inc(loaded, 16)
            sp.dma_start(before[:, :], k.before_in).then_inc(loaded, 16)
            sp.dma_start(numbers[:, :], k.numbers_in).then_inc(loaded, 16)
            sp.dma_start(r.b1[:, :, :], b1.rearrange("e p k -> p e k")).then_inc(weights_in, 16)
            r.w1_in.start(sp)
            for e in range(E):
                sp.dma_start(r.w2[:, e, :, :], w2[e].rearrange("(k p) n -> p k n", p=P)).then_inc(weights_in, 16)
            sp.wait_ge(weights_in, (E + 1) * 16)
            r.w1_in.wait(sp)

        @block.gpsimd
        def _(pool):
            pool.memset(ones[:, :], 1.0).then_inc(ones_set, 1)
            pool.wait_ge(k.slots_zeroed, 16)
            pool.wait_ge(placed, 1)
            pool.wait_ge(numbered, 2)
            for n in range(2 * NT):
                choice, t = divmod(n, NT)
                pool.indirect_dma_start(out=scratch.x[:, :], out_offset=bass.IndirectOffsetOnAxis(ap=r.slot[:, choice, t:t + 1], axis=0),
                                        in_=xn[:, t, :], in_offset=None).then_inc(scattered, 16)
            pool.wait_ge(scattered, 2 * NT * 16)

        @block.tensor
        def _(pe):
            pe.wait_ge(loaded, 96)
            for t in range(NT):
                for kd in range(KD):
                    last = pe.matmul(k.ps[:, 0, t * E:(t + 1) * E], k.xt[:, kd, t * P:(t + 1) * P], wg_sb[:, kd, :],
                                     start=kd == 0, stop=kd == KD - 1)
            last.then_inc(gated, 1)
            pe.wait_ge(hot_done, 1)
            pe.wait_ge(ones_set, 1)
            hs = both[:, :, :].rearrange("p t e -> p (t e)")
            pe.matmul(k.ps[:, 7, 0:NT * E], before[:, :], hs, start=True, stop=True)
            pe.matmul(k.ps[:, 7, NT * E:2 * NT * E], ones[:, :], hs, start=True, stop=True).then_inc(counted, 1)
            pe.wait_ge(cw_done, 1)
            for g in range(NG):
                for j in range(TPG):
                    last = pe.transpose(k.ps[0:E, 1 + g, j * P:(j + 1) * P], cw[:, g * TPG + j, :], k.ident[:, :])
                last.then_inc(turned, 1)
            for t in range(NT):
                pe.wait_ge(turned_done, t // TPG + 1)
                wait(pe, b2_added, t - 1)
                pe.matmul(k.ps[:, 5 + t % 2, 0:D], cwt[:, t, :], b2_sb[:, :], start=True, stop=True).then_inc(b2_ready, 1)

        @block.scalar
        def _(act):
            act.wait_ge(exp_ready, 1)
            act.activation(prob[:, :, :].rearrange("p t e -> p (t e)"), logit[:, :, :].rearrange("p t e -> p (t e)"),
                           ACT.Exp).then_inc(exp_done, 1)
            for g in range(NG):
                act.wait_ge(turned, g + 1)
                act.activation(cwt[:, g * TPG:(g + 1) * TPG, :].rearrange("p t n -> p (t n)"), k.ps[0:E, 1 + g, :],
                               ACT.Copy).then_inc(turned_done, 1)

        @block.vector
        def _(dve):
            own = Steps(dve, own_sem)

            def step(ins):
                own.did(ins)
                own.wait()

            dve.wait_ge(loaded, 96)
            dve.tensor_copy(xn[:, :, D], numbers[:, :]).then_inc(numbered, 1)
            dve.wait_ge(gated, 1)
            step(dve.tensor_tensor(logit[:, :, :], k.ps[:, 0, 0:NT * E].rearrange("p (t e) -> p t e", e=E),
                                   bg_sb[:, :].unsqueeze(1).to_broadcast([P, NT, E]), ALU.add))
            step(dve.tensor_reduce(m1[:, :], logit[:, :, :], AX, ALU.max))
            dve.tensor_tensor(logit[:, :, :], logit[:, :, :], wide(m1[:, :]), ALU.subtract).then_inc(exp_ready, 1)
            dve.wait_ge(exp_done, 1)
            step(dve.tensor_reduce(ssum[:, :], prob[:, :, :], AX, ALU.add))
            step(dve.reciprocal(inv[:, :], ssum[:, :]))
            step(dve.tensor_tensor(prob[:, :, :], prob[:, :, :], wide(inv[:, :]), ALU.mult))
            for t in range(NT):
                own.did(dve.max(best[:, t, :], prob[:, t, :]))
            own.wait()
            for t in range(NT):
                own.did(dve.max_index(best_at[:, t, :], best[:, t, :], prob[:, t, :]))
            own.wait()
            step(dve.tensor_copy(at[:, :, :], best_at[:, :, :]))
            dve.tensor_scalar(xn[:, :, D + 1], at[:, :, 0], 1.0, None, ALU.add).then_inc(numbered, 1)
            for n in range(2):
                own.did(dve.tensor_tensor(hot[:, n, :, :], iota[:, 0:E].unsqueeze(1).to_broadcast([P, NT, E]),
                                          wide(at[:, :, n]), ALU.is_equal))
            own.wait()
            dve.tensor_tensor(both[:, :, :], hot[:, 0, :, :], hot[:, 1, :, :], ALU.add).then_inc(hot_done, 1)
            own.did(dve.memset(upto[:, 0, :], 0.0))
            dve.wait_ge(counted, 1)
            step(dve.tensor_copy(total[:, :, :], k.ps[:, 7, NT * E:2 * NT * E].rearrange("p (t e) -> p t e", e=E)))
            for t in range(NT):
                step(dve.tensor_tensor(upto[:, t + 1, :], upto[:, t, :], total[:, t, :], ALU.add))
            step(dve.tensor_scalar(tiles[:, :], upto[:, NT, :], 1.0 / P, None, ALU.mult))
            step(dve.tensor_tensor(over[:, :, :], tiles[:, :].unsqueeze(2).to_broadcast([P, E, NT]),
                                   iota[:, 0:NT].unsqueeze(1).to_broadcast([P, E, NT]), ALU.is_gt))
            own.did(dve.memset(first[:, 0:1], 0.0))
            step(dve.tensor_reduce(tiles[:, :], over[:, :, :], AX, ALU.add))
            for e in range(1, E):
                step(dve.tensor_tensor(first[:, e:e + 1], first[:, e - 1:e], tiles[:, e - 1:e], ALU.add))
            step(dve.tensor_tensor(place[:, :, :], upto[:, 0:NT, :],
                                   k.ps[:, 7, 0:NT * E].rearrange("p (t e) -> p t e", e=E), ALU.add))
            step(dve.tensor_scalar(tiles[:, :], first[:, :], float(P), None, ALU.mult))
            step(dve.tensor_tensor(place[:, :, :], place[:, :, :], tiles[:, :].unsqueeze(1).to_broadcast([P, NT, E]), ALU.add))
            for n in range(2):
                step(dve.tensor_tensor(weighed[:, :, :], hot[:, n, :, :], place[:, :, :], ALU.mult))
                step(dve.tensor_reduce(place_r[:, n, :], weighed[:, :, :], AX, ALU.add))
            dve.tensor_copy(r.slot[:, :, :], place_r[:, :, :]).then_inc(placed, 1)
            step(dve.tensor_tensor(owned[:, :, :], iota[:, 0:SLOT_TILES].unsqueeze(2).to_broadcast([P, SLOT_TILES, E]),
                                   first[:, :].unsqueeze(1).to_broadcast([P, SLOT_TILES, E]), ALU.is_ge))
            step(dve.tensor_reduce(r.owned[:, :], owned[:, :, :], AX, ALU.add))
            step(dve.tensor_scalar(owner[:, :], r.owned[0:1, :], -1.0, None, ALU.add))
            own.did(dve.tensor_copy(r.owner[:, :], owner[:, :]))
            step(dve.tensor_tensor(ssum[:, :], best[:, :, 0], best[:, :, 1], ALU.add))
            step(dve.tensor_scalar(ssum[:, :], ssum[:, :], 1e-8, None, ALU.add))
            step(dve.reciprocal(inv[:, :], ssum[:, :]))
            for n in range(2):
                step(dve.tensor_tensor(r.weight[:, n, :], best[:, :, n], inv[:, :], ALU.mult))
                step(dve.tensor_tensor(hot[:, n, :, :], hot[:, n, :, :], wide(r.weight[:, n, :]), ALU.mult))
            dve.tensor_tensor(cw[:, :, :], hot[:, 0, :, :], hot[:, 1, :, :], ALU.add).then_inc(cw_done, 1)
            for t in range(NT):
                dve.wait_ge(b2_ready, t + 1)
                dve.tensor_tensor(k.x[:, t, :], k.x[:, t, :], k.ps[:, 5 + t % 2, 0:D], ALU.add).then_inc(b2_added, 1)


def experts(k, r, scratch):
    nc = k.nc
    k.next_block()
    x_in = [k.sem(f"x_in{u}") for u in range(2)]
    y_out = [k.sem(f"y_out{u}") for u in range(2)]
    x_turned, x_copied, chosen = k.sem("x_turned"), k.sem("x_copied"), k.sem("chosen")
    pre_ready, h_done = k.sem("pre_ready"), k.sem("h_done")
    y_ready, y_copied, to_taken = k.sem("y_ready"), k.sem("y_copied"), k.sem("to_taken")
    BODY = 2
    NB = (SLOT_TILES - 1) // BODY
    HALF = FT // 2
    idle_in, row_step = k.sem("idle_in"), k.sem("row_step")
    with ExitStack() as c, nc.Block() as block:
        w1 = k.sb(c, "tile_w1", [P, 2, KD, F])
        b1 = k.sb(c, "tile_b1", [P, 2, FT])
        xs = k.sb(c, "slots_x", [P, 2, SLOT])
        is_best = k.sb(c, "is_best", [P, 2])
        to = k.sb(c, "output_row", [P, 2], U32)
        idle = k.sb(c, "idle_rows", [P, SLOT_TILES])
        xst = k.sb(c, "slots_xt", [P, 2, KD, P])
        ys = k.sb(c, "slots_y", [P, 2, D])
        ht = k.xt[:, 0, :].rearrange("p (u f n) -> p u f n", u=2, f=FT)

        def bodies(eng, step):
            for s in range(BODY):
                step(0, s)
            with eng.Fori(1, NB - 1) as i:
                for s in range(BODY):
                    step(i, s)
            for s in range(BODY):
                step(NB - 1, s)
            step(NB, 0)

        def exists(i, s):
            return not isinstance(i, int) or i * BODY + s < SLOT_TILES

        @block.sync
        def _(sp):
            def step(i, s):
                n = i * BODY + s
                wait(sp, x_turned, n - 1)
                wait(sp, to_taken, n - 1)
                sp.dma_start(xs[:, s, :], scratch.x[bass.ds(n * P, P), :]).then_inc(x_in[s], 16)
            sp.dma_start(idle[:, :], k.idle_in).then_inc(idle_in, 16)
            bodies(sp, step)

        @block.tensor
        def _(pe):
            def turn_x(i, s):
                n = i * BODY + s
                u = s % 2
                pe.wait_ge(x_in[u], (i + s // BODY + 1) * 16)
                wait(pe, x_copied, n)
                for kd in range(KD):
                    last = pe.transpose(k.ps[:, 7, (u * KD + kd) * P:(u * KD + kd + 1) * P],
                                        xs[:, u, kd * P:(kd + 1) * P], k.ident[:, :])
                last.then_inc(x_turned, 1)

            def up(i, s):
                n = i * BODY + s
                u = s % 2
                pe.wait_ge(x_copied, n + 1)
                pe.wait_ge(chosen, 2 * n + 2)
                for f in range(FT):
                    if f % HALF == 0:
                        wait(pe, h_done, 2 * (n - 2) + f // HALF + 1)
                    for kd in range(KD):
                        last = pe.matmul(k.ps[:, 2 * u + f // HALF, (f % HALF) * P:(f % HALF + 1) * P],
                                         w1[:, u, kd, f * P:(f + 1) * P], xst[:, u, kd, :], start=kd == 0, stop=kd == KD - 1)
                    if f % HALF == HALF - 1:
                        last.then_inc(pre_ready, 1)

            def down(i, s):
                n = i * BODY + s
                pe.wait_ge(h_done, 2 * n + 2)
                wait(pe, y_copied, n)
                pe.nop(nofuse=True)
                e = pe.value_load(r.owner[0:1, bass.ds(n, 1)], min_val=0, max_val=E - 1)
                for f in range(FT):
                    last = pe.matmul(k.ps[:, 6, s * D:(s + 1) * D], ht[:, s, f, :],
                                     r.w2[:, bass.ds(e, 1), f, :].rearrange("p a n -> p (a n)"), start=f == 0, stop=f == FT - 1)
                last.then_inc(y_ready, 1)

            def step(i, s):
                if exists(i, s + 1):
                    up(i, s + 1)
                if exists(i, s + 2):
                    turn_x(i, s + 2)
                down(i, s)

            turn_x(0, 0)
            turn_x(0, 1)
            up(0, 0)
            bodies(pe, step)

        @block.gpsimd
        def _(pool):
            def step(i, s):
                n = i * BODY + s
                pool.wait_ge(to_taken, n + 1)
                pool.wait_ge(y_copied, n + 1)
                pool.nop(nofuse=True)
                pool.indirect_dma_start(out=scratch.y[:, :], out_offset=bass.IndirectOffsetOnAxis(ap=to[:, s:s + 1], axis=0),
                                        in_=ys[:, s, :], in_offset=None).then_inc(y_out[s], 16)
            bodies(pool, step)

        @block.scalar
        def _(act):
            def copy_x(i, s):
                n = i * BODY + s
                u = s % 2
                act.wait_ge(x_turned, n + 1)
                wait(act, pre_ready, 2 * (n - 1))
                act.activation(xst[:, u, :, :].rearrange("p k n -> p (k n)"), k.ps[:, 7, u * D:(u + 1) * D],
                               ACT.Copy).then_inc(x_copied, 1)

            def hidden(i, s):
                n = i * BODY + s
                act.wait_ge(chosen, 2 * n + 2)
                wait(act, y_ready, n - 1)
                for f in range(FT):
                    if f % HALF == 0:
                        act.wait_ge(pre_ready, 2 * n + f // HALF + 1)
                    ins = act.activation(ht[:, s, f, :], k.ps[:, 2 * s + f // HALF, (f % HALF) * P:(f % HALF + 1) * P],
                                         ACT.Gelu_apprx_tanh, bias=b1[:, s, f:f + 1])
                    if f % HALF == HALF - 1:
                        ins.then_inc(h_done, 1)

            def step(i, s):
                hidden(i, s)
                if exists(i, s + 2):
                    copy_x(i, s + 2)

            copy_x(0, 0)
            copy_x(0, 1)
            bodies(act, step)

        @block.vector
        def _(dve):
            def take_rows(i, s):
                u, later = s % 2, s // BODY
                dve.wait_ge(x_in[u], (i + later + 1) * 16)
                if not (isinstance(i, int) and i + later == 0):
                    dve.wait_ge(y_out[u], (i + later) * 16)
                tile = bass.ds(i * BODY + s, 1)
                dve.tensor_tensor(is_best[:, u:u + 1], xs[:, u, D + 1:SLOT], r.owned[:, tile], ALU.is_equal).then_inc(row_step, 1)
                dve.wait_ge(row_step, 2 * (i * BODY + s) + 1)
                dve.scalar_tensor_tensor(out=is_best[:, u:u + 1], in0=is_best[:, u:u + 1], scalar=float(T), in1=xs[:, u, D:D + 1],
                                         op0=ALU.mult, op1=ALU.add).then_inc(row_step, 1)
                dve.wait_ge(row_step, 2 * (i * BODY + s) + 2)
                dve.tensor_tensor(to[:, u:u + 1], is_best[:, u:u + 1], idle[:, tile], ALU.max).then_inc(to_taken, 1)

            def choose(i, s):
                n = i * BODY + s
                u = s % 2
                wait(dve, pre_ready, 2 * (n - 1))
                wait(dve, h_done, 2 * (n - 1))
                dve.nop(nofuse=True)
                e = dve.value_load(r.owner[0:1, bass.ds(n, 1)], min_val=0, max_val=E - 1)
                dve.tensor_copy(w1[:, u, :, :].rearrange("p k n -> p (k n)"),
                                r.w1[:, bass.ds(e, 1), :, :].rearrange("p a k n -> p (a k n)")).then_inc(chosen, 1)
                dve.tensor_copy(b1[:, u, :], r.b1[:, bass.ds(e, 1), :].rearrange("p a n -> p (a n)")).then_inc(chosen, 1)

            def step(i, s):
                n = i * BODY + s
                if exists(i, s + 1):
                    take_rows(i, s + 1)
                if exists(i, s + 2):
                    choose(i, s + 2)
                dve.wait_ge(y_ready, n + 1)
                if not (isinstance(i, int) and i == 0):
                    dve.wait_ge(y_out[s], i * 16)
                dve.tensor_copy(ys[:, s, :], k.ps[:, 6, s * D:(s + 1) * D]).then_inc(y_copied, 1)
            choose(0, 0)
            choose(0, 1)
            dve.wait_ge(idle_in, 16)
            take_rows(0, 0)
            bodies(dve, step)
            for s in range(BODY):
                dve.wait_ge(y_out[s], (NB + (s == 0)) * 16)


def combine(k, r, scratch, out):
    nc = k.nc
    k.next_block()
    y_in = [k.sem(f"y_in{u}") for u in range(TPG)]
    added, stored = k.sem("added"), k.sem("stored")
    with nc.Block() as block:
        rows = k.xt[:, :, :].rearrange("p k n -> p (k n)").rearrange("p (u t n) -> p u t n", u=TPG, n=D)

        @block.sync
        def _(sp):
            def fetch(n):
                g, choice = divmod(n, 2)
                wait(sp, added, (n - TPG + 1) * TPG)
                first = SLOT_TILES * P + (1 - choice) * T + g * G
                sp.dma_start(rows[:, n % TPG, :, :], scratch.y[first:first + G, :].rearrange("(t p) n -> p t n", p=P)
                             ).then_inc(y_in[n % TPG], 16)

            for n in range(2 * NG):
                fetch(n)

        @block.vector
        def _(dve):
            for n in range(2 * NG):
                g, choice = divmod(n, 2)
                dve.wait_ge(y_in[n % TPG], 16 * (n // TPG + 1))
                wait(dve, added, n * TPG)
                for j in range(TPG):
                    t = g * TPG + j
                    dve.scalar_tensor_tensor(out=k.x[:, t, :], in0=rows[:, n % TPG, j, :], scalar=r.weight[:, choice, t:t + 1],
                                             in1=k.x[:, t, :], op0=ALU.mult, op1=ALU.add).then_inc(added, 1)

        @block.scalar
        def _(act):
            for g in range(NG):
                act.wait_ge(added, 2 * TPG * (g + 1))
                b, q = divmod(g * TPG, QT)
                act.dma_start(out[b, q * P:(q + TPG) * P, :].rearrange("(t p) n -> p t n", p=P),
                              k.x[:, g * TPG:(g + 1) * TPG, :]).then_inc(stored, 16)
            act.wait_ge(stored, NG * 16)


INS = ["x", "L0_attn_W_down_kv", "L0_attn_W_up_k", "L0_attn_W_up_v", "L0_attn_Wq", "L0_attn_Wo",
       "L0_xattn_bq", "L0_xattn_bk", "L0_xattn_bv", "L0_xattn_bo", "L0_ffn_b1", "L0_ffn_b2",
       "L1_attn_Wq", "L1_attn_bq", "L1_attn_Wk", "L1_attn_bk", "L1_attn_Wv", "L1_attn_bv", "L1_attn_Wo", "L1_attn_bo",
       "L1_attn_random_matrix", "L1_xattn_bq", "L1_xattn_bk", "L1_xattn_bv", "L1_xattn_bo",
       "L1_ffn_Wg", "L1_ffn_bg", "L1_ffn_W1", "L1_ffn_b1", "L1_ffn_W2", "L1_ffn_b2"]
TURNED = {"wk_t": "L0_attn_Wk", "wv_t": "L0_attn_Wv", "x0q": "L0_xattn_Wq", "x0k": "L0_xattn_Wk", "x0v": "L0_xattn_Wv",
          "x0o": "L0_xattn_Wo", "x1q": "L1_xattn_Wq", "x1k": "L1_xattn_Wk", "x1v": "L1_xattn_Wv", "x1o": "L1_xattn_Wo",
          "w1_t": "L0_ffn_w1", "w2_t": "L0_ffn_w2"}


class Routing:
    pass


class Slots:
    pass


def program(nc, d, out):
    with ExitStack() as ctx:
        k = Core(nc)
        k.x = k.sb(ctx, "x", [P, NT, D])
        k.xt = k.sb(ctx, "xt", [P, KD, T])
        attn = k.sb(ctx, "attn", [P, NT, SLOT])
        k.ident = k.sb(ctx, "ident", [P, P])
        k.hmask = k.sb(ctx, "hmask", [P, HP])
        k.iota_in, k.before_in, k.numbers_in, k.idle_in = d["c_iota"], d["c_before"], d["c_numbers"], d["c_idle"]
        k.ps = ctx.enter_context(nc.psum_tensor("banks", [P, 8, 512], F32))
        k.stats, k.stats_known = k.sb(ctx, "stats", [P, NT, 6]), False
        k.zeros = k.sb(ctx, "zeros", [P, SLOT])
        k.slots_zeroed = nc.alloc_semaphore(name="slots_zeroed")
        k.slots_x = nc.dram_tensor("slots_x", (SLOT_TILES * P, SLOT), F32).ap()
        load_tokens(k, d)

        with ExitStack() as c:
            q_scratch = nc.dram_tensor("q_parts", (3, B * D, S), BF16).ap()
            k_scratch = nc.dram_tensor("k_parts", (3, B * D, S), BF16).ap()
            k.w, loads = square_weights(k, c, d, ["L0_attn_Wq", "L0_attn_Wo", "wk_t", "wv_t"])
            k.wd = k.sb(c, "wd", [P, KD, L])
            k.wuk = k.sb(c, "wuk", [L, D])
            k.wuv = k.sb(c, "wuv", [L, D])
            k.inside = k.sb(c, "inside", [1, 1], I32)
            k.decay = k.sb(c, "decay", [P, (2 * QT - 1) * P])
            loads += [(k.wd[:, :, :], d["L0_attn_W_down_kv"].rearrange("(k p) n -> p k n", p=P)),
                      (k.wuk[:, :], d["L0_attn_W_up_k"]), (k.wuv[:, :], d["L0_attn_W_up_v"]),
                      (k.decay[:, :], d["c_decay"])]
            v_heads = k.sb(c, "v_heads", [P, B * H, QT, HD])
            normalise(k, loads)
            latent_projections(k, v_heads, q_scratch, k_scratch)
            latent_attention(k, v_heads, attn, k.decay, q_scratch, k_scratch)
            project_out(k, k.w["L0_attn_Wo"], None, attn)
        with ExitStack() as c:
            w1_raw = k.sb(c, "w1_raw", [P, KD, F])
            w2_raw = k.sb(c, "w2_raw", [P, FT, D])
            raws = Incoming(nc, "ternary_raws", [(w1_raw[:, :, :], d["w1_t"].rearrange("(k p) n -> p k n", p=P)),
                                                 (w2_raw[:, :, :], d["w2_t"].rearrange("(k p) n -> p k n", p=P))])
            raws.tiles = [a[:, :, :].rearrange("p k n -> p (k n)") for a in (w1_raw, w2_raw)]
            with ExitStack() as c2:
                w, loads = square_weights(k, c2, d, ["x0q", "x0k", "x0v", "x0o"])
                operands, more = context_operands(k, c2, d, 0, d["c_mask0"], d["c_fill0"])
                normalise(k, loads + more)
                cross_attention(k, attn, w["x0q"], w["x0k"], w["x0v"], operands, raws)
                project_out(k, w["x0o"], d["L0_xattn_bo"], attn)
            w1q = k.sb(c, "w1q", [P, KD, F], BF16)
            w2q = k.sb(c, "w2q", [P, FT, D], BF16)
            winv = k.sb(c, "winv", [P, 2])
            quantise_weights(k, raws, [a[:, :, :].rearrange("p k n -> p (k n)") for a in (w1q, w2q)], winv)
            ternary_ffn(k, w1q, w2q, winv, d["L0_ffn_b1"], d["L0_ffn_b2"])

        with ExitStack() as c:
            w, loads = square_weights(k, c, d, ["L1_attn_Wq", "L1_attn_Wk", "L1_attn_Wv", "L1_attn_Wo"])
            operands, more = feature_operands(k, c, d)
            normalise(k, loads + more)
            feature_attention(k, attn, w["L1_attn_Wq"], w["L1_attn_Wk"], w["L1_attn_Wv"], operands)
            project_out(k, w["L1_attn_Wo"], d["L1_attn_bo"], attn)
        with ExitStack() as c:
            r = Routing()
            r.w1 = k.sb(c, "experts_w1", [P, E, KD, F])
            r.w1_in = Incoming(nc, "experts_w1_in", [(r.w1[:, e, :, :], d["L1_ffn_W1"][e].rearrange("(k p) n -> p k n", p=P))
                                                     for e in range(E)])
            with ExitStack() as c2:
                w, loads = square_weights(k, c2, d, ["x1q", "x1k", "x1v", "x1o"])
                operands, more = context_operands(k, c2, d, 1, d["c_mask1"], d["c_fill1"])
                normalise(k, loads + more)
                cross_attention(k, attn, w["x1q"], w["x1k"], w["x1v"], operands, r.w1_in)
                project_out(k, w["x1o"], d["L1_xattn_bo"], attn)
            r.w2 = k.sb(c, "experts_w2", [P, E, FT, D])
            r.slot = k.sb(c, "slot", [P, 2, NT], U32)
            r.weight = k.sb(c, "choice_weight", [P, 2, NT])
            r.owned = k.sb(c, "tile_owned", [P, SLOT_TILES])
            r.owner = k.sb(c, "tile_owner", [1, SLOT_TILES], I32)
            scratch = Slots()
            scratch.x = k.slots_x
            scratch.y = nc.dram_tensor("outputs_y", (2 * T + SLOT_TILES * P, D), F32).ap()
            r.b1 = k.sb(c, "experts_b1", [P, E, FT])
            normalise(k, [], keep=attn)
            route(k, r, attn, scratch, d["L1_ffn_Wg"], d["L1_ffn_bg"], d["L1_ffn_b1"], d["L1_ffn_W2"], d["L1_ffn_b2"])
            experts(k, r, scratch)
            combine(k, r, scratch, out)


COLUMNS = ["L0_xattn_bq", "L0_xattn_bk", "L1_attn_bq", "L1_attn_bk", "L1_xattn_bq", "L1_xattn_bk", "L1_ffn_b1"]


def split3(v):
    rows = []
    for _ in range(3):
        m, e = np.frexp(v)
        part = np.trunc(m * 256.0) / 256.0 * 2.0 ** e
        rows.append(part)
        v = v - part
    assert v == 0
    return np.repeat(np.array(rows, np.float32)[:, None], P, axis=1)


def layout(inputs):
    a = {n: np.ascontiguousarray(inputs[n]) for n in INS}
    for n, src in TURNED.items():
        a[n] = np.ascontiguousarray(np.swapaxes(np.asarray(inputs[src]), -1, -2))
    for n in COLUMNS:
        b = np.asarray(inputs[n])
        a[n] = np.ascontiguousarray(np.swapaxes(b.reshape(b.shape[:-1] + (-1, P)), -1, -2))
    a["c_ctx_t"] = np.ascontiguousarray(np.asarray(inputs["ctx_1024"]).reshape(B * C, D).T)
    a["c_mask0"] = np.ascontiguousarray(inputs["mask_BxS2_bf1"]).view(np.uint8).reshape(B * C)
    a["c_mask1"] = np.ascontiguousarray(inputs["mask_Bx1x1xS2_ik0"]).reshape(B * C)
    a["c_fill0"], a["c_fill1"] = split3(-1e8), split3(-1e9)
    a["c_ident"] = np.eye(P, dtype=np.float32)
    a["c_hmask"] = (np.arange(P)[:, None] // HD == np.arange(HP)[None, :]).astype(np.float32)
    a["c_iota"] = np.repeat(np.arange(IOTA, dtype=np.float32)[None, :], P, axis=0)
    a["c_idle"] = np.ascontiguousarray(np.arange(SLOT_TILES * P, dtype=np.float32).reshape(SLOT_TILES, P).T)
    a["c_numbers"] = np.ascontiguousarray((SLOT_TILES * P + np.arange(T, dtype=np.float32)).reshape(NT, P).T)
    a["c_before"] = np.triu(np.ones((P, P), np.float32), 1)
    width = (2 * QT - 1) * P
    a["c_decay"] = np.exp(-DECAY * np.abs(np.arange(P)[:, None] + (QT - 1) * P - np.arange(width)[None, :])).astype(np.float32)
    return a


def kernel(**inputs):
    import concourse.bacc as bacc
    from concourse.bass_utils import run_bass_kernel_spmd

    nc = bacc.Bacc("TRN2", target_bir_lowering=False, num_devices=1)
    arrays = layout(inputs)
    d = {n: nc.dram_tensor(f"in_{n}", a.shape, mybir.dt.from_np(a.dtype), kind="ExternalInput").ap()
         for n, a in arrays.items()}
    out = nc.dram_tensor("out_0", (B, S, D), F32, kind="ExternalOutput").ap()
    program(nc, d, out)
    got = run_bass_kernel_spmd(nc, [{f"in_{n}": a for n, a in arrays.items()}], core_ids=[0])
    return got.results[0]["out_0"]
```
